# Optimizing a Trainium2 kernel written in Bass

```python
import numpy as np
import jax
import jax.numpy as jnp

def _softmax(x, axis=-1):
    return jax.nn.softmax(x, axis=axis)

def _gelu(x):
    return jax.nn.gelu(x, approximate=True)

def _silu(x):
    return jax.nn.silu(x)

def _sigmoid(x):
    return jax.nn.sigmoid(x)

def _layernorm(x, axis=-1, eps=1e-05):
    m = jnp.mean(x, axis=axis, keepdims=True)
    v = jnp.var(x, axis=axis, keepdims=True)
    return (x - m) / jnp.sqrt(v + eps)

def _scatter_add(tgt, idx, src, axis=0):
    return tgt.at[idx].add(src)

def _segment_sum(src, seg, n):
    return jax.ops.segment_sum(src, seg, n)
kernel_name = 'mk_gnn_preln_d2_gnn_r8_e4c010'

def setup_inputs(seed: int=0):
    np.random.seed(seed)
    _w = jnp.asarray

    def _rec_inputs():
        import jax
        import jax.numpy as jnp
        _gk = jax.random.key(seed)
        x = -8.776e-05 + 1 * jax.random.normal(jax.random.fold_in(_gk, 1), (2500, 256), jnp.float32)
        src = jax.random.randint(jax.random.fold_in(_gk, 2), (40000,), 0, 2500, jnp.int32)
        dst = jax.random.randint(jax.random.fold_in(_gk, 3), (40000,), 0, 2500, jnp.int32)
        _o = jnp.argsort(dst, stable=True)
        src = src[_o]
        dst = dst[_o]
        edge_attr_128 = -8.513e-05 + 0.999844 * jax.random.normal(jax.random.fold_in(_gk, 12), (40000, 128), jnp.float32)
        edge_attr_64 = 0.000167468 + 1.0002 * jax.random.normal(jax.random.fold_in(_gk, 13), (40000, 64), jnp.float32)
        return (x, src, dst, edge_attr_128, edge_attr_64)
    x, src, dst, edge_attr_128, edge_attr_64 = _rec_inputs()

    def _L0_gnn_setup():
        import jax, jax.numpy as jnp
        import numpy as np
        N = 2500
        E = 40000
        IN = 256
        HID = 512
        OUT = 256
        H = 4
        C1 = HID // 2 // H
        NEG_SLOPE = 0.2

        def gat_conv(x, src, dst, W, a_s, a_d, b, heads, ch):
            h = (x @ W).reshape(-1, heads, ch)
            al_s = jnp.einsum('nhc,hc->nh', h, a_s)
            al_d = jnp.einsum('nhc,hc->nh', h, a_d)
            e = jax.nn.leaky_relu(al_s[src] + al_d[dst], NEG_SLOPE)
            m = jax.ops.segment_max(e, dst, num_segments=N)
            ex = jnp.exp(e - m[dst])
            denom = jax.ops.segment_sum(ex, dst, num_segments=N)
            alpha = ex / denom[dst]
            out = jax.ops.segment_sum(alpha[:, :, None] * h[src], dst, num_segments=N)
            return out.reshape(-1, heads * ch) + b
        key = jax.random.key(seed)
        ks = jax.random.split(key, 10)
        s = 0.1
        return {'x': jax.random.normal(ks[0], (N, IN), jnp.float32), 'edge_index': jax.random.randint(ks[1], (2, E), 0, N, dtype=jnp.int64), 'W1': jax.random.normal(ks[2], (IN, H * C1), jnp.float32) * s, 'att_src1': jax.random.normal(ks[3], (H, C1), jnp.float32) * s, 'att_dst1': jax.random.normal(ks[4], (H, C1), jnp.float32) * s, 'b1': jax.random.normal(ks[5], (H * C1,), jnp.float32) * s, 'W2': jax.random.normal(ks[6], (H * C1, OUT), jnp.float32) * s, 'att_src2': jax.random.normal(ks[7], (1, OUT), jnp.float32) * s, 'att_dst2': jax.random.normal(ks[8], (1, OUT), jnp.float32) * s, 'b2': jax.random.normal(ks[9], (OUT,), jnp.float32) * s}
    _L0_gnn_all = _L0_gnn_setup()
    _L0_gnn_in = {k: v for k, v in _L0_gnn_all.items() if k in ('W1', 'att_src1', 'att_dst1', 'b1', 'W2', 'att_src2', 'att_dst2', 'b2')}
    del _L0_gnn_all

    def _L1_gnn_setup():
        import jax, jax.numpy as jnp
        import numpy as np
        N_NODES = 2500
        N_EDGES = 80000
        DIM_NODE = 256
        DIM_EDGE = 128
        N_CENTERS = 64
        DIM_HIDDEN = 128
        key = jax.random.key(seed)
        ks = jax.random.split(key, 12)
        inp = {'node_h': jax.random.normal(ks[0], (N_NODES, DIM_NODE), dtype=jnp.float32), 'edge_h': jax.random.normal(ks[1], (N_EDGES, DIM_EDGE), dtype=jnp.float32), 'dist': jax.random.normal(ks[2], (N_EDGES, N_CENTERS), dtype=jnp.float32), 'src': jax.random.randint(ks[3], (N_EDGES,), 0, N_NODES, dtype=jnp.int32), 'dst': jax.random.randint(ks[4], (N_EDGES,), 0, N_NODES, dtype=jnp.int32), 'W_node': jax.random.normal(ks[5], (DIM_NODE, DIM_HIDDEN), dtype=jnp.float32) / np.sqrt(DIM_NODE), 'b_node': jnp.zeros((DIM_HIDDEN,), dtype=jnp.float32), 'W_edge': jax.random.normal(ks[6], (DIM_EDGE, DIM_HIDDEN), dtype=jnp.float32) / np.sqrt(DIM_EDGE), 'b_edge': jnp.zeros((DIM_HIDDEN,), dtype=jnp.float32), 'W_dist': jax.random.normal(ks[7], (N_CENTERS, DIM_HIDDEN), dtype=jnp.float32) / np.sqrt(N_CENTERS), 'b_dist': jnp.zeros((DIM_HIDDEN,), dtype=jnp.float32), 'W_comb': jax.random.normal(ks[8], (2 * DIM_HIDDEN, DIM_NODE), dtype=jnp.float32) / np.sqrt(2 * DIM_HIDDEN)}
        return inp
    _L1_gnn_all = _L1_gnn_setup()
    _L1_gnn_in = {k: v for k, v in _L1_gnn_all.items() if k in ('W_node', 'b_node', 'W_edge', 'b_edge', 'W_dist', 'b_dist', 'W_comb')}
    del _L1_gnn_all
    return {'x': x, 'src': src, 'dst': dst, 'edge_attr_128': edge_attr_128, 'edge_attr_64': edge_attr_64, 'L0_gnn_W1': _L0_gnn_in['W1'], 'L0_gnn_att_src1': _L0_gnn_in['att_src1'], 'L0_gnn_att_dst1': _L0_gnn_in['att_dst1'], 'L0_gnn_b1': _L0_gnn_in['b1'], 'L0_gnn_W2': _L0_gnn_in['W2'], 'L0_gnn_att_src2': _L0_gnn_in['att_src2'], 'L0_gnn_att_dst2': _L0_gnn_in['att_dst2'], 'L0_gnn_b2': _L0_gnn_in['b2'], 'L1_gnn_W_node': _L1_gnn_in['W_node'], 'L1_gnn_b_node': _L1_gnn_in['b_node'], 'L1_gnn_W_edge': _L1_gnn_in['W_edge'], 'L1_gnn_b_edge': _L1_gnn_in['b_edge'], 'L1_gnn_W_dist': _L1_gnn_in['W_dist'], 'L1_gnn_b_dist': _L1_gnn_in['b_dist'], 'L1_gnn_W_comb': _L1_gnn_in['W_comb']}

def reference(x, src, dst, edge_attr_128, edge_attr_64, L0_gnn_W1, L0_gnn_att_src1, L0_gnn_att_dst1, L0_gnn_b1, L0_gnn_W2, L0_gnn_att_src2, L0_gnn_att_dst2, L0_gnn_b2, L1_gnn_W_node, L1_gnn_b_node, L1_gnn_W_edge, L1_gnn_b_edge, L1_gnn_W_dist, L1_gnn_b_dist, L1_gnn_W_comb):
    import jax
    import jax.numpy as jnp

    def _L0_gnn_ref(x, edge_index, W1, att_src1, att_dst1, b1, W2, att_src2, att_dst2, b2):
        import jax, jax.numpy as jnp
        import numpy as np
        N = 2500
        E = 40000
        IN = 256
        HID = 512
        OUT = 256
        H = 4
        C1 = HID // 2 // H
        NEG_SLOPE = 0.2

        def gat_conv(x, src, dst, W, a_s, a_d, b, heads, ch):
            h = (x @ W).reshape(-1, heads, ch)
            al_s = jnp.einsum('nhc,hc->nh', h, a_s)
            al_d = jnp.einsum('nhc,hc->nh', h, a_d)
            e = jax.nn.leaky_relu(al_s[src] + al_d[dst], NEG_SLOPE)
            m = jax.ops.segment_max(e, dst, num_segments=N)
            ex = jnp.exp(e - m[dst])
            denom = jax.ops.segment_sum(ex, dst, num_segments=N)
            alpha = ex / denom[dst]
            out = jax.ops.segment_sum(alpha[:, :, None] * h[src], dst, num_segments=N)
            return out.reshape(-1, heads * ch) + b
        loop = jnp.arange(N, dtype=edge_index.dtype)
        src = jnp.concatenate([edge_index[0], loop])
        dst = jnp.concatenate([edge_index[1], loop])
        h1 = jax.nn.relu(gat_conv(x, src, dst, W1, att_src1, att_dst1, b1, H, C1))
        return gat_conv(h1, src, dst, W2, att_src2, att_dst2, b2, 1, OUT)

    def _L1_gnn_ref(node_h, edge_h, dist, src, dst, W_node, b_node, W_edge, b_edge, W_dist, b_dist, W_comb):
        import jax, jax.numpy as jnp
        import numpy as np
        N_NODES = 2500
        N_EDGES = 80000
        DIM_NODE = 256
        DIM_EDGE = 128
        N_CENTERS = 64
        DIM_HIDDEN = 128
        node_proj = node_h @ W_node + b_node
        m1 = node_proj[src] * (dist @ W_dist + b_dist)
        m2 = edge_h @ W_edge + b_edge
        m = jnp.tanh(jnp.concatenate([m1, m2], axis=1) @ W_comb)
        h = jax.ops.segment_sum(m, dst, num_segments=N_NODES)
        h = h / jnp.linalg.norm(h, axis=1, keepdims=True)
        return h
    edge_index = jnp.stack([src, dst])
    h = jnp.maximum(_layernorm(x, axis=-1), 0.0)
    x = x + _L0_gnn_ref(h, edge_index, L0_gnn_W1, L0_gnn_att_src1, L0_gnn_att_dst1, L0_gnn_b1, L0_gnn_W2, L0_gnn_att_src2, L0_gnn_att_dst2, L0_gnn_b2)
    h = jnp.maximum(_layernorm(x, axis=-1), 0.0)
    x = x + _L1_gnn_ref(h, edge_attr_128, edge_attr_64, src, dst, L1_gnn_W_node, L1_gnn_b_node, L1_gnn_W_edge, L1_gnn_b_edge, L1_gnn_W_dist, L1_gnn_b_dist, L1_gnn_W_comb)
    return x

_drawn_inputs = setup_inputs


def setup_inputs(seed=0):
    import zlib

    import numpy as np

    out = dict(_drawn_inputs(seed))
    spreads = {'L1_gnn_b_node': (0.0, 0.8), 'L1_gnn_b_edge': (0.0, 1.47), 'L1_gnn_b_dist': (0.0, 0.8)}
    factors = {'L0_gnn_att_dst1': 4.672,
     'L0_gnn_att_src2': 8.0,
     'L0_gnn_att_dst2': 32.936,
     'edge_attr_128': 3.62,
     'edge_attr_64': 3.383,
     'L1_gnn_W_edge': 3.619,
     'L1_gnn_W_dist': 3.406}
    for name, (base, spread) in spreads.items():
        noise = np.random.default_rng([zlib.crc32(name.encode()), seed]).standard_normal(out[name].shape)
        drawn = base * np.exp(spread * noise) if base else spread * noise
        out[name] = jnp.asarray(drawn.astype(out[name].dtype))
    for name, factor in factors.items():
        out[name] = (out[name] * factor).astype(out[name].dtype)
    return out
```

```python
from contextlib import ExitStack

import concourse.bass as bass
from concourse import mybir

FP32 = mybir.dt.float32
BF16 = mybir.dt.bfloat16
I32 = mybir.dt.int32
ALU = mybir.AluOpType
ACT = mybir.ActivationFunctionType
AX_X = mybir.AxisListType.X

P = 128
N, E = 2500, 40000
D = 256
HID = 128
DE, DC = 128, 64
NT = (N + P - 1) // P
NPAD = NT * P
NLAST = N - (NT - 1) * P

TE = 125
ET = E // TE
KR = 4
ER = ET // KR
EC = KR * TE

STEPS = ET + NT
VC = 4
VP = STEPS // VC
RING = 10
LOAD = 12

NB = 32
NA = NPAD // NB

NEG = -1.0e38
SKIP = 1 << 20
SLOPE = 0.2
EPS = 1e-5


def bcast(ap, dims):
    return bass.AP(tensor=ap.tensor, offset=ap.offset, ap=[ap.ap[0], *dims])


def chain(eng, sem):
    count = [0]

    def link(ins):
        count[0] += 1
        ins.then_inc(sem, 1)
        eng.wait_ge(sem, count[0])

    return link


class Kernel:
    def __init__(self, nc, ctx):
        self.nc, self.ctx = nc, ctx
        self.sems = []

    def sb(self, name, shape, dt=FP32, ctx=None):
        return (ctx or self.ctx).enter_context(self.nc.sbuf_tensor(name, shape, dt))

    def ps(self, name, shape, dt=FP32, ctx=None):
        return (ctx or self.ctx).enter_context(self.nc.psum_tensor(name, shape, dt))

    def sem(self, name):
        self.sems.append(self.nc.alloc_semaphore(name=name))
        return self.sems[-1]

    def free_sems(self):
        self.nc.clear_and_free_semaphores(self.sems)
        self.nc.all_engine_barrier()
        self.sems = []

    def dram(self, name, shape, dt=FP32):
        return self.nc.dram_tensor(name, shape, dt).ap()


def prepare_edges(k, src, dst):
    nc = k.nc
    k.ident = k.sb("ident", [P, P])
    k.mirror = k.sb("mirror", [P, P])
    k.iota_n = k.sb("iota_n", [P, P])
    k.no_node = k.sb("no_node", [P, 1])
    k.onehot_a = k.sb("onehot_a", [NA, E], BF16)
    k.mask_b = k.sb("mask_b", [TE, ET, NB], BF16)
    k.keep = k.sb("keep", [ER, EC])
    k.stop_rev = k.sb("stop_rev", [ER, EC])
    k.row_stop = k.sb("row_stop", [4, ER])
    k.row_first = k.sb("row_first", [ER, 1], I32)
    k.step_tile_p = k.sb("step_tile_p", [VP, VC], I32)
    k.edge_tile = k.sb("edge_tile", [1, STEPS // RING, LOAD], I32)
    k.node_tile_before = k.sb("node_tile_before", [1, STEPS // RING, LOAD], I32)
    k.step_src = k.sb("step_src", [TE, STEPS], I32)
    k.step_dst = k.sb("step_dst", [TE, STEPS])
    k.start_at = k.sb("start_at", [P, NT], I32)
    k.start_rev = k.sb("start_rev", [P, NT], I32)
    k.dst_rows = k.dram("dst_rows", [ET, TE])
    k.src_rows = k.dram("src_rows", [ET, TE])
    src_a_row = k.dram("src_a_row", [ER, EC], BF16)
    k.spread = {4: k.dram("spread4", [E, 8]), 1: k.dram("spread1", [E, 2])}

    tmp = ExitStack()
    with tmp:
        def sb(name, shape, dt=FP32):
            return k.sb(name, shape, dt, tmp)

        iota_i = sb("iota_i", [P, NPAD], I32)
        iota_f = sb("iota_f", [P, NPAD])
        part_i = sb("part_i", [P, 1], I32)
        part_f = sb("part_f", [P, 1])
        node_i = sb("node_i", [P, NT], I32)
        node_f = sb("node_f", [P, NT])
        tile_i = sb("tile_i", [ER, KR], I32)
        step_i = sb("step_i", [VP, VC], I32)
        step_f = sb("step_f", [VP, VC])
        dst_i = sb("dst_i", [ER, EC], I32)
        src_i = sb("src_i", [ER, EC], I32)
        prev_i = sb("prev_i", [ER, EC], I32)
        next_i = sb("next_i", [ER, EC], I32)
        dst_f = sb("dst_f", [ER, EC])
        src_f = sb("src_f", [ER, EC])
        next_f = sb("next_f", [ER, EC])
        src_a = sb("src_a", [ER, EC], BF16)
        src_b = sb("src_b", [ER, EC], I32)
        src_bf = sb("src_bf", [ER, EC])
        src_bt = sb("src_bt", [TE, ET])
        next_t = sb("next_t", [TE, KR, ER])
        key_i = sb("key_i", [ER, KR], I32)
        key_f = sb("key_f", [ER, KR])
        passed = sb("passed", [ER, KR, STEPS])
        ones = sb("ones", [P, 1])
        ones_b = sb("ones_b", [P, 1], BF16)
        below = sb("below", [ER, KR, NPAD], BF16)
        zeros = sb("zeros", [ER, KR * P])
        rowflag = sb("rowflag", [ER, 1])
        rowflag4 = sb("rowflag4", [ER, 4])
        node_tile = sb("node_tile", [P, NT], I32)
        node_tile_f = sb("node_tile_f", [P, NT])
        node_row = sb("node_row", [P, NT], I32)
        rows = sb("rows", [P, NT, TE])
        cmp = sb("cmp", [P, NT, TE])
        count = sb("count", [P, NT])
        has = sb("has", [P, NT])
        start = sb("start", [P, NT])
        tab_f = sb("tab_f", [1, 2, STEPS + 1])
        win = sb("win", [VP, VC])
        src_v = sb("src_v", [VP, VC, TE])
        dst_v = sb("dst_v", [VP, VC, TE])

        ps_t = k.ps("prep_t", [TE, KR, P], FP32, tmp)
        ps_r = k.ps("prep_r", [ER, 512], FP32, tmp)
        ps_s = k.ps("prep_s", [P, 512], FP32, tmp)
        ps_n = k.ps("prep_n", [P, 512], FP32, tmp)

        edges_in = k.sem("edges_in")
        consts = k.sem("consts")
        pool_chain = k.sem("pool_chain0")
        dve_chain = k.sem("dve_chain0")
        floats = k.sem("floats")
        rows_ready = k.sem("rows_ready")
        rows_out = k.sem("rows_out")
        a_ready = k.sem("a_ready")
        a_out = k.sem("a_out")
        a_in = [k.sem(f"a_in{i}") for i in range(4)]
        passed_ready = k.sem("passed_ready")
        steps_ready = k.sem("steps_ready")
        below_ready = k.sem("below_ready")
        tiles_ready = k.sem("tiles_ready")
        tile_idx = k.sem("tile_idx")
        rows_in = k.sem("rows_in")
        step_idx = k.sem("step_idx")
        step_rows = k.sem("step_rows")
        rows_preset = k.sem("rows_preset")
        tr = k.sem("prep_tr")
        tr_used = k.sem("prep_tr_used")
        b_ready = k.sem("b_ready")
        v_fixed = k.sem("v_fixed")
        flag_ready = k.sem("flag_ready")
        zero_ready = k.sem("zero_ready")
        zero_out = k.sem("zero_out")

        d1 = dst.rearrange("(p j) -> p j", j=EC)
        s1 = src.rearrange("(p j) -> p j", j=EC)
        block = tmp.enter_context(nc.Block())

        @block.gpsimd
        def _(pool):
            link = chain(pool, pool_chain)
            pool.iota(part_i[:, :], [[0, 1]], base=0, channel_multiplier=1).then_inc(consts, 1)
            pool.iota(tile_i[:, :], [[1, KR]], base=0, channel_multiplier=KR).then_inc(consts, 1)
            pool.iota(iota_i[:, :], [[1, NPAD]], base=0, channel_multiplier=0).then_inc(consts, 1)
            pool.iota(node_i[:, :], [[P, NT]], base=0, channel_multiplier=1).then_inc(consts, 1)
            pool.iota(step_i[:, :], [[VP, VC]], base=0, channel_multiplier=1).then_inc(consts, 1)
            pool.memset(ones[:, :], 1.0).then_inc(consts, 1)
            pool.memset(ones_b[:, :], 1.0).then_inc(consts, 1)
            link(pool.memset(k.ident[:, :], 0.0))
            link(pool.memset(k.mirror[:, :], 0.0))
            link(pool.memset(k.no_node[:, :], 1.0))
            pool.affine_select(out=k.no_node[:, :], in_=k.no_node[:, :], compare_op=ALU.is_ge, fill=0.0,
                               base=-NLAST, pattern=[[0, 1]], channel_multiplier=1)
            pool.affine_select(out=k.ident[:, :], in_=k.ident[:, :], compare_op=ALU.not_equal, fill=1.0,
                               base=0, pattern=[[-1, P]], channel_multiplier=1).then_inc(consts, 1)
            pool.affine_select(out=k.mirror[:, :], in_=k.mirror[:, :], compare_op=ALU.not_equal, fill=1.0,
                               base=1 - P, pattern=[[1, P]], channel_multiplier=1).then_inc(consts, 1)
            pool.wait_ge(step_idx, 1)
            pool.wait_ge(rows_preset, 2)
            pool.wait_ge(rows_out, 32)
            for c in range(VC):
                at = bass.IndirectOffsetOnAxis(ap=k.step_tile_p[:, c:c + 1], axis=0)
                pool.indirect_dma_start(src_v[:, c, :], None, k.src_rows, at, bounds_check=ET - 1,
                                        oob_is_err=False).then_inc(step_rows, 16)
                pool.indirect_dma_start(dst_v[:, c, :], None, k.dst_rows, at, bounds_check=ET - 1,
                                        oob_is_err=False).then_inc(step_rows, 16)
            pool.wait_ge(tile_idx, 1)
            for i in range(NT):
                pool.indirect_dma_start(rows[:, i, :], None, k.dst_rows,
                                        bass.IndirectOffsetOnAxis(ap=node_row[:, i:i + 1], axis=0),
                                        bounds_check=ET - 1, oob_is_err=False).then_inc(rows_in, 16)

        @block.sync
        def _(sp):
            sp.dma_start(dst_i[:, :], d1).then_inc(edges_in, 16)
            sp.dma_start(src_i[:, :], s1).then_inc(edges_in, 16)
            sp.wait_ge(rows_preset, 4)
            sp.dma_start(prev_i[0:1, 1:EC], dst[0:EC - 1].rearrange("(a n) -> a n", a=1)).then_inc(edges_in, 16)
            sp.dma_start(prev_i[1:ER, :], dst[EC - 1:E - 1].rearrange("(p j) -> p j", j=EC)).then_inc(edges_in, 16)
            sp.dma_start(next_i[0:ER - 1, :], dst[1:E - EC + 1].rearrange("(p j) -> p j", j=EC)).then_inc(edges_in, 16)
            sp.dma_start(next_i[ER - 1:ER, 0:EC - 1],
                         dst[E - EC + 1:E].rearrange("(a n) -> a n", a=1)).then_inc(edges_in, 16)
            sp.wait_ge(rows_ready, 2)
            sp.dma_start(k.dst_rows.rearrange("(p c) q -> p (c q)", c=KR), dst_f[:, :]).then_inc(rows_out, 16)
            sp.dma_start(k.src_rows.rearrange("(p c) q -> p (c q)", c=KR), src_f[:, :]).then_inc(rows_out, 16)
            sp.wait_ge(a_ready, 1)
            sp.dma_start(src_a_row, src_a[:, :]).then_inc(a_out, 16)
            sp.wait_ge(a_out, 16)
            whole = src_a_row.rearrange("p j -> (p j)").rearrange("(a n) -> a n", a=4)
            for i in range(4):
                part = whole[i:i + 1, :]
                sp.dma_start(k.onehot_a[:, i * (E // 4):(i + 1) * (E // 4)],
                             bass.AP(tensor=part.tensor, offset=part.offset, ap=[[0, NA], [1, E // 4]])
                             ).then_inc(a_in[i], 16)
            sp.wait_ge(zero_ready, 1)
            for width, at in ((8, k.spread[4]), (2, k.spread[1])):
                flat = at.rearrange("(p j) c -> p (j c)", p=ER)
                cols = EC * width
                for c in range(0, cols, 500):
                    sp.dma_start(flat[:, c:c + 500], zeros[:, 0:500]).then_inc(zero_out, 16)
            sp.wait_ge(zero_out, 16 * 10)

        @block.tensor
        def _(pe):
            pe.wait_ge(consts, 9)
            pe.wait_ge(passed_ready, 1)
            for c in range(KR):
                pe.matmul(ps_r[0:1, 0:STEPS], ones[0:ER, :], passed[:, c, :], start=c == 0, stop=c == KR - 1)
            for v in range(VC):
                for c in range(KR):
                    last = pe.matmul(ps_s[0:VP, v:v + 1], passed[:, c, v * VP:(v + 1) * VP], ones[0:ER, :],
                                     start=c == 0, stop=c == KR - 1)
            last.then_inc(steps_ready, 1)
            pe.wait_ge(below_ready, 1)
            for i in range(NT):
                for c in range(KR):
                    last = pe.matmul(ps_n[:, i:i + 1], below[:, c, i * P:(i + 1) * P], ones_b[0:ER, :],
                                     start=c == 0, stop=c == KR - 1)
            last.then_inc(tiles_ready, 1)
            pe.wait_ge(b_ready, 1)
            for c in range(KR):
                last = pe.transpose(ps_t[:, c, 0:ER], src_bf[:, c * TE:(c + 1) * TE], k.ident[0:ER, 0:ER])
            last.then_inc(tr, 1)
            pe.wait_ge(tr_used, 1)
            for c in range(KR):
                last = pe.transpose(ps_t[:, c, 0:ER], next_f[:, c * TE:(c + 1) * TE], k.ident[0:ER, 0:ER])
            last.then_inc(tr, 1)
            pe.wait_ge(tr_used, 2)
            for c in range(KR):
                last = pe.matmul(ps_r[:, (KR - 1 - c) * TE:(KR - c) * TE], next_t[:, c, :],
                                 k.mirror[0:TE, P - TE:P], start=True, stop=True)
            last.then_inc(tr, 1)
            pe.wait_ge(flag_ready, 1)
            pe.matmul(ps_s[0:4, 128:128 + ER], rowflag4[:, :], k.mirror[0:ER, P - ER:P],
                      start=True, stop=True).then_inc(tr, 1)
            pe.wait_ge(v_fixed, 1)
            pe.wait_ge(tr_used, 3)
            for c in range(VC):
                last = pe.transpose(ps_t[:, c, 0:VP], src_v[:, c, :], k.ident[0:VP, 0:VP])
            last.then_inc(tr, 1)
            pe.wait_ge(tr_used, 4)
            for c in range(VC):
                last = pe.transpose(ps_t[:, c, 0:VP], dst_v[:, c, :], k.ident[0:VP, 0:VP])
            last.then_inc(tr, 1)

        @block.vector
        def _(dve):
            link = chain(dve, dve_chain)
            dve.memset(prev_i[:, :], -1).then_inc(rows_preset, 1)
            dve.memset(next_i[:, :], -1).then_inc(rows_preset, 1)
            dve.memset(src_v[:, :, :], 0.0).then_inc(rows_preset, 1)
            dve.memset(dst_v[:, :, :], -1.0).then_inc(rows_preset, 1)
            dve.memset(zeros[:, :], 0.0).then_inc(zero_ready, 1)
            dve.wait_ge(edges_in, 16 * 6)
            dve.tensor_copy(dst_f[:, :], dst_i[:, :]).then_inc(rows_ready, 1)
            dve.tensor_copy(src_f[:, :], src_i[:, :]).then_inc(rows_ready, 1)
            link(dve.tensor_scalar(src_b[:, :], src_i[:, :], 5, None, ALU.logical_shift_right))
            dve.tensor_copy(src_a[:, :], src_b[:, :]).then_inc(a_ready, 1)
            dve.wait_ge(a_ready, 1)
            link(dve.tensor_scalar(src_b[:, :], src_i[:, :], NB - 1, None, ALU.bitwise_and))
            dve.tensor_copy(src_bf[:, :], src_b[:, :]).then_inc(b_ready, 1)
            dve.wait_ge(consts, 9)
            link(dve.tensor_scalar(key_i[:, :], dst_i[:, TE - 1::TE], 7, None, ALU.logical_shift_right))
            link(dve.tensor_tensor(key_f[:, :], key_i[:, :], tile_i[:, :], ALU.add))
            link(dve.tensor_copy(iota_f[:, :], iota_i[:, :]))
            dve.tensor_copy(k.iota_n[:, :], iota_i[:, 0:P])
            for c in range(KR):
                last = dve.tensor_scalar(passed[:, c, :], iota_f[0:ER, 0:STEPS], key_f[:, c:c + 1], None, ALU.is_gt)
            last.then_inc(passed_ready, 1)
            dve.wait_ge(rows_ready, 2)
            for c in range(KR):
                last = dve.tensor_scalar(below[:, c, :], iota_f[0:ER, :], dst_f[:, (c + 1) * TE - 1:(c + 1) * TE],
                                         None, ALU.is_gt)
            last.then_inc(below_ready, 1)
            link(dve.tensor_tensor(k.keep[:, :], prev_i[:, :], dst_i[:, :], ALU.is_equal))
            link(dve.tensor_tensor(next_f[:, :], next_i[:, :], dst_i[:, :], ALU.is_equal))
            link(dve.tensor_reduce(rowflag[:, :], next_f[:, :], AX_X, ALU.min))
            dve.tensor_scalar(rowflag4[:, :], bcast(rowflag[:, 0:1], [[0, 4]]), -1.0, -NEG, ALU.add,
                              ALU.mult).then_inc(flag_ready, 1)
            link(dve.tensor_copy(k.row_first[:, :], dst_i[:, 0:1]))
            link(dve.tensor_copy(part_f[:, :], part_i[:, :]))
            link(dve.tensor_copy(node_f[:, :], node_i[:, :]))
            link(dve.tensor_copy(step_f[:, :], step_i[:, :]))
            dve.wait_ge(steps_ready, 1)
            link(dve.tensor_copy(k.step_tile_p[:, :], ps_s[0:VP, 0:VC]))
            dve.sem_inc(step_idx, 1)
            link(dve.tensor_tensor(win[:, :], step_f[:, :], ps_s[0:VP, 0:VC], ALU.subtract))
            link(dve.tensor_scalar(win[:, :], win[:, :], float(NT - 1), float(P), ALU.min, ALU.mult))
            link(dve.memset(tab_f[:, :, :], 0.0))
            link(dve.tensor_scalar(tab_f[:, 0, 0:STEPS], ps_r[0:1, 0:STEPS], float(ET - 1), None, ALU.min))
            link(dve.tensor_tensor(tab_f[:, 1, 1:STEPS + 1], iota_f[0:1, 0:STEPS], tab_f[:, 0, 0:STEPS], ALU.subtract))
            link(dve.tensor_scalar(tab_f[:, 1, :], tab_f[:, 1, :], float(NT - 1), None, ALU.min))
            dve.tensor_copy(k.edge_tile[:, :, 0:RING], tab_f[:, 0, 0:STEPS].rearrange("a (i s) -> a i s", s=RING))
            dve.tensor_copy(k.node_tile_before[:, :, 0:RING], tab_f[:, 1, 0:STEPS].rearrange("a (i s) -> a i s", s=RING))
            dve.wait_ge(tiles_ready, 1)
            link(dve.tensor_scalar(node_tile_f[:, :], ps_n[:, 0:NT], float(ET - 1), None, ALU.min))
            dve.tensor_copy(node_row[:, :], node_tile_f[:, :]).then_inc(tile_idx, 1)
            dve.wait_ge(tile_idx, 1)
            dve.wait_ge(tr, 1)
            for c in range(KR):
                last = dve.tensor_copy(src_bt[:, c::KR], ps_t[:, c, 0:ER])
            last.then_inc(tr_used, 1)
            dve.wait_ge(tr, 2)
            dve.tensor_copy(next_t[:, :, :], ps_t[:, :, 0:ER]).then_inc(tr_used, 1)
            dve.wait_ge(tr, 4)
            dve.wait_ge(tr_used, 2)
            dve.tensor_scalar(k.stop_rev[:, :], ps_r[:, 0:EC], -1.0, -NEG, ALU.add, ALU.mult)
            dve.tensor_copy(k.row_stop[:, :], ps_s[0:4, 128:128 + ER]).then_inc(tr_used, 1)
            dve.wait_ge(step_rows, 16 * 2 * VC)
            for c in range(VC):
                last = dve.tensor_scalar(dst_v[:, c, :], dst_v[:, c, :], win[:, c:c + 1], None, ALU.subtract)
            last.then_inc(v_fixed, 1)
            dve.wait_ge(tr, 5)
            for c in range(VC):
                last = dve.tensor_copy(k.step_src[:, c * VP:(c + 1) * VP], ps_t[:, c, 0:VP])
            last.then_inc(tr_used, 1)
            dve.tensor_tensor(k.mask_b[:, :, :], bcast(k.iota_n[0:TE, 0:NB], [[0, ET], [1, NB]]),
                              bcast(src_bt[:, :], [[1, ET], [0, NB]]), ALU.is_equal)
            for i in range(4):
                dve.wait_ge(a_in[i], 16)
                part = k.onehot_a[:, i * (E // 4):(i + 1) * (E // 4)]
                dve.tensor_scalar(part, part, part_f[0:NA, :], None, ALU.is_equal)
            dve.wait_ge(tr, 6)
            for c in range(VC):
                last = dve.tensor_copy(k.step_dst[:, c * VP:(c + 1) * VP], ps_t[:, c, 0:VP])
            last.then_inc(tr_used, 1)
            dve.wait_ge(rows_in, 16 * NT)
            node_b = bcast(node_f[:, :], [[1, NT], [0, TE]])
            link(dve.tensor_tensor(cmp[:, :, :], rows[:, :, :], node_b, ALU.is_lt))
            link(dve.tensor_reduce(count[:, :], cmp[:, :, :], AX_X, ALU.add))
            link(dve.tensor_tensor(cmp[:, :, :], rows[:, :, :], node_b, ALU.is_equal))
            link(dve.tensor_reduce(has[:, :], cmp[:, :, :], AX_X, ALU.max))
            link(dve.scalar_tensor_tensor(start[:, :], node_tile_f[:, :], float(TE), count[:, :], ALU.mult, ALU.add))
            link(dve.tensor_scalar(has[:, :], has[:, :], -float(SKIP), float(SKIP), ALU.mult, ALU.add))
            link(dve.tensor_tensor(k.start_at[:, :], start[:, :], has[:, :], ALU.add))
            link(dve.tensor_scalar(node_tile[:, :], node_row[:, :], 2, None, ALU.logical_shift_right))
            link(dve.tensor_scalar(count[:, :], node_tile[:, :], float(2 * EC), float(EC - 1), ALU.mult, ALU.add))
            link(dve.tensor_tensor(count[:, :], count[:, :], start[:, :], ALU.subtract))
            link(dve.tensor_tensor(k.start_rev[:, :], count[:, :], has[:, :], ALU.add))


def at_least(eng, sem, value):
    if not isinstance(value, int) or value > 0:
        eng.wait_ge(sem, value)


def rolled(eng, n, body):
    body(0)
    with eng.Fori(1, n - 1) as it:
        body(it)
    body(n - 1)


def step_list(eng, regs, table, it, n):
    eng.load(regs, table[0:1, bass.ds(it, 1), 0:RING].rearrange("a i s -> a (i s)"))
    return [eng.snap(r, min_val=0, max_val=n - 1) for r in regs]


def load_weights(k, x, w1, att_s1, att_d1, b1, w2, att_s2, att_d2, b2, w_node, b_node, w_edge, b_edge,
                 w_dist, b_dist, w_comb):
    nc = k.nc
    H, C = att_s1.shape
    k.x = k.sb("x_nodes", [P, NT, D])
    k.nodes = k.sb("nodes", [P, NT, D + 4])
    k.w1 = k.sb("w1_ext", [P, 2, D + 8])
    k.w2 = k.sb("w2_ext", [P, 2, D + 2])
    k.wn = k.sb("w_node", [P, 2, HID])
    k.b1 = k.sb("b1_row", [P, D])
    k.b2 = k.sb("b2_row", [P, D])
    k.bn = k.sb("bn_row", [P, HID])
    k.w_edge_comb = k.sb("w_edge_comb", [DE, D])
    k.w_comb1 = k.sb("w_comb1", [HID, D])
    k.w_dist = k.sb("w_dist_ext", [DC + 1, HID])
    k.bias3 = k.sb("bias3", [DC + 1, D], BF16)
    k.ones3 = k.sb("ones3", [DC + 1, TE], BF16)
    tmp = ExitStack()
    with tmp:
        att = k.sb("att", [P, 4, D], FP32, tmp)
        prod = k.sb("att_prod", [P, 2, D], FP32, tmp)
        we = k.sb("w_edge", [DE, HID], FP32, tmp)
        wet = k.sb("w_edge_t", [HID, DE], FP32, tmp)
        wc2 = k.sb("w_comb2", [HID, D], FP32, tmp)
        be = k.sb("b_edge", [HID, 1], FP32, tmp)
        rest = k.sb("bias_rest", [DC + 1, D], FP32, tmp)
        pt = k.ps("w_pt", [P, 512], FP32, tmp)
        pw = k.ps("w_pw", [P, 512], FP32, tmp)
        pb = k.ps("w_pb", [P, 512], FP32, tmp)
        preset = k.sem("w_preset")
        loaded = k.sem("w_loaded")
        turned = k.sem("w_turned")
        turned_out = k.sem("w_turned_out")
        folded = k.sem("w_folded")
        dve_chain = k.sem("w_chain")
        block = tmp.enter_context(nc.Block())

        def everywhere(ap, n):
            return bass.AP(tensor=ap.tensor, offset=ap.offset, ap=[[0, P], [1, n]])

        @block.sync
        def _(sp):
            sp.wait_ge(preset, 1)
            sp.dma_start(k.x[:, 0:NT - 1, :], x[0:(NT - 1) * P, :].rearrange("(i p) c -> p i c", p=P)).then_inc(loaded, 16)
            sp.dma_start(k.x[0:NLAST, NT - 1, :], x[(NT - 1) * P:N, :]).then_inc(loaded, 16)
            sp.dma_start(k.w1[:, :, 0:D], w1.rearrange("(c p) n -> p c n", p=P)).then_inc(loaded, 16)
            sp.dma_start(k.w2[:, :, 0:D], w2.rearrange("(c p) n -> p c n", p=P)).then_inc(loaded, 16)
            sp.dma_start(k.wn[:, :, :], w_node.rearrange("(c p) n -> p c n", p=P)).then_inc(loaded, 16)
            sp.dma_start(k.w_comb1[:, :], w_comb[0:HID, :]).then_inc(loaded, 16)
            sp.dma_start(wc2[:, :], w_comb[HID:2 * HID, :]).then_inc(loaded, 16)
            sp.dma_start(we[:, :], w_edge).then_inc(loaded, 16)
            sp.dma_start(k.w_dist[0:DC, :], w_dist).then_inc(loaded, 16)

        @block.scalar
        def _(act):
            for n, a in enumerate((att_s1, att_d1, att_s2, att_d2)):
                act.dma_start(att[:, n, :], everywhere(a, D)).then_inc(loaded, 16)
            act.dma_start(k.b1[:, :], everywhere(b1, D)).then_inc(loaded, 16)
            act.dma_start(k.b2[:, :], everywhere(b2, D)).then_inc(loaded, 16)
            act.dma_start(k.bn[:, :], everywhere(b_node, HID)).then_inc(loaded, 16)
            act.dma_start(k.w_dist[DC:DC + 1, :], b_dist.rearrange("(a n) -> a n", a=1)).then_inc(loaded, 16)
            act.dma_start(be[:, :], b_edge.rearrange("(n a) -> n a", a=1)).then_inc(loaded, 16)

        @block.tensor
        def _(pe):
            pe.wait_ge(loaded, 16 * 18)
            pe.transpose(pt[:, 0:DE], we[:, :], k.ident[:, :]).then_inc(turned, 1)
            pe.wait_ge(turned_out, 1)
            pe.matmul(pw[:, 0:D], wet[:, :], wc2[:, :], start=True, stop=True)
            pe.matmul(pb[0:DC + 1, 0:D], bcast(be[:, :], [[0, DC + 1]]), wc2[:, :], start=True,
                      stop=True).then_inc(folded, 1)

        @block.vector
        def _(dve):
            link = chain(dve, dve_chain)
            dve.memset(k.x[:, NT - 1, :], 0.0).then_inc(preset, 1)
            link(dve.memset(k.bias3[:, :], 0.0))
            dve.memset(k.ones3[:, :], 1.0)
            dve.wait_ge(loaded, 16 * 18)
            for n, (w, heads) in enumerate(((k.w1, H), (k.w1, H), (k.w2, 1), (k.w2, 1))):
                link(dve.tensor_tensor(prod[:, :, :], w[:, :, 0:D], bcast(att[:, n, :], [[0, 2], [1, D]]), ALU.mult))
                at = D + heads * (n % 2)
                link(dve.tensor_reduce(w[:, :, at:at + heads],
                                       prod[:, :, :].rearrange("p c (h n) -> p c h n", h=heads), AX_X, ALU.add))
            dve.wait_ge(turned, 1)
            dve.tensor_copy(wet[:, :], pt[:, 0:DE]).then_inc(turned_out, 1)
            dve.wait_ge(folded, 1)
            dve.tensor_copy(k.w_edge_comb[:, :], pw[:, 0:D])
            link(dve.tensor_copy(rest[:, :], pb[0:DC + 1, 0:D]))
            link(dve.tensor_copy(k.bias3[0:1, :], rest[0:1, :]))
            part = k.sb("bias_part", [DC + 1, D], BF16, tmp)
            for n in range(2):
                link(dve.tensor_copy(part[:, :], rest[:, :]))
                link(dve.tensor_tensor(rest[:, :], rest[:, :], part[:, :], ALU.subtract))
                row = 32 * (n + 1)
                link(dve.tensor_copy(k.bias3[row:row + 1, :], rest[row:row + 1, :]))


def project_nodes(k, name, x_in, heads_in, norm, w, heads, table, table_dram, alpha, bias=None):
    nc = k.nc
    cols = w.shape[2]
    tmp = ExitStack()
    with tmp:
        stats = k.sb(name + "stats", [P, NT, 6], FP32, tmp)
        ones = k.sb(name + "ones", [P, max(heads, 1)], FP32, tmp)
        mv = k.sb(name + "mv", [P, NT, 2], FP32, tmp)
        rstd = k.sb(name + "rstd", [P, NT], FP32, tmp)
        shift = k.sb(name + "shift", [P, NT], FP32, tmp)
        eps = k.sb(name + "eps", [P, 1], FP32, tmp)
        h = k.sb(name + "h", [P, 2, D], FP32, tmp)
        ht = k.sb(name + "ht", [P, 2, 2, P], FP32, tmp)
        ps_t = [k.ps(f"{name}ps_t{i}", [P, 2, P], FP32, tmp) for i in range(2)]
        ps_o = [k.ps(f"{name}ps_o{i}", [P, cols], FP32, tmp) for i in range(2)]
        aggr = k.sem(name + "aggr")
        root = k.sem(name + "root")
        normed = k.sem(name + "normed")
        h_ready = k.sem(name + "h_ready")
        h_turned = k.sem(name + "h_turned")
        ht_ready = k.sem(name + "ht_ready")
        projected = k.sem(name + "projected")
        out_ready = k.sem(name + "out_ready")
        stored = k.sem(name + "stored")
        dve_chain = k.sem(name + "chain")
        stat_chain = k.sem(name + "stat_chain")
        block = tmp.enter_context(nc.Block())
        CH = 5
        width = table.shape[2]

        @block.gpsimd
        def _(pool):
            pool.memset(eps[:, :], EPS).then_inc(aggr, 1)

        @block.sync
        def _(sp):
            view = table_dram.rearrange("(i p) c -> p i c", p=P)
            for i in range(0, NT, CH):
                sp.wait_ge(out_ready, i + CH)
                sp.dma_start(view[:, i:i + CH, :], table[:, i:i + CH, :]).then_inc(stored, 16)
            if heads:
                sp.dma_start(k.alpha_dram[heads].rearrange("(i p) c -> p i c", p=P),
                             alpha[:, :, :]).then_inc(stored, 16)
            sp.wait_ge(stored, 16 * (NT // CH + (1 if heads else 0)))

        @block.scalar
        def _(act):
            if norm:
                act.wait_ge(aggr, 2)
                act.activation(rstd[:, :], mv[:, :, 1], ACT.Sqrt, bias=eps[:, :]).then_inc(root, 1)
                act.wait_ge(normed, 1)

            def body(it):
                for s in range(2):
                    v = 2 * it + s
                    at_least(act, h_turned, v - 1)
                    out = h[:, s, :]
                    tile = bass.ds(v, 1)
                    xin = x_in[:, tile, :].rearrange("p a (h c) -> p (a h) c", h=heads_in)[:, :, 0:D // heads_in]
                    out = out.rearrange("p (h c) -> p h c", h=heads_in)
                    if norm:
                        ins = act.activation(out, xin, ACT.Relu, bias=shift[:, tile], scale=rstd[:, tile])
                    else:
                        ins = act.activation(out, xin, ACT.Relu)
                    ins.then_inc(h_ready, 1)

            rolled(act, NT // 2, body)

        @block.tensor
        def _(pe):
            def turn(v, s):
                pe.wait_ge(h_ready, v + 1)
                at_least(pe, ht_ready, v - 1)
                for c in range(2):
                    last = pe.transpose(ps_t[s][:, c, :], h[:, s, c * P:(c + 1) * P], k.ident[:, :])
                last.then_inc(h_turned, 1)

            def project(v, s):
                pe.wait_ge(ht_ready, v + 1)
                at_least(pe, out_ready, v - 1)
                for c in range(2):
                    last = pe.matmul(ps_o[s][:, :], ht[:, s, c, :], w[:, c, :], start=c == 0, stop=c == 1)
                last.then_inc(projected, 1)

            turn(0, 0)

            def body(it):
                for s in range(2):
                    v = 2 * it + s
                    if not isinstance(v, int) or v + 1 < NT:
                        turn(v + 1, 1 - s)
                    project(v, s)

            rolled(pe, NT // 2, body)

        @block.vector
        def _(dve):
            link = chain(dve, dve_chain)
            link(dve.memset(ones[:, :], 1.0))
            if norm:
                def stat(it):
                    for s in range(2):
                        tile = bass.ds(2 * it + s, 1)
                        dve.bn_stats(stats[:, tile, :].rearrange("p a c -> p (a c)"),
                                     x_in[:, tile, :].rearrange("p a c -> p (a c)")).then_inc(stat_chain, 1)

                rolled(dve, NT // 2, stat)
                dve.wait_ge(stat_chain, NT)
                for i in range(NT):
                    dve.bn_aggr(mv[:, i, :], stats[:, i, :]).then_inc(stat_chain, 1)
                dve.wait_ge(stat_chain, 2 * NT)
                dve.sem_inc(aggr, 1)
                dve.wait_ge(root, 1)
                link(dve.reciprocal(rstd[:, :], rstd[:, :]))
                dve.scalar_tensor_tensor(shift[:, :], mv[:, :, 0], -1.0, rstd[:, :], ALU.mult,
                                         ALU.mult).then_inc(normed, 1)

            def copy(v, s):
                dve.wait_ge(h_turned, v + 1)
                at_least(dve, projected, v - 1)
                dve.tensor_copy(ht[:, s, :, :], ps_t[s][:, :, :]).then_inc(ht_ready, 1)

            def keep(v, s):
                dve.wait_ge(projected, v + 1)
                tile = bass.ds(v, 1)
                to = table[:, tile, :].rearrange("p a c -> p (a c)")
                if heads:
                    dve.tensor_copy(to.rearrange("p (h c) -> p h c", h=heads)[:, :, D // heads], ones[:, :])
                    dve.tensor_copy(to.rearrange("p (h c) -> p h c", h=heads)[:, :, 0:D // heads],
                                    ps_o[s][:, 0:D].rearrange("p (h c) -> p h c", h=heads))
                    dve.tensor_copy(alpha[:, tile, :].rearrange("p a c -> p (a c)"),
                                    ps_o[s][:, D:D + 2 * heads]).then_inc(out_ready, 1)
                else:
                    dve.tensor_tensor(to, ps_o[s][:, :], bias[:, :], ALU.add).then_inc(out_ready, 1)

            copy(0, 0)

            def body(it):
                for s in range(2):
                    v = 2 * it + s
                    if not isinstance(v, int) or v + 1 < NT:
                        copy(v + 1, 1 - s)
                    keep(v, s)

            rolled(dve, NT // 2, body)


def edge_weights(k, name, H, alpha, table, step_ex):
    nc = k.nc
    W = 2 * H
    G = 512 // (H * NB)
    groups = ET // G
    alpha_dram = k.alpha_dram[H]
    spread = k.spread[H]
    max_rev = k.dram(name + "max_rev", [E, H])
    am_dram = k.dram(name + "am", [NPAD, W])
    ex_rows = k.dram(name + "ex_rows", [ET, H * TE])
    outer = ExitStack()
    with outer:
        as_t = k.sb(name + "as_t", [TE, ET, H], FP32, outer)
        inner = ExitStack()
        with inner:
            tab = k.sb(name + "tab", [NA, NB, W], FP32, inner)
            rest = k.sb(name + "rest", [NA, H, NB], FP32, inner)
            parts = k.sb(name + "parts", [NA, 3, H, NB], BF16, inner)
            picked = k.sb(name + "picked", [TE, 2, G, H, NB], FP32, inner)
            ps = [k.ps(f"{name}pick{i}", [TE, G, H, NB], FP32, inner) for i in range(2)]
            tab_in = k.sem(name + "tab_in")
            split = k.sem(name + "split")
            rows_read = k.sem(name + "rows_read")
            masked = k.sem(name + "masked")
            summed = k.sem(name + "summed")
            block = inner.enter_context(nc.Block())

            @block.sync
            def _(sp):
                sp.dma_start(tab[:, :, :], alpha_dram.rearrange("(a b) h -> a b h", b=NB)).then_inc(tab_in, 16)

            @block.vector
            def _(dve):
                link = chain(dve, split)
                dve.wait_ge(tab_in, 16)
                link(dve.tensor_copy(rest[:, :, :], tab[:, :, 0:H].rearrange("a b h -> a h b")))
                for n in range(3):
                    link(dve.tensor_copy(parts[:, n, :, :], rest[:, :, :]))
                    if n < 2:
                        link(dve.tensor_tensor(rest[:, :, :], rest[:, :, :], parts[:, n, :, :], ALU.subtract))

                def body(it):
                    for s in range(2):
                        g = 2 * it + s
                        dve.wait_ge(rows_read, g + 1)
                        at_least(dve, summed, g - 1)
                        mask = bcast(k.mask_b[:, bass.ds(g * G, G), :], [[NB, G], [0, H], [1, NB]])
                        dve.tensor_tensor(picked[:, s, :, :, :], ps[s][:, :, :, :], mask, ALU.mult).then_inc(masked, 1)
                        dve.wait_ge(masked, g + 1)
                        dve.tensor_reduce(as_t[:, bass.ds(g * G, G), :], picked[:, s, :, :, :], AX_X,
                                          ALU.add).then_inc(summed, 1)

                rolled(dve, groups // 2, body)

            @block.tensor
            def _(pe):
                pe.wait_ge(split, 6)

                def body(it):
                    for s in range(2):
                        g = 2 * it + s
                        at_least(pe, masked, g - 1)
                        for j in range(G):
                            for n in range(3):
                                last = pe.matmul(ps[s][:, j, :, :], k.onehot_a[:, bass.ds((g * G + j) * TE, TE)],
                                                 parts[:, n, :, :], start=n == 0, stop=n == 2)
                        last.then_inc(rows_read, 1)

                rolled(pe, groups // 2, body)

        tmp = outer
        turns = k.sb(name + "turns", [ER, 2, H * EC], FP32, tmp)
        as_rev = turns[:, 0, :].rearrange("p (h j) -> p h j", h=H)
        scan = turns[:, 1, :].rearrange("p (h j) -> p h j", h=H)
        sparse = turns[:, :, :].rearrange("p a n -> p (a n)").rearrange("p (j c) -> p j c", c=W)
        score = ex = as_rev
        as_rows = scan
        full_v = k.sb(name + "full", [VP, W, EC], FP32, tmp)
        full = full_v[0:ER, :, :]
        ex_v = full_v[:, 0:H, :].rearrange("p h j -> p (h j)").rearrange("p (c h q) -> p c h q", c=VC, h=H)
        max_rows = full[:, 0:H, :].rearrange("p h j -> p (h j)").rearrange("p (j h) -> p j h", h=H)
        local = k.sb(name + "local", [ER, H], FP32, tmp)
        across = k.sb(name + "across", [H, ER + 1], FP32, tmp)
        carry_r = k.sb(name + "carry_r", [ER, H], FP32, tmp)
        carry = k.sb(name + "carry", [ER, H], FP32, tmp)
        node_max = k.sb(name + "node_max", [P, NT, H], FP32, tmp)
        am = k.sb(name + "am_sb", [P, NT, W], FP32, tmp)
        self_e = k.sb(name + "self_e", [P, NT, H], FP32, tmp)
        self_x = k.sb(name + "self_x", [P, NT, H], FP32, tmp)
        first = k.sb(name + "first", [ER, W], FP32, tmp)
        banks = [k.ps(f"{name}bank{i}", [P, 512], FP32, tmp) for i in range(4)]
        small = k.ps(name + "small", [P, 512], FP32, tmp)

        def sem(n):
            return k.sem(name + n)

        rev_ready, rev_used, fwd_ready, fwd_used = sem("rev_ready"), sem("rev_used"), sem("fwd_ready"), sem("fwd_used")
        local_ready, turned, turned_used = sem("local_ready"), sem("turned"), sem("turned_used")
        max_ready, max_out, max_in, max_preset = sem("max_ready"), sem("max_out"), sem("max_in"), sem("max_preset")
        am_ready, am_out, spread_out, first_in, sparse_in = (sem("am_ready"), sem("am_out"), sem("spread_out"),
                                                             sem("first_in"), sem("sparse_in"))
        self_ready, self_done, score_ready, ex_ready = (sem("self_ready"), sem("self_done"), sem("score_ready"),
                                                        sem("ex_ready"))
        ex_out, ex_in, ex_turned, dve_chain = sem("ex_out"), sem("ex_in"), sem("ex_turned"), sem("chain")
        ex_used = sem("ex_used")
        block = tmp.enter_context(nc.Block())

        @block.sync
        def _(sp):
            sp.wait_ge(max_ready, 1)
            sp.dma_start(max_rev.rearrange("(p j) h -> p j h", j=EC), max_rows[:, :, :]).then_inc(max_out, 16)
            sp.wait_ge(am_ready, 1)
            sp.dma_start(am_dram.rearrange("(i p) c -> p i c", p=P), am[:, :, :]).then_inc(am_out, 16)
            sp.wait_ge(spread_out, 16 * NT)
            sp.dma_start(sparse[:, :, :], spread.rearrange("(p j) c -> p j c", j=EC)).then_inc(sparse_in, 16)
            sp.wait_ge(ex_ready, 1)
            to = ex_rows.rearrange("(p c) (h q) -> p h c q", c=KR, h=H)
            for h in range(H):
                sp.dma_start(to[:, h], ex[:, h, :].rearrange("p (c q) -> p c q", c=KR)).then_inc(ex_out, 16)

        @block.gpsimd
        def _(pool):
            pool.wait_ge(max_preset, 1)
            pool.wait_ge(max_out, 16)
            for i in range(NT):
                pool.indirect_dma_start(node_max[:, i, :], None, max_rev,
                                        bass.IndirectOffsetOnAxis(ap=k.start_rev[:, i:i + 1], axis=0),
                                        bounds_check=E - 1, oob_is_err=False).then_inc(max_in, 16)
            pool.wait_ge(am_ready, 1)
            for i in range(NT):
                pool.indirect_dma_start(spread, bass.IndirectOffsetOnAxis(ap=k.start_at[:, i:i + 1], axis=0),
                                        am[:, i, :], None, bounds_check=E - 1,
                                        oob_is_err=False).then_inc(spread_out, 16)
            pool.wait_ge(am_out, 16)
            pool.indirect_dma_start(first[:, :], None, am_dram,
                                    bass.IndirectOffsetOnAxis(ap=k.row_first[:, :], axis=0)).then_inc(first_in, 16)
            pool.wait_ge(max_preset, 2)
            pool.wait_ge(ex_out, 16 * H)
            for c in range(VC):
                pool.indirect_dma_start(ex_v[:, c, :, :].rearrange("p h q -> p (h q)"), None, ex_rows,
                                        bass.IndirectOffsetOnAxis(ap=k.step_tile_p[:, c:c + 1], axis=0),
                                        bounds_check=ET - 1, oob_is_err=False).then_inc(ex_in, 16)

        @block.scalar
        def _(act):
            act.wait_ge(self_ready, 1)
            act.activation(self_x[:, :, :], self_e[:, :, :], ACT.Exp).then_inc(self_done, 1)
            act.wait_ge(score_ready, 1)
            act.activation(ex[:, :, :], score[:, :, :], ACT.Exp).then_inc(ex_ready, 1)

        @block.tensor
        def _(pe):
            for h in range(H):
                for c in range(KR):
                    last = pe.matmul(banks[h][0:ER, (KR - 1 - c) * TE:(KR - c) * TE], as_t[:, c::KR, h],
                                     k.mirror[0:TE, P - TE:P], start=True, stop=True)
                last.then_inc(rev_ready, 1)
            for h in range(H):
                pe.wait_ge(rev_used, h + 1)
                for c in range(KR):
                    last = pe.transpose(banks[h][0:ER, c * TE:(c + 1) * TE], as_t[:, c::KR, h], k.ident[0:TE, 0:TE])
                last.then_inc(fwd_ready, 1)
            pe.wait_ge(local_ready, 1)
            pe.matmul(small[0:H, 0:ER], local[:, :], k.mirror[0:ER, P - ER:P], start=True, stop=True).then_inc(turned, 1)
            pe.wait_ge(turned_used, 1)
            pe.matmul(small[0:ER, 128:128 + H], across[:, 0:ER], k.ident[0:H, 0:H], start=True,
                      stop=True).then_inc(turned, 1)
            pe.wait_ge(turned_used, 2)
            pe.matmul(small[0:ER, 256:256 + H], k.mirror[0:ER, P - ER:P], carry_r[:, :], start=True,
                      stop=True).then_inc(turned, 1)
            pe.wait_ge(fwd_used, H)
            pe.wait_ge(ex_in, 16 * VC)
            for h in range(H):
                for c in range(VC):
                    last = pe.transpose(banks[h][0:TE, c * VP:(c + 1) * VP], ex_v[:, c, h, :], k.ident[0:VP, 0:VP])
                last.then_inc(ex_turned, 1)

        @block.vector
        def _(dve):
            link = chain(dve, dve_chain)
            dve.memset(node_max[:, :, :], NEG).then_inc(max_preset, 1)
            link(dve.memset(across[:, :], NEG))
            for h in range(H):
                dve.wait_ge(rev_ready, h + 1)
                dve.tensor_copy(as_rev[:, h, :], banks[h][0:ER, 0:EC]).then_inc(rev_used, 1)
            dve.wait_ge(rev_used, H)
            for h in range(H):
                link(dve.tensor_tensor_scan(scan[:, h, :], k.stop_rev[:, :], as_rev[:, h, :], NEG, ALU.add, ALU.max))
            dve.tensor_copy(local[:, :], scan[:, :, EC - 1]).then_inc(local_ready, 1)
            dve.wait_ge(turned, 1)
            link(dve.tensor_tensor_scan(across[:, 1:ER + 1], k.row_stop[0:H, :], small[0:H, 0:ER], NEG,
                                        ALU.add, ALU.max))
            dve.sem_inc(turned_used, 1)
            dve.wait_ge(turned, 2)
            dve.tensor_copy(carry_r[:, :], small[0:ER, 128:128 + H]).then_inc(turned_used, 1)
            dve.wait_ge(turned, 3)
            link(dve.tensor_copy(carry[:, :], small[0:ER, 256:256 + H]))
            for h in range(H):
                last = dve.tensor_tensor_scan(max_rows[:, :, h], k.stop_rev[:, :], as_rev[:, h, :],
                                              carry[:, h:h + 1], ALU.add, ALU.max)
                link(last)
            dve.sem_inc(max_ready, 1)
            dve.wait_ge(max_in, 16 * NT)
            link(dve.tensor_tensor(node_max[:, :, :], node_max[:, :, :], alpha[:, :, 0:H], ALU.max))
            link(dve.tensor_tensor(node_max[:, :, :], node_max[:, :, :], alpha[:, :, H:W], ALU.add))
            link(dve.tensor_copy(am[:, :, 0:H], alpha[:, :, H:W]))
            link(dve.scalar_tensor_tensor(am[:, :, H:W], node_max[:, :, :], SLOPE, node_max[:, :, :], ALU.mult, ALU.max))
            dve.sem_inc(am_ready, 1)
            link(dve.tensor_tensor(self_e[:, :, :], alpha[:, :, 0:H], alpha[:, :, H:W], ALU.add))
            link(dve.scalar_tensor_tensor(self_e[:, :, :], self_e[:, :, :], SLOPE, self_e[:, :, :], ALU.mult, ALU.max))
            dve.tensor_tensor(self_e[:, :, :], self_e[:, :, :], am[:, :, H:W], ALU.subtract).then_inc(self_ready, 1)
            dve.wait_ge(self_done, 1)
            for h in range(H):
                own = table[:, :, h * (D // H + 1):(h + 1) * (D // H + 1)]
                link(dve.tensor_tensor(own, own, bcast(self_x[:, :, h], [[H, NT], [0, D // H + 1]]), ALU.mult))
            dve.wait_ge(sparse_in, 16)
            dve.wait_ge(first_in, 16)
            for c in range(W):
                link(dve.tensor_tensor_scan(full[:, c, :], k.keep[:, :], sparse[:, :, c], first[:, c:c + 1],
                                            ALU.mult, ALU.add))
            for h in range(H):
                dve.wait_ge(fwd_ready, h + 1)
                dve.tensor_copy(as_rows[:, h, :], banks[h][0:ER, 0:EC]).then_inc(fwd_used, 1)
            dve.wait_ge(fwd_used, H)
            link(dve.tensor_tensor(score[:, :, :], as_rows[:, :, :], full[:, 0:H, :], ALU.add))
            link(dve.scalar_tensor_tensor(score[:, :, :], score[:, :, :], SLOPE, score[:, :, :], ALU.mult, ALU.max))
            dve.tensor_tensor(score[:, :, :], score[:, :, :], full[:, H:W, :], ALU.subtract).then_inc(score_ready, 1)
            dve.wait_ge(score_ready, 1)
            dve.memset(ex_v, 0.0).then_inc(max_preset, 1)
            for h in range(H):
                dve.wait_ge(ex_turned, h + 1)
                last = dve.tensor_copy(step_ex[:, :, h], banks[h][0:TE, 0:STEPS])
            last.then_inc(ex_used, 1)


def sum_messages(k, name, H, table_dram, acc, step_ex):
    nc = k.nc
    cols = D + H
    tmp = ExitStack()
    with tmp:
        idx = k.sb(name + "idx", [TE, RING], I32, tmp)
        got = k.sb(name + "got", [TE, RING, cols], FP32, tmp)
        onehot = k.sb(name + "onehot", [TE, 2, P], FP32, tmp)
        msg = k.sb(name + "msg", [TE, 2, cols], FP32, tmp) if H > 1 else None
        ps = [k.ps(f"{name}sum{i}", [P, cols], FP32, tmp) for i in range(2)]
        idx_ready = k.sem(name + "idx_ready")
        got_ready = [k.sem(f"{name}got_ready{s}") for s in range(RING)]
        msg_ready = k.sem(name + "msg_ready")
        gathers_begun = k.sem(name + "gathers_begun")
        summed = k.sem(name + "summed_step")
        added = k.sem(name + "added")
        block = tmp.enter_context(nc.Block())

        @block.scalar
        def _(act):
            def body(it):
                for s in range(RING):
                    at_least(act, got_ready[s], 16 * it)
                    act.activation(idx[:, s:s + 1], k.step_src[:, bass.ds(RING * it + s, 1)],
                                   ACT.Copy).then_inc(idx_ready, 1)

            rolled(act, STEPS // RING, body)

        @block.gpsimd
        def _(pool):
            def body(it):
                for s in range(RING):
                    v = RING * it + s
                    pool.wait_ge(idx_ready, v + 1)
                    at_least(pool, msg_ready if H > 1 else summed, v + 1 - RING)
                    pool.sem_inc(gathers_begun, 1)
                    pool.indirect_dma_start(got[:, s, :], None, table_dram,
                                            bass.IndirectOffsetOnAxis(ap=idx[:, s:s + 1], axis=0)
                                            ).then_inc(got_ready[s], 16)

            rolled(pool, STEPS // RING, body)

        @block.tensor
        def _(pe):
            def body(it):
                for s in range(RING):
                    v, b = RING * it + s, s % 2
                    pe.wait_ge(msg_ready, v + 1)
                    if H == 1:
                        pe.wait_ge(got_ready[s], 16 * it + 16)
                    at_least(pe, added, v - 1)
                    pe.matmul(ps[b][:, :], onehot[:, b, :], msg[:, b, :] if H > 1 else got[:, s, :],
                              start=True, stop=True).then_inc(summed, 1)

            rolled(pe, STEPS // RING, body)

        @block.vector
        def _(dve):
            regs = [dve.alloc_register(f"{name}tile{s}") for s in range(RING)]

            def add(v, b, at):
                dve.wait_ge(summed, v + 1)
                at_least(dve, added, v)
                to = acc[:, at, :].rearrange("p a c -> p (a c)")
                dve.tensor_tensor(to, ps[b][:, :], to, ALU.add).then_inc(added, 1)

            def body(it):
                before = step_list(dve, regs, k.node_tile_before, it, NT)
                for s in range(RING):
                    v, b = RING * it + s, s % 2
                    step = bass.ds(v, 1)
                    if H > 1:
                        dve.tensor_scalar(onehot[:, b, :], k.iota_n[0:TE, :], k.step_dst[:, step], None, ALU.is_equal)
                        dve.wait_ge(got_ready[s], 16 * it + 16)
                        dve.tensor_tensor(msg[:, b, :].rearrange("p (h c) -> p h c", h=H),
                                          got[:, s, :].rearrange("p (h c) -> p h c", h=H),
                                          bcast(step_ex[:, step, :], [[1, H], [0, D // H + 1]]),
                                          ALU.mult).then_inc(msg_ready, 1)
                    else:
                        dve.tensor_scalar(onehot[:, b, :], k.iota_n[0:TE, :], k.step_dst[:, step],
                                          step_ex[:, step, :].rearrange("p a c -> p (a c)"), ALU.is_equal,
                                          ALU.mult).then_inc(msg_ready, 1)
                    if not isinstance(v, int) or v > 0:
                        add(v - 1, 1 - b, bass.ds(before[s], 1))

            rolled(dve, STEPS // RING, body)
            add(STEPS - 1, (STEPS - 1) % 2, bass.ds(NT - 1, 1))


def normalize_sums(k, name, H, acc, bias, add_to=None):
    nc = k.nc
    C = D // H
    tmp = ExitStack()
    with tmp:
        inv = k.sb(name + "inv", [P, NT, H], FP32, tmp)
        dve_chain = k.sem(name + "chain")
        block = tmp.enter_context(nc.Block())

        @block.vector
        def _(dve):
            link = chain(dve, dve_chain)
            a = acc.rearrange("p i (h c) -> p i h c", h=H)
            link(dve.reciprocal(inv[:, :, :], a[:, :, :, C]))
            for h in range(H):
                o = a[:, :, h, 0:C]
                link(dve.tensor_tensor(o, o, bcast(inv[:, :, h], [[H, NT], [0, C]]), ALU.mult))
                link(dve.tensor_tensor(o, o, bcast(bias[:, h * C:(h + 1) * C], [[0, NT], [1, C]]), ALU.add))
            if add_to is not None:
                link(dve.tensor_tensor(add_to[:, :, :], add_to[:, :, :], acc[:, :, 0:D], ALU.add))


def attention_layer(k, name, H, x_in, heads_in, norm, w, bias, add_to=None):
    width = D + H
    outer = ExitStack()
    with outer:
        table = k.nodes[:, :, 0:width]
        alpha = k.sb(name + "alpha", [P, NT, 2 * H], FP32, outer)
        step_ex = k.sb(name + "step_ex", [TE, STEPS, H], FP32, outer)
        table_dram = k.dram(name + "table_dram", [NPAD, width])
        project_nodes(k, name + "p_", x_in, heads_in, norm, w, H, table, table_dram, alpha)
        edge_weights(k, name + "w_", H, alpha, table, step_ex)
        sum_messages(k, name + "s_", H, table_dram, table, step_ex)
        normalize_sums(k, name + "n_", H, table, bias, add_to)
        k.free_sems()


def edge_network(k, ea, ed, table_dram, out):
    nc = k.nc
    acc = k.nodes[:, :, 0:D]
    SLOTS = 5
    tmp = ExitStack()
    with tmp:
        def sb(name, shape, dt=FP32):
            return k.sb("e_" + name, shape, dt, tmp)

        def sem(name):
            return k.sem("e_" + name)

        idx = sb("idx", [TE, RING], I32)
        node = sb("node", [TE, RING, HID])
        ea_sb = sb("ea", [TE, RING, DE])
        ed_sb = sb("ed", [TE, RING, DC + 1])
        wide_t = sb("wide_t", [DE, SLOTS, 2, TE])
        ed_t = sb("ed_t", [DC + 1, SLOTS, TE])
        gated = sb("gated", [HID, 2, TE])
        onehot = sb("onehot", [TE, 2, P])
        msg = sb("msg", [TE, 2, D])
        square = sb("square", [P, NT, D])
        norm = sb("norm", [P, NT])
        ps_t = [k.ps(f"e_turn{i}", [P, 2, P], FP32, tmp) for i in range(2)]
        ps_e = [k.ps(f"e_dist{i}", [P, 2, P], FP32, tmp) for i in range(2)]
        ps_d = [ps[:, 0, 0:TE] for ps in ps_e]
        ps_z = [k.ps(f"e_z{i}", [TE, D], FP32, tmp) for i in range(2)]
        ps_s = [k.ps(f"e_sum{i}", [P, D], FP32, tmp) for i in range(2)]
        preset = sem("preset")
        idx_ready = sem("idx_ready")
        node_in = [sem(f"node_in{s}") for s in range(RING)]
        attrs_in = [sem(f"attrs_in{s}") for s in range(RING)]
        gathers_begun = sem("gathers_begun")
        turned = sem("turned")
        wide_ready = sem("wide_ready")
        ed_ready = sem("ed_ready")
        dist_ready = sem("dist_ready")
        gated_ready = sem("gated_ready")
        z_ready = sem("z_ready")
        msg_ready = sem("msg_ready")
        onehot_ready = sem("onehot_ready")
        summed = sem("summed")
        added = sem("added")
        dve_chain = sem("chain")
        squared = sem("squared")
        rooted = sem("rooted")
        done = sem("done")
        out_done = sem("out_done")
        block = tmp.enter_context(nc.Block())
        LAST = STEPS - 1

        @block.sync
        def _(sp):
            regs = [sp.alloc_register(f"e_edge_tile{s}") for s in range(RING)]
            sp.wait_ge(preset, 1)

            def body(it):
                tiles = step_list(sp, regs, k.edge_tile, it, ET)
                for s in range(RING):
                    at_least(sp, turned, RING * it + s + 1 - RING)
                    sp.dma_start(ea_sb[:, s, :], ea[bass.ds(tiles[s] * TE, TE), :]).then_inc(attrs_in[s], 16)
                    sp.dma_start(ed_sb[:, s, 0:DC], ed[bass.ds(tiles[s] * TE, TE), :]).then_inc(attrs_in[s], 16)

            rolled(sp, STEPS // RING, body)
            sp.wait_ge(done, 1)
            sp.dma_start(out[0:(NT - 1) * P, :].rearrange("(i p) c -> p i c", p=P),
                         k.x[:, 0:NT - 1, :]).then_inc(out_done, 16)
            sp.dma_start(out[(NT - 1) * P:N, :], k.x[0:NLAST, NT - 1, :]).then_inc(out_done, 16)
            sp.wait_ge(out_done, 32)

        @block.gpsimd
        def _(pool):
            def body(it):
                for s in range(RING):
                    v = RING * it + s
                    pool.wait_ge(idx_ready, v + 1)
                    at_least(pool, turned, v + 1 - RING)
                    pool.sem_inc(gathers_begun, 1)
                    pool.indirect_dma_start(node[:, s, :], None, table_dram,
                                            bass.IndirectOffsetOnAxis(ap=idx[:, s:s + 1], axis=0)
                                            ).then_inc(node_in[s], 16)

            rolled(pool, STEPS // RING, body)

        @block.scalar
        def _(act):
            def index(v, s, landed):
                at_least(act, node_in[s], landed)
                act.activation(idx[:, s:s + 1], k.step_src[:, bass.ds(v, 1)], ACT.Copy).then_inc(idx_ready, 1)

            def copy_wide(v, s):
                act.wait_ge(turned, v + 1)
                at_least(act, z_ready, v + 1 - SLOTS)
                act.activation(wide_t[:, s % SLOTS, :, :], ps_t[s % 2][:, :, 0:TE], ACT.Copy).then_inc(wide_ready, 1)

            def tanh(v, s):
                act.wait_ge(z_ready, v + 1)
                at_least(act, summed, v - 1)
                act.activation(msg[:, s % 2, :], ps_z[s % 2][:, :], ACT.Tanh).then_inc(msg_ready, 1)

            AHEAD = 6
            for s in range(AHEAD):
                index(s, s, 0)
            copy_wide(0, 0)
            copy_wide(1, 1)

            def body(it):
                for s in range(RING):
                    v = RING * it + s
                    if not isinstance(v, int) or v + AHEAD <= LAST:
                        index(v + AHEAD, (s + AHEAD) % RING, 16 * it + 16 * ((s + AHEAD) // RING))
                    if not isinstance(v, int) or v + 2 <= LAST:
                        copy_wide(v + 2, (s + 2) % RING)
                    tanh(v, s)

            rolled(act, STEPS // RING, body)
            act.wait_ge(squared, 1)
            act.activation(norm[:, :], norm[:, :], ACT.Sqrt).then_inc(rooted, 1)

        @block.tensor
        def _(pe):
            def turn(v, s, landed):
                pe.wait_ge(attrs_in[s], 2 * landed)
                pe.wait_ge(node_in[s], landed)
                at_least(pe, wide_ready, v - 1)
                ps = ps_t[s % 2]
                pe.transpose(ps[:, 0, 0:TE], ea_sb[:, s, :], k.ident[0:TE, 0:TE])
                pe.transpose(ps[:, 1, 0:TE], node[:, s, :], k.ident[0:TE, 0:TE])
                at_least(pe, gated_ready, v - 1)
                pe.transpose(ps_e[s % 2][0:DC + 1, 1, 0:TE], ed_sb[:, s, :], k.ident[0:TE, 0:TE]).then_inc(turned, 1)

            def dist(v, s):
                pe.wait_ge(ed_ready, v + 1)
                at_least(pe, gated_ready, v - 1)
                pe.matmul(ps_d[s % 2], k.w_dist[:, :], ed_t[:, s % SLOTS, :], start=True,
                          stop=True).then_inc(dist_ready, 1)

            def combine(v, s):
                b = s % 2
                pe.wait_ge(wide_ready, v + 1)
                at_least(pe, msg_ready, v - 1)
                pe.matmul(ps_z[b][:, :], k.ones3[:, :], k.bias3[:, :], start=True, stop=False)
                pe.matmul(ps_z[b][:, :], wide_t[:, s % SLOTS, 0, :], k.w_edge_comb[:, :], start=False, stop=False)
                pe.wait_ge(gated_ready, v + 1)
                pe.matmul(ps_z[b][:, :], gated[:, b, :], k.w_comb1[:, :], start=False, stop=True).then_inc(z_ready, 1)

            def scatter(v, s):
                b = s % 2
                pe.wait_ge(msg_ready, v + 1)
                pe.wait_ge(onehot_ready, v + 1)
                at_least(pe, added, v - 1)
                pe.matmul(ps_s[b][:, :], onehot[:, b, :], msg[:, b, :], start=True, stop=True).then_inc(summed, 1)

            turn(0, 0, 16)
            turn(1, 1, 16)
            dist(0, 0)

            def body(it):
                for s in range(RING):
                    v = RING * it + s
                    if not isinstance(v, int) or v + 2 <= LAST:
                        turn(v + 2, (s + 2) % RING, 16 * it + 16 * ((s + 2) // RING) + 16)
                    if not isinstance(v, int) or v + 1 <= LAST:
                        dist(v + 1, (s + 1) % RING)
                    combine(v, s)
                    if not isinstance(v, int) or v > 0:
                        scatter(v - 1, (s - 1) % RING)

            rolled(pe, STEPS // RING, body)
            scatter(LAST, LAST % RING)

        @block.vector
        def _(dve):
            link = chain(dve, dve_chain)
            regs = [dve.alloc_register(f"e_tile{s}") for s in range(RING)]
            dve.memset(ed_sb[:, :, DC:DC + 1], 1.0).then_inc(preset, 1)
            link(dve.memset(acc, 0.0))

            def copy_ed(v, s):
                dve.wait_ge(turned, v + 1)
                at_least(dve, dist_ready, v + 1 - SLOTS)
                dve.tensor_copy(ed_t[:, s % SLOTS, :], ps_e[s % 2][0:DC + 1, 1, 0:TE]).then_inc(ed_ready, 1)

            def gate(v, s):
                dve.wait_ge(dist_ready, v + 1)
                dve.wait_ge(wide_ready, v + 1)
                at_least(dve, z_ready, v - 1)
                dve.tensor_tensor(gated[:, s % 2, :], ps_d[s % 2], wide_t[:, s % SLOTS, 1, :],
                                  ALU.mult).then_inc(gated_ready, 1)

            def place(v, s):
                dve.tensor_scalar(onehot[:, s % 2, :], k.iota_n[0:TE, :], k.step_dst[:, bass.ds(v, 1)], None,
                                  ALU.is_equal).then_inc(onehot_ready, 1)

            def add(v, s, at):
                dve.wait_ge(summed, v + 1)
                at_least(dve, added, v)
                to = acc[:, at, :].rearrange("p a c -> p (a c)")
                dve.tensor_tensor(to, ps_s[s % 2][:, :], to, ALU.add).then_inc(added, 1)

            copy_ed(0, 0)
            copy_ed(1, 1)
            gate(0, 0)

            def body(it):
                before = step_list(dve, regs, k.node_tile_before, it, NT)
                for s in range(RING):
                    v = RING * it + s
                    if not isinstance(v, int) or v + 2 <= LAST:
                        copy_ed(v + 2, (s + 2) % RING)
                    if not isinstance(v, int) or v + 1 <= LAST:
                        gate(v + 1, (s + 1) % RING)
                    place(v, s)
                    if not isinstance(v, int) or v > 0:
                        add(v - 1, (s - 1) % RING, bass.ds(before[s], 1))

            rolled(dve, STEPS // RING, body)
            add(LAST, LAST % RING, bass.ds(NT - 1, 1))
            dve.wait_ge(added, STEPS)
            link(dve.tensor_tensor(square[:, :, :], acc, acc, ALU.mult))
            link(dve.tensor_reduce(norm[:, :], square[:, :, :], AX_X, ALU.add))
            dve.tensor_tensor(norm[:, NT - 1:NT], norm[:, NT - 1:NT], k.no_node[:, :], ALU.add).then_inc(squared, 1)
            dve.wait_ge(rooted, 1)
            link(dve.reciprocal(norm[:, :], norm[:, :]))
            link(dve.tensor_tensor(square[:, :, :], acc, bcast(norm[:, :], [[1, NT], [0, D]]), ALU.mult))
            dve.tensor_tensor(k.x[:, :, :], k.x[:, :, :], square[:, :, :], ALU.add).then_inc(done, 1)


def graph_kernel(nc, x, src, dst, edge_attr_128, edge_attr_64, w1, att_s1, att_d1, b1, w2, att_s2, att_d2, b2,
                 w_node, b_node, w_edge, b_edge, w_dist, b_dist, w_comb, out):
    with ExitStack() as ctx:
        k = Kernel(nc, ctx)
        k.alpha_dram = {4: k.dram("alpha4", [NPAD, 8]), 1: k.dram("alpha1", [NPAD, 2])}
        node_dram = k.dram("node_dram", [NPAD, HID])
        prepare_edges(k, src, dst)
        load_weights(k, x, w1, att_s1, att_d1, b1, w2, att_s2, att_d2, b2, w_node, b_node, w_edge, b_edge,
                     w_dist, b_dist, w_comb)
        attention_layer(k, "a", 4, k.x, 1, True, k.w1, k.b1)
        attention_layer(k, "b", 1, k.nodes, 4, False, k.w2, k.b2, add_to=k.x)
        project_nodes(k, "c_", k.x, 1, True, k.wn, 0, k.nodes[:, :, 0:HID], node_dram, None, k.bn)
        edge_network(k, edge_attr_128, edge_attr_64, node_dram, out)


_INS = ['x', 'src', 'dst', 'edge_attr_128', 'edge_attr_64'] + ['L0_gnn_' + n for n in (
    'W1', 'att_src1', 'att_dst1', 'b1', 'W2', 'att_src2', 'att_dst2', 'b2')] + ['L1_gnn_' + n for n in (
        'W_node', 'b_node', 'W_edge', 'b_edge', 'W_dist', 'b_dist', 'W_comb')]


def kernel(**inputs):
    import numpy as _np
    import concourse.bacc as _bacc
    from concourse import mybir as _mybir
    from concourse.bass_utils import run_bass_kernel_spmd as _run

    nc = _bacc.Bacc("TRN2", target_bir_lowering=False, num_devices=1)
    arrays, args = {}, []
    for name in _INS:
        a = _np.ascontiguousarray(inputs[name])
        arrays[f"in_{name}_dram"] = a
        args.append(nc.dram_tensor(f"in_{name}_dram", a.shape, _mybir.dt.from_np(a.dtype), kind="ExternalInput").ap())
    out = nc.dram_tensor("out_0_dram", (N, D), _mybir.dt.float32, kind="ExternalOutput").ap()
    graph_kernel(nc, *args, out)
    r = _run(nc, [arrays], core_ids=[0])
    return r.results[0]["out_0_dram"]
```

```python
from contextlib import ExitStack

import concourse.bass as bass
from concourse import mybir

FP32 = mybir.dt.float32
BF16 = mybir.dt.bfloat16
I32 = mybir.dt.int32
ALU = mybir.AluOpType
ACT = mybir.ActivationFunctionType
AX_X = mybir.AxisListType.X

P = 128
N, E = 2500, 40000
D = 256
HID = 128
DE, DC = 128, 64
NT = (N + P - 1) // P
NPAD = NT * P
NLAST = N - (NT - 1) * P

TE = 125
ET = E // TE
KR = 4
ER = ET // KR
EC = KR * TE

STEPS = ET + NT
VC = 4
VP = STEPS // VC
RING = 20
SUM_LAG = 3
LIST = 10
LOAD = 12
GROUP = 5
PER_ITER = 2 * GROUP
FIRST_PART = STEPS // RING * PER_ITER

NA = 125
NB = N // NA
DIV_SHIFT = 16
DIV_MUL = -(-(1 << DIV_SHIFT) // NB)

NEG = -1.0e38
SKIP = 1 << 20
SLOPE = 0.2
EPS = 1e-5


def bcast(ap, dims):
    return bass.AP(tensor=ap.tensor, offset=ap.offset, ap=[ap.ap[0], *dims])


def chain(eng, sem):
    count = [0]

    def link(ins):
        count[0] += 1
        ins.then_inc(sem, 1)
        eng.wait_ge(sem, count[0])

    return link


class Kernel:
    def __init__(self, nc, ctx):
        self.nc, self.ctx = nc, ctx
        self.sems = []

    def sb(self, name, shape, dt=FP32, ctx=None):
        return (ctx or self.ctx).enter_context(self.nc.sbuf_tensor(name, shape, dt))

    def ps(self, name, shape, dt=FP32, ctx=None):
        return (ctx or self.ctx).enter_context(self.nc.psum_tensor(name, shape, dt))

    def sem(self, name):
        self.sems.append(self.nc.alloc_semaphore(name=name))
        return self.sems[-1]

    def free_sems(self):
        self.nc.clear_and_free_semaphores(self.sems)
        self.nc.all_engine_barrier()
        self.sems = []

    def dram(self, name, shape, dt=FP32):
        return self.nc.dram_tensor(name, shape, dt).ap()


def prepare_edges(k, src, dst):
    nc = k.nc
    k.ident = k.sb("ident", [P, P])
    k.mirror = k.sb("mirror", [P, P])
    k.iota_n = k.sb("iota_n", [P, P])
    k.no_node = k.sb("no_node", [P, 1])
    k.onehot_a = k.sb("onehot_a", [NA, E], BF16)
    k.mask_b = k.sb("mask_b", [TE, ET, NB], BF16)
    k.keep = k.sb("keep", [ER, EC])
    k.stop_rev = k.sb("stop_rev", [ER, EC])
    k.row_stop = k.sb("row_stop", [4, ER])
    k.row_first = k.sb("row_first", [ER, 1], I32)
    k.step_tile_p = k.sb("step_tile_p", [VP, VC], I32)
    k.edge_tile = k.sb("edge_tile", [1, STEPS // LIST, LOAD], I32)
    k.node_tile_before = k.sb("node_tile_before", [1, STEPS // LIST + 1, LOAD], I32)
    k.step_src = k.sb("step_src", [TE, STEPS], I32)
    k.step_dst = k.sb("step_dst", [TE, STEPS])
    k.start_at = k.sb("start_at", [P, NT], I32)
    k.start_rev = k.sb("start_rev", [P, NT], I32)
    k.dst_rows = k.dram("dst_rows", [ET, TE])
    k.src_rows = k.dram("src_rows", [ET, TE])
    src_a_row = k.dram("src_a_row", [ER, EC], BF16)
    k.spread = {4: k.dram("spread4", [E, 8]), 1: k.dram("spread1", [E, 2])}

    tmp = ExitStack()
    with tmp:
        def sb(name, shape, dt=FP32):
            return k.sb(name, shape, dt, tmp)

        iota_i = sb("iota_i", [P, NPAD], I32)
        iota_f = sb("iota_f", [P, NPAD])
        part_i = sb("part_i", [P, 1], I32)
        part_f = sb("part_f", [P, 1])
        node_i = sb("node_i", [P, NT], I32)
        node_f = sb("node_f", [P, NT])
        tile_i = sb("tile_i", [ER, KR], I32)
        step_i = sb("step_i", [VP, VC], I32)
        step_f = sb("step_f", [VP, VC])
        dst_i = sb("dst_i", [ER, EC], I32)
        src_i = sb("src_i", [ER, EC], I32)
        prev_i = sb("prev_i", [ER, EC], I32)
        next_i = sb("next_i", [ER, EC], I32)
        dst_f = sb("dst_f", [ER, EC])
        src_f = sb("src_f", [ER, EC])
        next_f = sb("next_f", [ER, EC])
        src_a = sb("src_a", [ER, EC], BF16)
        src_b = sb("src_b", [ER, EC], I32)
        src_bf = sb("src_bf", [ER, EC])
        src_bt = sb("src_bt", [TE, ET])
        next_t = sb("next_t", [TE, KR, ER])
        key_i = sb("key_i", [ER, KR], I32)
        key_f = sb("key_f", [ER, KR])
        passed = sb("passed", [ER, KR, STEPS])
        ones = sb("ones", [P, 1])
        ones_b = sb("ones_b", [P, 1], BF16)
        below = sb("below", [ER, KR, NPAD], BF16)
        zeros = sb("zeros", [ER, KR * P])
        rowflag = sb("rowflag", [ER, 1])
        rowflag4 = sb("rowflag4", [ER, 4])
        node_tile = sb("node_tile", [P, NT], I32)
        node_tile_f = sb("node_tile_f", [P, NT])
        node_row = sb("node_row", [P, NT], I32)
        rows = sb("rows", [P, NT, TE])
        cmp = sb("cmp", [P, NT, TE])
        count = sb("count", [P, NT])
        has = sb("has", [P, NT])
        start = sb("start", [P, NT])
        tab_f = sb("tab_f", [1, 2, STEPS + SUM_LAG])
        win = sb("win", [VP, VC])
        src_v = sb("src_v", [VP, VC, TE])
        dst_v = sb("dst_v", [VP, VC, TE])

        ps_t = k.ps("prep_t", [TE, KR, P], FP32, tmp)
        ps_r = k.ps("prep_r", [ER, 512], FP32, tmp)
        ps_s = k.ps("prep_s", [P, 512], FP32, tmp)
        ps_n = k.ps("prep_n", [P, 512], FP32, tmp)

        edges_in = k.sem("edges_in")
        consts = k.sem("consts")
        pool_chain = k.sem("pool_chain0")
        dve_chain = k.sem("dve_chain0")
        floats = k.sem("floats")
        rows_ready = k.sem("rows_ready")
        rows_out = k.sem("rows_out")
        a_ready = k.sem("a_ready")
        a_out = k.sem("a_out")
        a_in = [k.sem(f"a_in{i}") for i in range(4)]
        passed_ready = k.sem("passed_ready")
        steps_ready = k.sem("steps_ready")
        below_ready = k.sem("below_ready")
        tiles_ready = k.sem("tiles_ready")
        tile_idx = k.sem("tile_idx")
        rows_in = k.sem("rows_in")
        step_idx = k.sem("step_idx")
        step_rows = k.sem("step_rows")
        rows_preset = k.sem("rows_preset")
        tr = k.sem("prep_tr")
        tr_used = k.sem("prep_tr_used")
        b_ready = k.sem("b_ready")
        v_fixed = k.sem("v_fixed")
        flag_ready = k.sem("flag_ready")
        zero_ready = k.sem("zero_ready")
        zero_out = k.sem("zero_out")

        d1 = dst.rearrange("(p j) -> p j", j=EC)
        s1 = src.rearrange("(p j) -> p j", j=EC)
        block = tmp.enter_context(nc.Block())

        @block.gpsimd
        def _(pool):
            link = chain(pool, pool_chain)
            pool.iota(part_i[:, :], [[0, 1]], base=0, channel_multiplier=1).then_inc(consts, 1)
            pool.iota(tile_i[:, :], [[1, KR]], base=0, channel_multiplier=KR).then_inc(consts, 1)
            pool.iota(iota_i[:, :], [[1, NPAD]], base=0, channel_multiplier=0).then_inc(consts, 1)
            pool.iota(node_i[:, :], [[P, NT]], base=0, channel_multiplier=1).then_inc(consts, 1)
            pool.iota(step_i[:, :], [[VP, VC]], base=0, channel_multiplier=1).then_inc(consts, 1)
            pool.memset(ones[:, :], 1.0).then_inc(consts, 1)
            pool.memset(ones_b[:, :], 1.0).then_inc(consts, 1)
            link(pool.memset(k.ident[:, :], 0.0))
            link(pool.memset(k.mirror[:, :], 0.0))
            link(pool.memset(k.no_node[:, :], 1.0))
            pool.affine_select(out=k.no_node[:, :], in_=k.no_node[:, :], compare_op=ALU.is_ge, fill=0.0,
                               base=-NLAST, pattern=[[0, 1]], channel_multiplier=1)
            pool.affine_select(out=k.ident[:, :], in_=k.ident[:, :], compare_op=ALU.not_equal, fill=1.0,
                               base=0, pattern=[[-1, P]], channel_multiplier=1).then_inc(consts, 1)
            pool.affine_select(out=k.mirror[:, :], in_=k.mirror[:, :], compare_op=ALU.not_equal, fill=1.0,
                               base=1 - P, pattern=[[1, P]], channel_multiplier=1).then_inc(consts, 1)
            pool.wait_ge(step_idx, 1)
            pool.wait_ge(rows_preset, 2)
            pool.wait_ge(rows_out, 32)
            for c in range(VC):
                at = bass.IndirectOffsetOnAxis(ap=k.step_tile_p[:, c:c + 1], axis=0)
                pool.indirect_dma_start(src_v[:, c, :], None, k.src_rows, at, bounds_check=ET - 1,
                                        oob_is_err=False).then_inc(step_rows, 16)
                pool.indirect_dma_start(dst_v[:, c, :], None, k.dst_rows, at, bounds_check=ET - 1,
                                        oob_is_err=False).then_inc(step_rows, 16)
            pool.wait_ge(tile_idx, 1)
            for i in range(NT):
                pool.indirect_dma_start(rows[:, i, :], None, k.dst_rows,
                                        bass.IndirectOffsetOnAxis(ap=node_row[:, i:i + 1], axis=0),
                                        bounds_check=ET - 1, oob_is_err=False).then_inc(rows_in, 16)

        @block.sync
        def _(sp):
            sp.dma_start(dst_i[:, :], d1).then_inc(edges_in, 16)
            sp.dma_start(src_i[:, :], s1).then_inc(edges_in, 16)
            sp.wait_ge(rows_preset, 4)
            sp.dma_start(prev_i[0:1, 1:EC], dst[0:EC - 1].rearrange("(a n) -> a n", a=1)).then_inc(edges_in, 16)
            sp.dma_start(prev_i[1:ER, :], dst[EC - 1:E - 1].rearrange("(p j) -> p j", j=EC)).then_inc(edges_in, 16)
            sp.dma_start(next_i[0:ER - 1, :], dst[1:E - EC + 1].rearrange("(p j) -> p j", j=EC)).then_inc(edges_in, 16)
            sp.dma_start(next_i[ER - 1:ER, 0:EC - 1],
                         dst[E - EC + 1:E].rearrange("(a n) -> a n", a=1)).then_inc(edges_in, 16)
            sp.wait_ge(rows_ready, 2)
            sp.dma_start(k.dst_rows.rearrange("(p c) q -> p (c q)", c=KR), dst_f[:, :]).then_inc(rows_out, 16)
            sp.dma_start(k.src_rows.rearrange("(p c) q -> p (c q)", c=KR), src_f[:, :]).then_inc(rows_out, 16)
            sp.wait_ge(a_ready, 1)
            sp.dma_start(src_a_row, src_a[:, :]).then_inc(a_out, 16)
            sp.wait_ge(a_out, 16)
            whole = src_a_row.rearrange("p j -> (p j)").rearrange("(a n) -> a n", a=4)
            for i in range(4):
                part = whole[i:i + 1, :]
                sp.dma_start(k.onehot_a[:, i * (E // 4):(i + 1) * (E // 4)],
                             bass.AP(tensor=part.tensor, offset=part.offset, ap=[[0, NA], [1, E // 4]])
                             ).then_inc(a_in[i], 16)
            sp.wait_ge(zero_ready, 1)
            for width, at in ((8, k.spread[4]), (2, k.spread[1])):
                flat = at.rearrange("(p j) c -> p (j c)", p=ER)
                cols = EC * width
                for c in range(0, cols, 500):
                    sp.dma_start(flat[:, c:c + 500], zeros[:, 0:500]).then_inc(zero_out, 16)
            sp.wait_ge(zero_out, 16 * 10)

        @block.tensor
        def _(pe):
            pe.wait_ge(consts, 9)
            pe.wait_ge(passed_ready, 1)
            for c in range(KR):
                pe.matmul(ps_r[0:1, 0:STEPS], ones[0:ER, :], passed[:, c, :], start=c == 0, stop=c == KR - 1)
            for v in range(VC):
                for c in range(KR):
                    last = pe.matmul(ps_s[0:VP, v:v + 1], passed[:, c, v * VP:(v + 1) * VP], ones[0:ER, :],
                                     start=c == 0, stop=c == KR - 1)
            last.then_inc(steps_ready, 1)
            pe.wait_ge(below_ready, 1)
            for i in range(NT):
                for c in range(KR):
                    last = pe.matmul(ps_n[:, i:i + 1], below[:, c, i * P:(i + 1) * P], ones_b[0:ER, :],
                                     start=c == 0, stop=c == KR - 1)
            last.then_inc(tiles_ready, 1)
            pe.wait_ge(b_ready, 1)
            for c in range(KR):
                last = pe.transpose(ps_t[:, c, 0:ER], src_bf[:, c * TE:(c + 1) * TE], k.ident[0:ER, 0:ER])
            last.then_inc(tr, 1)
            pe.wait_ge(tr_used, 1)
            for c in range(KR):
                last = pe.transpose(ps_t[:, c, 0:ER], next_f[:, c * TE:(c + 1) * TE], k.ident[0:ER, 0:ER])
            last.then_inc(tr, 1)
            pe.wait_ge(tr_used, 2)
            for c in range(KR):
                last = pe.matmul(ps_r[:, (KR - 1 - c) * TE:(KR - c) * TE], next_t[:, c, :],
                                 k.mirror[0:TE, P - TE:P], start=True, stop=True)
            last.then_inc(tr, 1)
            pe.wait_ge(flag_ready, 1)
            pe.matmul(ps_s[0:4, 128:128 + ER], rowflag4[:, :], k.mirror[0:ER, P - ER:P],
                      start=True, stop=True).then_inc(tr, 1)
            pe.wait_ge(v_fixed, 1)
            pe.wait_ge(tr_used, 3)
            for c in range(VC):
                last = pe.transpose(ps_t[:, c, 0:VP], src_v[:, c, :], k.ident[0:VP, 0:VP])
            last.then_inc(tr, 1)
            pe.wait_ge(tr_used, 4)
            for c in range(VC):
                last = pe.transpose(ps_t[:, c, 0:VP], dst_v[:, c, :], k.ident[0:VP, 0:VP])
            last.then_inc(tr, 1)

        @block.vector
        def _(dve):
            link = chain(dve, dve_chain)
            dve.memset(prev_i[:, :], -1).then_inc(rows_preset, 1)
            dve.memset(next_i[:, :], -1).then_inc(rows_preset, 1)
            dve.memset(src_v[:, :, :], 0.0).then_inc(rows_preset, 1)
            dve.memset(dst_v[:, :, :], -1.0).then_inc(rows_preset, 1)
            dve.memset(zeros[:, :], 0.0).then_inc(zero_ready, 1)
            dve.wait_ge(edges_in, 16 * 6)
            dve.tensor_copy(dst_f[:, :], dst_i[:, :]).then_inc(rows_ready, 1)
            dve.tensor_copy(src_f[:, :], src_i[:, :]).then_inc(rows_ready, 1)
            link(dve.tensor_scalar(src_b[:, :], src_i[:, :], float(DIV_MUL), None, ALU.mult))
            link(dve.tensor_scalar(src_b[:, :], src_b[:, :], DIV_SHIFT, None, ALU.logical_shift_right))
            dve.tensor_copy(src_a[:, :], src_b[:, :]).then_inc(a_ready, 1)
            dve.scalar_tensor_tensor(src_bf[:, :], src_b[:, :], -float(NB), src_i[:, :], ALU.mult,
                                     ALU.add).then_inc(b_ready, 1)
            dve.wait_ge(consts, 9)
            link(dve.tensor_scalar(key_i[:, :], dst_i[:, TE - 1::TE], 7, None, ALU.logical_shift_right))
            link(dve.tensor_tensor(key_f[:, :], key_i[:, :], tile_i[:, :], ALU.add))
            link(dve.tensor_copy(iota_f[:, :], iota_i[:, :]))
            dve.tensor_copy(k.iota_n[:, :], iota_i[:, 0:P])
            for c in range(KR):
                last = dve.tensor_scalar(passed[:, c, :], iota_f[0:ER, 0:STEPS], key_f[:, c:c + 1], None, ALU.is_gt)
            last.then_inc(passed_ready, 1)
            dve.wait_ge(rows_ready, 2)
            for c in range(KR):
                last = dve.tensor_scalar(below[:, c, :], iota_f[0:ER, :], dst_f[:, (c + 1) * TE - 1:(c + 1) * TE],
                                         None, ALU.is_gt)
            last.then_inc(below_ready, 1)
            link(dve.tensor_tensor(k.keep[:, :], prev_i[:, :], dst_i[:, :], ALU.is_equal))
            link(dve.tensor_tensor(next_f[:, :], next_i[:, :], dst_i[:, :], ALU.is_equal))
            link(dve.tensor_reduce(rowflag[:, :], next_f[:, :], AX_X, ALU.min))
            dve.tensor_scalar(rowflag4[:, :], bcast(rowflag[:, 0:1], [[0, 4]]), -1.0, -NEG, ALU.add,
                              ALU.mult).then_inc(flag_ready, 1)
            link(dve.tensor_copy(k.row_first[:, :], dst_i[:, 0:1]))
            link(dve.tensor_copy(part_f[:, :], part_i[:, :]))
            link(dve.tensor_copy(node_f[:, :], node_i[:, :]))
            link(dve.tensor_copy(step_f[:, :], step_i[:, :]))
            dve.wait_ge(steps_ready, 1)
            link(dve.tensor_copy(k.step_tile_p[:, :], ps_s[0:VP, 0:VC]))
            dve.sem_inc(step_idx, 1)
            link(dve.tensor_tensor(win[:, :], step_f[:, :], ps_s[0:VP, 0:VC], ALU.subtract))
            link(dve.tensor_scalar(win[:, :], win[:, :], float(NT - 1), float(P), ALU.min, ALU.mult))
            link(dve.memset(tab_f[:, :, :], 0.0))
            link(dve.tensor_scalar(tab_f[:, 0, 0:STEPS], ps_r[0:1, 0:STEPS], float(ET - 1), None, ALU.min))
            link(dve.tensor_tensor(tab_f[:, 1, SUM_LAG:STEPS + SUM_LAG], iota_f[0:1, 0:STEPS], tab_f[:, 0, 0:STEPS], ALU.subtract))
            link(dve.tensor_scalar(tab_f[:, 1, :], tab_f[:, 1, :], float(NT - 1), None, ALU.min))
            dve.tensor_copy(k.edge_tile[:, :, 0:LIST], tab_f[:, 0, 0:STEPS].rearrange("a (i s) -> a i s", s=LIST))
            dve.tensor_copy(k.node_tile_before[:, STEPS // LIST, 0:SUM_LAG], tab_f[:, 1, STEPS:STEPS + SUM_LAG])
            dve.tensor_copy(k.node_tile_before[:, 0:STEPS // LIST, 0:LIST], tab_f[:, 1, 0:STEPS].rearrange("a (i s) -> a i s", s=LIST))
            dve.wait_ge(tiles_ready, 1)
            link(dve.tensor_scalar(node_tile_f[:, :], ps_n[:, 0:NT], float(ET - 1), None, ALU.min))
            dve.tensor_copy(node_row[:, :], node_tile_f[:, :]).then_inc(tile_idx, 1)
            dve.wait_ge(tile_idx, 1)
            dve.wait_ge(tr, 1)
            for c in range(KR):
                last = dve.tensor_copy(src_bt[:, c::KR], ps_t[:, c, 0:ER])
            last.then_inc(tr_used, 1)
            dve.wait_ge(tr, 2)
            dve.tensor_copy(next_t[:, :, :], ps_t[:, :, 0:ER]).then_inc(tr_used, 1)
            dve.wait_ge(tr, 4)
            dve.wait_ge(tr_used, 2)
            dve.tensor_scalar(k.stop_rev[:, :], ps_r[:, 0:EC], -1.0, -NEG, ALU.add, ALU.mult)
            dve.tensor_copy(k.row_stop[:, :], ps_s[0:4, 128:128 + ER]).then_inc(tr_used, 1)
            dve.wait_ge(step_rows, 16 * 2 * VC)
            for c in range(VC):
                last = dve.tensor_scalar(dst_v[:, c, :], dst_v[:, c, :], win[:, c:c + 1], None, ALU.subtract)
            last.then_inc(v_fixed, 1)
            dve.wait_ge(tr, 5)
            for c in range(VC):
                last = dve.tensor_copy(k.step_src[:, c * VP:(c + 1) * VP], ps_t[:, c, 0:VP])
            last.then_inc(tr_used, 1)
            dve.tensor_tensor(k.mask_b[:, :, :], bcast(k.iota_n[0:TE, 0:NB], [[0, ET], [1, NB]]),
                              bcast(src_bt[:, :], [[1, ET], [0, NB]]), ALU.is_equal)
            for i in range(4):
                dve.wait_ge(a_in[i], 16)
                part = k.onehot_a[:, i * (E // 4):(i + 1) * (E // 4)]
                dve.tensor_scalar(part, part, part_f[0:NA, :], None, ALU.is_equal)
            dve.wait_ge(tr, 6)
            for c in range(VC):
                last = dve.tensor_copy(k.step_dst[:, c * VP:(c + 1) * VP], ps_t[:, c, 0:VP])
            last.then_inc(tr_used, 1)
            dve.wait_ge(rows_in, 16 * NT)
            node_b = bcast(node_f[:, :], [[1, NT], [0, TE]])
            link(dve.tensor_tensor(cmp[:, :, :], rows[:, :, :], node_b, ALU.is_lt))
            link(dve.tensor_reduce(count[:, :], cmp[:, :, :], AX_X, ALU.add))
            link(dve.tensor_tensor(cmp[:, :, :], rows[:, :, :], node_b, ALU.is_equal))
            link(dve.tensor_reduce(has[:, :], cmp[:, :, :], AX_X, ALU.max))
            link(dve.scalar_tensor_tensor(start[:, :], node_tile_f[:, :], float(TE), count[:, :], ALU.mult, ALU.add))
            link(dve.tensor_scalar(has[:, :], has[:, :], -float(SKIP), float(SKIP), ALU.mult, ALU.add))
            link(dve.tensor_tensor(k.start_at[:, :], start[:, :], has[:, :], ALU.add))
            link(dve.tensor_scalar(node_tile[:, :], node_row[:, :], 2, None, ALU.logical_shift_right))
            link(dve.tensor_scalar(count[:, :], node_tile[:, :], float(2 * EC), float(EC - 1), ALU.mult, ALU.add))
            link(dve.tensor_tensor(count[:, :], count[:, :], start[:, :], ALU.subtract))
            link(dve.tensor_tensor(k.start_rev[:, :], count[:, :], has[:, :], ALU.add))


def at_least(eng, sem, value):
    if not isinstance(value, int) or value > 0:
        eng.wait_ge(sem, value)


def rolled(eng, n, body):
    body(0)
    with eng.Fori(1, n - 1) as it:
        body(it)
    body(n - 1)


def rolled_with(eng, n, upto, body):
    body(0, True)
    with eng.Fori(1, min(upto, n - 1)) as it:
        body(it, True)
    for it in range(upto, n - 1):
        body(it, False)
    body(n - 1, upto >= n)


def step_list(eng, regs, table, i, n):
    eng.load(regs, table[0:1, bass.ds(i, 1), 0:len(regs)].rearrange("a i s -> a (i s)"))
    return [eng.snap(r, min_val=0, max_val=n - 1) for r in regs]


def load_weights(k, x, w1, att_s1, att_d1, b1, w2, att_s2, att_d2, b2, w_node, b_node, w_edge, b_edge,
                 w_dist, b_dist, w_comb):
    nc = k.nc
    H, C = att_s1.shape
    k.x = k.sb("x_nodes", [P, NT, D])
    k.nodes = k.sb("nodes", [P, NT, D + 4])
    k.w1 = k.sb("w1_ext", [P, 2, D + 8])
    k.w2 = k.sb("w2_ext", [P, 2, D + 2])
    k.wn = k.sb("w_node", [P, 2, HID])
    k.b1 = k.sb("b1_row", [P, D])
    k.b2 = k.sb("b2_row", [P, D])
    k.bn = k.sb("bn_row", [P, HID])
    k.w_edge_comb = k.sb("w_edge_comb", [DE, D])
    k.w_comb1 = k.sb("w_comb1", [HID, D])
    k.w_dist = k.sb("w_dist_ext", [DC + 1, HID])
    k.bias3 = k.sb("bias3", [DC + 1, D], BF16)
    k.ones3 = k.sb("ones3", [DC + 1, P], BF16)
    tmp = ExitStack()
    with tmp:
        att = k.sb("att", [P, 4, D], FP32, tmp)
        prod = k.sb("att_prod", [P, 2, D], FP32, tmp)
        we = k.sb("w_edge", [DE, HID], FP32, tmp)
        wet = k.sb("w_edge_t", [HID, DE], FP32, tmp)
        wc2 = k.sb("w_comb2", [HID, D], FP32, tmp)
        be = k.sb("b_edge", [HID, 1], FP32, tmp)
        rest = k.sb("bias_rest", [DC + 1, D], FP32, tmp)
        pt = k.ps("w_pt", [P, 512], FP32, tmp)
        pw = k.ps("w_pw", [P, 512], FP32, tmp)
        pb = k.ps("w_pb", [P, 512], FP32, tmp)
        preset = k.sem("w_preset")
        loaded = k.sem("w_loaded")
        turned = k.sem("w_turned")
        turned_out = k.sem("w_turned_out")
        folded = k.sem("w_folded")
        dve_chain = k.sem("w_chain")
        block = tmp.enter_context(nc.Block())

        def everywhere(ap, n):
            return bass.AP(tensor=ap.tensor, offset=ap.offset, ap=[[0, P], [1, n]])

        @block.sync
        def _(sp):
            sp.wait_ge(preset, 1)
            sp.dma_start(k.x[:, 0:NT - 1, :], x[0:(NT - 1) * P, :].rearrange("(i p) c -> p i c", p=P)).then_inc(loaded, 16)
            sp.dma_start(k.x[0:NLAST, NT - 1, :], x[(NT - 1) * P:N, :]).then_inc(loaded, 16)
            sp.dma_start(k.w1[:, :, 0:D], w1.rearrange("(c p) n -> p c n", p=P)).then_inc(loaded, 16)
            sp.dma_start(k.w2[:, :, 0:D], w2.rearrange("(c p) n -> p c n", p=P)).then_inc(loaded, 16)
            sp.dma_start(k.wn[:, :, :], w_node.rearrange("(c p) n -> p c n", p=P)).then_inc(loaded, 16)
            sp.dma_start(k.w_comb1[:, :], w_comb[0:HID, :]).then_inc(loaded, 16)
            sp.dma_start(wc2[:, :], w_comb[HID:2 * HID, :]).then_inc(loaded, 16)
            sp.dma_start(we[:, :], w_edge).then_inc(loaded, 16)
            sp.dma_start(k.w_dist[0:DC, :], w_dist).then_inc(loaded, 16)

        @block.scalar
        def _(act):
            for n, a in enumerate((att_s1, att_d1, att_s2, att_d2)):
                act.dma_start(att[:, n, :], everywhere(a, D)).then_inc(loaded, 16)
            act.dma_start(k.b1[:, :], everywhere(b1, D)).then_inc(loaded, 16)
            act.dma_start(k.b2[:, :], everywhere(b2, D)).then_inc(loaded, 16)
            act.dma_start(k.bn[:, :], everywhere(b_node, HID)).then_inc(loaded, 16)
            act.dma_start(k.w_dist[DC:DC + 1, :], b_dist.rearrange("(a n) -> a n", a=1)).then_inc(loaded, 16)
            act.dma_start(be[:, :], b_edge.rearrange("(n a) -> n a", a=1)).then_inc(loaded, 16)

        @block.tensor
        def _(pe):
            pe.wait_ge(loaded, 16 * 18)
            pe.transpose(pt[:, 0:DE], we[:, :], k.ident[:, :]).then_inc(turned, 1)
            pe.wait_ge(turned_out, 1)
            pe.matmul(pw[:, 0:D], wet[:, :], wc2[:, :], start=True, stop=True)
            pe.matmul(pb[0:DC + 1, 0:D], bcast(be[:, :], [[0, DC + 1]]), wc2[:, :], start=True,
                      stop=True).then_inc(folded, 1)

        @block.vector
        def _(dve):
            link = chain(dve, dve_chain)
            dve.memset(k.x[:, NT - 1, :], 0.0).then_inc(preset, 1)
            link(dve.memset(k.bias3[:, :], 0.0))
            dve.memset(k.ones3[:, :], 1.0)
            dve.wait_ge(loaded, 16 * 18)
            for n, (w, heads) in enumerate(((k.w1, H), (k.w1, H), (k.w2, 1), (k.w2, 1))):
                link(dve.tensor_tensor(prod[:, :, :], w[:, :, 0:D], bcast(att[:, n, :], [[0, 2], [1, D]]), ALU.mult))
                at = D + heads * (n % 2)
                link(dve.tensor_reduce(w[:, :, at:at + heads],
                                       prod[:, :, :].rearrange("p c (h n) -> p c h n", h=heads), AX_X, ALU.add))
            dve.wait_ge(turned, 1)
            dve.tensor_copy(wet[:, :], pt[:, 0:DE]).then_inc(turned_out, 1)
            dve.wait_ge(folded, 1)
            dve.tensor_copy(k.w_edge_comb[:, :], pw[:, 0:D])
            link(dve.tensor_copy(rest[:, :], pb[0:DC + 1, 0:D]))
            link(dve.tensor_copy(k.bias3[0:1, :], rest[0:1, :]))
            part = k.sb("bias_part", [DC + 1, D], BF16, tmp)
            for n in range(2):
                link(dve.tensor_copy(part[:, :], rest[:, :]))
                link(dve.tensor_tensor(rest[:, :], rest[:, :], part[:, :], ALU.subtract))
                row = 32 * (n + 1)
                link(dve.tensor_copy(k.bias3[row:row + 1, :], rest[row:row + 1, :]))


def project_nodes(k, name, x_in, heads_in, norm, w, heads, table, table_dram, alpha, bias=None):
    nc = k.nc
    cols = w.shape[2]
    tmp = ExitStack()
    with tmp:
        stats = k.sb(name + "stats", [P, NT, 6], FP32, tmp)
        ones = k.sb(name + "ones", [P, max(heads, 1)], FP32, tmp)
        mv = k.sb(name + "mv", [P, NT, 2], FP32, tmp)
        rstd = k.sb(name + "rstd", [P, NT], FP32, tmp)
        shift = k.sb(name + "shift", [P, NT], FP32, tmp)
        eps = k.sb(name + "eps", [P, 1], FP32, tmp)
        h = k.sb(name + "h", [P, 2, D], FP32, tmp)
        ht = k.sb(name + "ht", [P, 2, 2, P], FP32, tmp)
        ps_t = [k.ps(f"{name}ps_t{i}", [P, 2, P], FP32, tmp) for i in range(2)]
        ps_o = [k.ps(f"{name}ps_o{i}", [P, cols], FP32, tmp) for i in range(2)]
        aggr = k.sem(name + "aggr")
        root = k.sem(name + "root")
        normed = k.sem(name + "normed")
        h_ready = k.sem(name + "h_ready")
        h_turned = k.sem(name + "h_turned")
        ht_ready = k.sem(name + "ht_ready")
        projected = k.sem(name + "projected")
        out_ready = k.sem(name + "out_ready")
        stored = k.sem(name + "stored")
        dve_chain = k.sem(name + "chain")
        stat_chain = k.sem(name + "stat_chain")
        block = tmp.enter_context(nc.Block())
        CH = 5
        width = table.shape[2]

        @block.gpsimd
        def _(pool):
            pool.memset(eps[:, :], EPS).then_inc(aggr, 1)

        @block.sync
        def _(sp):
            view = table_dram.rearrange("(i p) c -> p i c", p=P)
            for i in range(0, NT, CH):
                sp.wait_ge(out_ready, i + CH)
                sp.dma_start(view[:, i:i + CH, :], table[:, i:i + CH, :]).then_inc(stored, 16)
            if heads:
                sp.dma_start(k.alpha_dram[heads].rearrange("(i p) c -> p i c", p=P),
                             alpha[:, :, :]).then_inc(stored, 16)
            sp.wait_ge(stored, 16 * (NT // CH + (1 if heads else 0)))

        @block.scalar
        def _(act):
            if norm:
                act.wait_ge(aggr, 2)
                act.activation(rstd[:, :], mv[:, :, 1], ACT.Sqrt, bias=eps[:, :]).then_inc(root, 1)
                act.wait_ge(normed, 1)

            def body(it):
                for s in range(2):
                    v = 2 * it + s
                    at_least(act, h_turned, v - 1)
                    out = h[:, s, :]
                    tile = bass.ds(v, 1)
                    xin = x_in[:, tile, :].rearrange("p a (h c) -> p (a h) c", h=heads_in)[:, :, 0:D // heads_in]
                    out = out.rearrange("p (h c) -> p h c", h=heads_in)
                    if norm:
                        ins = act.activation(out, xin, ACT.Relu, bias=shift[:, tile], scale=rstd[:, tile])
                    else:
                        ins = act.activation(out, xin, ACT.Relu)
                    ins.then_inc(h_ready, 1)

            rolled(act, NT // 2, body)

        @block.tensor
        def _(pe):
            def turn(v, s):
                pe.wait_ge(h_ready, v + 1)
                at_least(pe, ht_ready, v - 1)
                for c in range(2):
                    last = pe.transpose(ps_t[s][:, c, :], h[:, s, c * P:(c + 1) * P], k.ident[:, :])
                last.then_inc(h_turned, 1)

            def project(v, s):
                pe.wait_ge(ht_ready, v + 1)
                at_least(pe, out_ready, v - 1)
                for c in range(2):
                    last = pe.matmul(ps_o[s][:, :], ht[:, s, c, :], w[:, c, :], start=c == 0, stop=c == 1)
                last.then_inc(projected, 1)

            turn(0, 0)

            def body(it):
                for s in range(2):
                    v = 2 * it + s
                    if not isinstance(v, int) or v + 1 < NT:
                        turn(v + 1, 1 - s)
                    project(v, s)

            rolled(pe, NT // 2, body)

        @block.vector
        def _(dve):
            link = chain(dve, dve_chain)
            link(dve.memset(ones[:, :], 1.0))
            if norm:
                def stat(it):
                    for s in range(2):
                        tile = bass.ds(2 * it + s, 1)
                        dve.bn_stats(stats[:, tile, :].rearrange("p a c -> p (a c)"),
                                     x_in[:, tile, :].rearrange("p a c -> p (a c)")).then_inc(stat_chain, 1)

                rolled(dve, NT // 2, stat)
                dve.wait_ge(stat_chain, NT)
                for i in range(NT):
                    dve.bn_aggr(mv[:, i, :], stats[:, i, :]).then_inc(stat_chain, 1)
                dve.wait_ge(stat_chain, 2 * NT)
                dve.sem_inc(aggr, 1)
                dve.wait_ge(root, 1)
                link(dve.reciprocal(rstd[:, :], rstd[:, :]))
                dve.scalar_tensor_tensor(shift[:, :], mv[:, :, 0], -1.0, rstd[:, :], ALU.mult,
                                         ALU.mult).then_inc(normed, 1)

            def copy(v, s):
                dve.wait_ge(h_turned, v + 1)
                at_least(dve, projected, v - 1)
                dve.tensor_copy(ht[:, s, :, :], ps_t[s][:, :, :]).then_inc(ht_ready, 1)

            def keep(v, s):
                dve.wait_ge(projected, v + 1)
                tile = bass.ds(v, 1)
                to = table[:, tile, :].rearrange("p a c -> p (a c)")
                if heads:
                    dve.tensor_copy(to.rearrange("p (h c) -> p h c", h=heads)[:, :, D // heads], ones[:, :])
                    dve.tensor_copy(to.rearrange("p (h c) -> p h c", h=heads)[:, :, 0:D // heads],
                                    ps_o[s][:, 0:D].rearrange("p (h c) -> p h c", h=heads))
                    dve.tensor_copy(alpha[:, tile, :].rearrange("p a c -> p (a c)"),
                                    ps_o[s][:, D:D + 2 * heads]).then_inc(out_ready, 1)
                else:
                    dve.tensor_tensor(to, ps_o[s][:, :], bias[:, :], ALU.add).then_inc(out_ready, 1)

            copy(0, 0)

            def body(it):
                for s in range(2):
                    v = 2 * it + s
                    if not isinstance(v, int) or v + 1 < NT:
                        copy(v + 1, 1 - s)
                    keep(v, s)

            rolled(dve, NT // 2, body)


def edge_weights(k, name, H, alpha, table, step_ex, table_dram, got, got_ready):
    nc = k.nc
    W = 2 * H
    G = 400 // (H * NB)
    groups = ET // G
    alpha_dram = k.alpha_dram[H]
    spread = k.spread[H]
    max_rev = k.dram(name + "max_rev", [E, H])
    am_dram = k.dram(name + "am", [NPAD, W])
    ex_rows = k.dram(name + "ex_rows", [ET, H * TE])
    outer = ExitStack()
    with outer:
        as_t = k.sb(name + "as_t", [TE, ET, H], FP32, outer)
        inner = ExitStack()
        with inner:
            tab = k.sb(name + "tab", [NA, NB, W], FP32, inner)
            rest = k.sb(name + "rest", [NA, H, NB], FP32, inner)
            parts = k.sb(name + "parts", [NA, 3, H, NB], BF16, inner)
            picked = k.sb(name + "picked", [TE, 2, G, H, NB], FP32, inner)
            staged = k.sb(name + "staged", [NA, 2, G * TE + P - TE], BF16, inner)
            ps = [k.ps(f"{name}pick{i}", [P, G, H, NB], FP32, inner) for i in range(2)]
            tab_in = k.sem(name + "tab_in")
            split = k.sem(name + "split")
            rows_read = k.sem(name + "rows_read")
            masked = k.sem(name + "masked")
            staged_ready = k.sem(name + "staged_ready")
            ends_preset = k.sem(name + "ends_preset")
            summed = k.sem(name + "summed")
            block = inner.enter_context(nc.Block())

            @block.sync
            def _(sp):
                sp.dma_start(tab[:, :, :], alpha_dram[0:N, :].rearrange("(a b) h -> a b h", b=NB)).then_inc(tab_in, 16)

            @block.vector
            def _(dve):
                link = chain(dve, split)
                dve.wait_ge(tab_in, 16)
                link(dve.tensor_copy(rest[:, :, :], tab[:, :, 0:H].rearrange("a b h -> a h b")))
                for n in range(3):
                    link(dve.tensor_copy(parts[:, n, :, :], rest[:, :, :]))
                    if n < 2:
                        link(dve.tensor_tensor(rest[:, :, :], rest[:, :, :], parts[:, n, :, :], ALU.subtract))

                def body(it):
                    for s in range(2):
                        g = 2 * it + s
                        dve.wait_ge(rows_read, g + 1)
                        at_least(dve, summed, g - 1)
                        mask = bcast(k.mask_b[:, bass.ds(g * G, G), :], [[NB, G], [0, H], [1, NB]])
                        dve.tensor_tensor(picked[:, s, :, :, :], ps[s][0:TE, :, :, :], mask, ALU.mult).then_inc(masked, 1)
                        if not isinstance(g, int) or g > 0:
                            add_up(g - 1, 1 - s)

                def add_up(g, s):
                    dve.wait_ge(masked, g + 1)
                    dve.tensor_reduce(as_t[:, bass.ds(g * G, G), :], picked[:, s, :, :, :], AX_X,
                                      ALU.add).then_inc(summed, 1)

                rolled(dve, groups // 2, body)
                add_up(groups - 1, 1)

            @block.scalar
            def _(act):
                def body(it):
                    for s in range(2):
                        g = 2 * it + s
                        at_least(act, rows_read, g - 1)
                        act.activation(staged[:, s, 0:G * TE], k.onehot_a[:, bass.ds(g * (G * TE), G * TE)],
                                       ACT.Copy).then_inc(staged_ready, 1)

                rolled(act, groups // 2, body)

            @block.gpsimd
            def _(pool):
                pool.memset(staged[:, :, G * TE:], 0.0).then_inc(ends_preset, 1)
                for s in range(RING):
                    pool.indirect_dma_start(got[:, s, :], None, table_dram,
                                            bass.IndirectOffsetOnAxis(ap=k.step_src[:, s:s + 1], axis=0)
                                            ).then_inc(got_ready[s], 16)

            @block.tensor
            def _(pe):
                pe.wait_ge(split, 6)
                pe.wait_ge(ends_preset, 1)

                def body(it):
                    for s in range(2):
                        g = 2 * it + s
                        pe.wait_ge(staged_ready, g + 1)
                        at_least(pe, masked, g - 1)
                        for j in range(G):
                            for n in range(3):
                                last = pe.matmul(ps[s][:, j, :, :], staged[:, s, j * TE:j * TE + P],
                                                 parts[:, n, :, :], start=n == 0, stop=n == 2)
                        last.then_inc(rows_read, 1)

                rolled(pe, groups // 2, body)

        tmp = outer
        turns = k.sb(name + "turns", [ER, 2, H * EC], FP32, tmp)
        as_rev = turns[:, 0, :].rearrange("p (h j) -> p h j", h=H)
        scan = turns[:, 1, :].rearrange("p (h j) -> p h j", h=H)
        sparse = turns[:, :, :].rearrange("p a n -> p (a n)").rearrange("p (j c) -> p j c", c=W)
        score = ex = as_rev
        as_rows = scan
        full_v = k.x[0:VP, 0:NT - 1, :].rearrange("p i c -> p (i c)")[:, 0:W * EC].rearrange("p (w j) -> p w j", w=W)
        full = full_v[0:ER, :, :]
        ex_v = full_v[:, 0:H, :].rearrange("p h j -> p (h j)").rearrange("p (c h q) -> p c h q", c=VC, h=H)
        max_rows = full[:, 0:H, :].rearrange("p h j -> p (h j)").rearrange("p (j h) -> p j h", h=H)
        local = k.sb(name + "local", [ER, H], FP32, tmp)
        across = k.sb(name + "across", [H, ER + 1], FP32, tmp)
        carry_r = k.sb(name + "carry_r", [ER, H], FP32, tmp)
        carry = k.sb(name + "carry", [ER, H], FP32, tmp)
        node_max = k.sb(name + "node_max", [P, NT, H], FP32, tmp)
        am = k.sb(name + "am_sb", [P, NT, W], FP32, tmp)
        self_e = k.sb(name + "self_e", [P, NT, H], FP32, tmp)
        self_x = k.sb(name + "self_x", [P, NT, H], FP32, tmp)
        first = k.sb(name + "first", [ER, W], FP32, tmp)
        banks = [k.ps(f"{name}bank{i}", [P, 512], FP32, tmp) for i in range(4)]
        small = k.ps(name + "small", [P, 512], FP32, tmp)

        def sem(n):
            return k.sem(name + n)

        rev_ready, rev_used, fwd_ready, fwd_used = sem("rev_ready"), sem("rev_used"), sem("fwd_ready"), sem("fwd_used")
        local_ready, turned, turned_used = sem("local_ready"), sem("turned"), sem("turned_used")
        max_ready, max_out, max_in, max_preset = sem("max_ready"), sem("max_out"), sem("max_in"), sem("max_preset")
        am_ready, am_out, spread_out, first_in, sparse_in = (sem("am_ready"), sem("am_out"), sem("spread_out"),
                                                             sem("first_in"), sem("sparse_in"))
        self_ready, self_done, score_ready, ex_ready = (sem("self_ready"), sem("self_done"), sem("score_ready"),
                                                        sem("ex_ready"))
        ex_out, ex_in, ex_turned, dve_chain = sem("ex_out"), sem("ex_in"), sem("ex_turned"), sem("chain")
        ex_used = sem("ex_used")
        block = tmp.enter_context(nc.Block())

        @block.sync
        def _(sp):
            sp.wait_ge(max_ready, 1)
            sp.dma_start(max_rev.rearrange("(p j) h -> p j h", j=EC), max_rows[:, :, :]).then_inc(max_out, 16)
            sp.wait_ge(am_ready, 1)
            sp.dma_start(am_dram.rearrange("(i p) c -> p i c", p=P), am[:, :, :]).then_inc(am_out, 16)
            sp.wait_ge(spread_out, 16 * NT)
            sp.dma_start(sparse[:, :, :], spread.rearrange("(p j) c -> p j c", j=EC)).then_inc(sparse_in, 16)
            sp.wait_ge(ex_ready, 1)
            to = ex_rows.rearrange("(p c) (h q) -> p h c q", c=KR, h=H)
            for h in range(H):
                sp.dma_start(to[:, h], ex[:, h, :].rearrange("p (c q) -> p c q", c=KR)).then_inc(ex_out, 16)

        @block.gpsimd
        def _(pool):
            pool.wait_ge(max_preset, 1)
            pool.wait_ge(max_out, 16)
            for i in range(NT):
                pool.indirect_dma_start(node_max[:, i, :], None, max_rev,
                                        bass.IndirectOffsetOnAxis(ap=k.start_rev[:, i:i + 1], axis=0),
                                        bounds_check=E - 1, oob_is_err=False).then_inc(max_in, 16)
            pool.wait_ge(am_ready, 1)
            for i in range(NT):
                pool.indirect_dma_start(spread, bass.IndirectOffsetOnAxis(ap=k.start_at[:, i:i + 1], axis=0),
                                        am[:, i, :], None, bounds_check=E - 1,
                                        oob_is_err=False).then_inc(spread_out, 16)
            pool.wait_ge(am_out, 16)
            pool.indirect_dma_start(first[:, :], None, am_dram,
                                    bass.IndirectOffsetOnAxis(ap=k.row_first[:, :], axis=0)).then_inc(first_in, 16)
            pool.wait_ge(max_preset, 2)
            pool.wait_ge(ex_out, 16 * H)
            for c in range(VC):
                pool.indirect_dma_start(ex_v[:, c, :, :].rearrange("p h q -> p (h q)"), None, ex_rows,
                                        bass.IndirectOffsetOnAxis(ap=k.step_tile_p[:, c:c + 1], axis=0),
                                        bounds_check=ET - 1, oob_is_err=False).then_inc(ex_in, 16)

        @block.scalar
        def _(act):
            act.wait_ge(self_ready, 1)
            act.activation(self_x[:, :, :], self_e[:, :, :], ACT.Exp).then_inc(self_done, 1)
            act.wait_ge(score_ready, 1)
            act.activation(ex[:, :, :], score[:, :, :], ACT.Exp).then_inc(ex_ready, 1)

        @block.tensor
        def _(pe):
            for h in range(H):
                for c in range(KR):
                    last = pe.matmul(banks[h][0:ER, (KR - 1 - c) * TE:(KR - c) * TE], as_t[:, c::KR, h],
                                     k.mirror[0:TE, P - TE:P], start=True, stop=True)
                last.then_inc(rev_ready, 1)
            for h in range(H):
                pe.wait_ge(rev_used, h + 1)
                for c in range(KR):
                    last = pe.transpose(banks[h][0:ER, c * TE:(c + 1) * TE], as_t[:, c::KR, h], k.ident[0:TE, 0:TE])
                last.then_inc(fwd_ready, 1)
            pe.wait_ge(local_ready, 1)
            pe.matmul(small[0:H, 0:ER], local[:, :], k.mirror[0:ER, P - ER:P], start=True, stop=True).then_inc(turned, 1)
            pe.wait_ge(turned_used, 1)
            pe.matmul(small[0:ER, 128:128 + H], across[:, 0:ER], k.ident[0:H, 0:H], start=True,
                      stop=True).then_inc(turned, 1)
            pe.wait_ge(turned_used, 2)
            pe.matmul(small[0:ER, 256:256 + H], k.mirror[0:ER, P - ER:P], carry_r[:, :], start=True,
                      stop=True).then_inc(turned, 1)
            pe.wait_ge(fwd_used, H)
            pe.wait_ge(ex_in, 16 * VC)
            for h in range(H):
                for c in range(VC):
                    last = pe.transpose(banks[h][0:TE, c * VP:(c + 1) * VP], ex_v[:, c, h, :], k.ident[0:VP, 0:VP])
                last.then_inc(ex_turned, 1)

        @block.vector
        def _(dve):
            link = chain(dve, dve_chain)
            dve.memset(node_max[:, :, :], NEG).then_inc(max_preset, 1)
            link(dve.memset(across[:, :], NEG))
            for h in range(H):
                dve.wait_ge(rev_ready, h + 1)
                dve.tensor_copy(as_rev[:, h, :], banks[h][0:ER, 0:EC]).then_inc(rev_used, 1)
            dve.wait_ge(rev_used, H)
            for h in range(H):
                link(dve.tensor_tensor_scan(scan[:, h, :], k.stop_rev[:, :], as_rev[:, h, :], NEG, ALU.add, ALU.max))
            dve.tensor_copy(local[:, :], scan[:, :, EC - 1]).then_inc(local_ready, 1)
            dve.wait_ge(turned, 1)
            link(dve.tensor_tensor_scan(across[:, 1:ER + 1], k.row_stop[0:H, :], small[0:H, 0:ER], NEG,
                                        ALU.add, ALU.max))
            dve.sem_inc(turned_used, 1)
            dve.wait_ge(turned, 2)
            dve.tensor_copy(carry_r[:, :], small[0:ER, 128:128 + H]).then_inc(turned_used, 1)
            dve.wait_ge(turned, 3)
            link(dve.tensor_copy(carry[:, :], small[0:ER, 256:256 + H]))
            for h in range(H):
                last = dve.tensor_tensor_scan(max_rows[:, :, h], k.stop_rev[:, :], as_rev[:, h, :],
                                              carry[:, h:h + 1], ALU.add, ALU.max)
                link(last)
            dve.sem_inc(max_ready, 1)
            dve.wait_ge(max_in, 16 * NT)
            link(dve.tensor_tensor(node_max[:, :, :], node_max[:, :, :], alpha[:, :, 0:H], ALU.max))
            link(dve.tensor_tensor(node_max[:, :, :], node_max[:, :, :], alpha[:, :, H:W], ALU.add))
            link(dve.tensor_copy(am[:, :, 0:H], alpha[:, :, H:W]))
            link(dve.scalar_tensor_tensor(am[:, :, H:W], node_max[:, :, :], SLOPE, node_max[:, :, :], ALU.mult, ALU.max))
            dve.sem_inc(am_ready, 1)
            link(dve.tensor_tensor(self_e[:, :, :], alpha[:, :, 0:H], alpha[:, :, H:W], ALU.add))
            link(dve.scalar_tensor_tensor(self_e[:, :, :], self_e[:, :, :], SLOPE, self_e[:, :, :], ALU.mult, ALU.max))
            dve.tensor_tensor(self_e[:, :, :], self_e[:, :, :], am[:, :, H:W], ALU.subtract).then_inc(self_ready, 1)
            dve.wait_ge(self_done, 1)
            for h in range(H):
                own = table[:, :, h * (D // H + 1):(h + 1) * (D // H + 1)]
                link(dve.tensor_tensor(own, own, bcast(self_x[:, :, h], [[H, NT], [0, D // H + 1]]), ALU.mult))
            dve.wait_ge(sparse_in, 16)
            dve.wait_ge(first_in, 16)
            for c in range(W):
                link(dve.tensor_tensor_scan(full[:, c, :], k.keep[:, :], sparse[:, :, c], first[:, c:c + 1],
                                            ALU.mult, ALU.add))
            for h in range(H):
                dve.wait_ge(fwd_ready, h + 1)
                dve.tensor_copy(as_rows[:, h, :], banks[h][0:ER, 0:EC]).then_inc(fwd_used, 1)
            dve.wait_ge(fwd_used, H)
            link(dve.tensor_tensor(score[:, :, :], as_rows[:, :, :], full[:, 0:H, :], ALU.add))
            link(dve.scalar_tensor_tensor(score[:, :, :], score[:, :, :], SLOPE, score[:, :, :], ALU.mult, ALU.max))
            dve.tensor_tensor(score[:, :, :], score[:, :, :], full[:, H:W, :], ALU.subtract).then_inc(score_ready, 1)
            dve.wait_ge(score_ready, 1)
            dve.memset(ex_v, 0.0).then_inc(max_preset, 1)
            for h in range(H):
                dve.wait_ge(ex_turned, h + 1)
                last = dve.tensor_copy(step_ex[:, :, h], banks[h][0:TE, 0:STEPS])
            last.then_inc(ex_used, 1)


def sum_messages(k, name, H, table_dram, acc, step_ex, got, got_ready, first_tile, tiles):
    nc = k.nc
    cols = D + H
    SUMS = 4
    LAST = STEPS - 1
    AHEAD = 8
    iters = tiles // PER_ITER
    tmp = ExitStack()
    with tmp:
        def sb(n, shape, dt=FP32):
            return k.sb(name + n, shape, dt, tmp)

        def sem(n):
            return k.sem(name + n)

        idx = sb("idx", [TE, RING], I32)
        onehot = sb("onehot", [TE, SUMS, P])
        msg = sb("msg", [TE, SUMS, cols]) if H > 1 else None
        ps = [k.ps(f"{name}sum{i}", [P, cols], FP32, tmp) for i in range(SUMS)]
        words = 2 * 2 * GROUP * DE
        room = (k.x[0:TE, 0:NT - 1, :].rearrange("p i c -> p (i c)")[:, 0:words] if first_tile == 0 else
                k.onehot_a[0:TE, 0:2 * words].bitcast(FP32))
        attrs = room.rearrange("p (g n t c) -> p g n t c", g=2, n=2, t=GROUP)
        attrs_t = sb("attrs_t", [DE, 2, 2, P])
        parts = sb("parts", [P, 2, GROUP, D + HID])
        ps_t = [k.ps(f"{name}turn{i}", [DE, 2, P], FP32, tmp) for i in range(2)]
        ps_p = [k.ps(f"{name}part{i}", [P, D + HID], FP32, tmp) for i in range(2)]
        idx_ready = sem("idx_ready")
        msg_ready = sem("msg_ready")
        gathers_begun = sem("gathers_begun")
        summed = sem("summed_step")
        added = sem("added")
        preset = sem("preset")
        preset_zero = sem("preset_zero")
        x_in = sem("x_in")
        attrs_in = [sem(f"attrs_in{g}") for g in range(2)]
        turned = sem("turned")
        turned_out = sem("turned_out")
        parts_made = sem("parts_made")
        parts_ready = sem("parts_ready")
        parts_out = [sem(f"parts_out{g}") for g in range(2)]
        block = tmp.enter_context(nc.Block())

        @block.sync
        def _(sp):
            def load(n, g):
                at_least(sp, turned, GROUP * (n - 1))
                at = bass.ds((first_tile + GROUP * n) * TE, GROUP * TE)
                sp.dma_start(attrs[:, g, 0, :, :], k.ea[at, :].rearrange("(t p) c -> p t c", p=TE)
                             ).then_inc(attrs_in[g], 16)
                sp.dma_start(attrs[:, g, 1, :, 0:DC], k.ed[at, :].rearrange("(t p) c -> p t c", p=TE)
                             ).then_inc(attrs_in[g], 16)

            def store(n, g):
                sp.wait_ge(parts_ready, GROUP * (n + 1))
                at = bass.ds((first_tile + GROUP * n) * P, GROUP * P)
                sp.dma_start(k.parts_dram[at, :].rearrange("(t p) c -> p t c", p=P),
                             parts[:, g, :, :]).then_inc(parts_out[g], 16)

            if first_tile > 0:
                sp.dma_start(k.x[:, 0:NT - 1, :], k.x_dram[0:(NT - 1) * P, :].rearrange("(i p) c -> p i c", p=P)
                             ).then_inc(x_in, 16)
            sp.wait_ge(preset, 3)
            load(0, 0)
            load(1, 1)

            def body(it):
                for g in range(2):
                    n = 2 * it + g
                    store(n, g)
                    if not isinstance(n, int) or n + 2 < 2 * iters:
                        load(n + 2, g)

            rolled(sp, iters, body)
            for g in range(2):
                sp.wait_ge(parts_out[g], 16 * iters)
            if first_tile > 0:
                sp.wait_ge(x_in, 16)

        @block.scalar
        def _(act):
            def index(v, s, landed):
                act.wait_ge(got_ready[s], landed)
                act.activation(idx[:, s:s + 1], k.step_src[:, bass.ds(v, 1)], ACT.Copy).then_inc(idx_ready, 1)

            def copy_turned(u, j):
                act.wait_ge(turned, u + 1)
                at_least(act, parts_made, u - 1)
                act.activation(attrs_t[:, j % 2, :, 0:TE], ps_t[j % 2][:, :, 0:TE], ACT.Copy).then_inc(turned_out, 1)

            def copy_parts(u, j, it):
                act.wait_ge(parts_made, u + 1)
                if j % GROUP == 0:
                    at_least(act, parts_out[j // GROUP], 16 * it)
                act.activation(parts[:, j // GROUP, j % GROUP, :], ps_p[j % 2][:, :], ACT.Copy).then_inc(parts_ready, 1)

            for s in range(AHEAD):
                index(RING + s, s, 16)

            def body(it, with_tiles):
                for s in range(RING):
                    v = RING * it + s
                    to = (s + AHEAD) % RING
                    if not isinstance(v, int) or v + AHEAD + RING <= LAST:
                        index(v + AHEAD + RING, to, 16 * it + 16 * (1 + (s + AHEAD) // RING))
                    u, j = PER_ITER * it + s // 2, s // 2
                    if with_tiles and s % 2 == 0:
                        copy_turned(u, j)
                    elif with_tiles:
                        copy_parts(u, j, it)

            body(0, True)
            with act.Fori(1, min(iters, STEPS // RING - 2)) as it:
                body(it, True)
            for it in range(min(iters, STEPS // RING - 2), STEPS // RING):
                body(it, it < iters)

        @block.gpsimd
        def _(pool):
            with pool.Fori(1, STEPS // RING) as it:
                for s in range(RING):
                    v = RING * it + s
                    pool.wait_ge(idx_ready, v + 1 - RING)
                    pool.wait_ge(msg_ready if H > 1 else summed, v + 1 - RING)
                    pool.sem_inc(gathers_begun, 1)
                    pool.indirect_dma_start(got[:, s, :], None, table_dram,
                                            bass.IndirectOffsetOnAxis(ap=idx[:, s:s + 1], axis=0)
                                            ).then_inc(got_ready[s], 16)

        @block.tensor
        def _(pe):
            pe.wait_ge(preset, 3)

            def turn(u, j, it):
                pe.wait_ge(attrs_in[j // GROUP], 32 * it + 32)
                at_least(pe, turned_out, u - 1)
                for n in range(2):
                    last = pe.transpose(ps_t[j % 2][:, n, 0:TE], attrs[:, j // GROUP, n, j % GROUP, :],
                                        k.ident[0:TE, 0:TE])
                last.then_inc(turned, 1)

            def products(u, j):
                pe.wait_ge(turned_out, u + 1)
                at_least(pe, parts_ready, u - 1)
                ea_t, ed_t = attrs_t[:, j % 2, 0, :], attrs_t[0:DC + 1, j % 2, 1, :]
                pe.matmul(ps_p[j % 2][:, 0:D], k.ones3[:, :], k.bias3[:, :], start=True, stop=False)
                pe.matmul(ps_p[j % 2][:, 0:D], ea_t, k.w_edge_comb[:, :], start=False, stop=True)
                pe.matmul(ps_p[j % 2][:, D:D + HID], ed_t, k.w_dist[:, :], start=True, stop=True
                          ).then_inc(parts_made, 1)

            def body(it, with_tiles):
                for s in range(RING):
                    v, b = RING * it + s, s % SUMS
                    u, j = PER_ITER * it + s // 2, s // 2
                    if with_tiles and s % 2 == 0:
                        turn(u, j, it)
                    pe.wait_ge(msg_ready, v + 1)
                    if H == 1:
                        pe.wait_ge(got_ready[s], 16 * it + 16)
                    at_least(pe, added, v + 1 - SUMS)
                    pe.matmul(ps[b][:, :], onehot[:, b, :], msg[:, b, :] if H > 1 else got[:, s, :],
                              start=True, stop=True).then_inc(summed, 1)
                    if with_tiles and s % 2 == 1:
                        products(u, j)

            rolled_with(pe, STEPS // RING, iters, body)

        @block.vector
        def _(dve):
            regs = [dve.alloc_register(f"{name}tile{s}") for s in range(LIST)]
            for n in range(2):
                dve.memset(attrs[:, n, 1, :, DC:], 0.0).then_inc(preset_zero, 1)
            dve.wait_ge(preset_zero, 2)
            dve.memset(attrs[:, 0, 1, :, DC:DC + 1], 1.0).then_inc(preset, 1)
            dve.memset(attrs[:, 1, 1, :, DC:DC + 1], 1.0).then_inc(preset, 1)
            dve.memset(attrs_t[:, :, :, TE:], 0.0).then_inc(preset, 1)

            def add(v, b, at):
                dve.wait_ge(summed, v + 1)
                at_least(dve, added, v)
                to = acc[:, at, :].rearrange("p a c -> p (a c)")
                dve.tensor_tensor(to, ps[b][:, :], to, ALU.add).then_inc(added, 1)

            def body(it):
                for s in range(RING):
                    if s % LIST == 0:
                        before = step_list(dve, regs, k.node_tile_before, RING // LIST * it + s // LIST, NT)
                    v, b = RING * it + s, s % SUMS
                    step = bass.ds(v, 1)
                    if H > 1:
                        dve.tensor_scalar(onehot[:, b, :], k.iota_n[0:TE, :], k.step_dst[:, step], None, ALU.is_equal)
                        dve.wait_ge(got_ready[s], 16 * it + 16)
                        dve.tensor_tensor(msg[:, b, :].rearrange("p (h c) -> p h c", h=H),
                                          got[:, s, :].rearrange("p (h c) -> p h c", h=H),
                                          bcast(step_ex[:, step, :], [[1, H], [0, D // H + 1]]),
                                          ALU.mult).then_inc(msg_ready, 1)
                    else:
                        dve.tensor_scalar(onehot[:, b, :], k.iota_n[0:TE, :], k.step_dst[:, step],
                                          step_ex[:, step, :].rearrange("p a c -> p (a c)"), ALU.is_equal,
                                          ALU.mult).then_inc(msg_ready, 1)
                    if not isinstance(v, int) or v >= SUM_LAG:
                        add(v - SUM_LAG, (s - SUM_LAG) % SUMS, bass.ds(before[s % LIST], 1))

            rolled(dve, STEPS // RING, body)
            before = step_list(dve, regs[0:SUM_LAG], k.node_tile_before, STEPS // LIST, NT)
            for v in range(STEPS - SUM_LAG, STEPS):
                add(v, v % SUMS, bass.ds(before[v + SUM_LAG - STEPS], 1))


def normalize_sums(k, name, H, acc, bias, add_to=None):
    nc = k.nc
    C = D // H
    tmp = ExitStack()
    with tmp:
        inv = k.sb(name + "inv", [P, NT, H], FP32, tmp)
        dve_chain = k.sem(name + "chain")
        block = tmp.enter_context(nc.Block())

        @block.vector
        def _(dve):
            link = chain(dve, dve_chain)
            a = acc.rearrange("p i (h c) -> p i h c", h=H)
            link(dve.reciprocal(inv[:, :, :], a[:, :, :, C]))
            for h in range(H):
                o = a[:, :, h, 0:C]
                link(dve.tensor_tensor(o, o, bcast(inv[:, :, h], [[H, NT], [0, C]]), ALU.mult))
                link(dve.tensor_tensor(o, o, bcast(bias[:, h * C:(h + 1) * C], [[0, NT], [1, C]]), ALU.add))
            if add_to is not None:
                link(dve.tensor_tensor(add_to[:, :, :], add_to[:, :, :], acc[:, :, 0:D], ALU.add))


def attention_layer(k, name, H, x_in, heads_in, norm, w, bias, first_tile, tiles, add_to=None):
    width = D + H
    outer = ExitStack()
    with outer:
        table = k.nodes[:, :, 0:width]
        alpha = k.sb(name + "alpha", [P, NT, 2 * H], FP32, outer)
        step_ex = k.sb(name + "step_ex", [TE, STEPS, H], FP32, outer)
        got = k.sb(name + "got", [TE, RING, width], FP32, outer)
        got_ready = [k.sem(f"{name}got_ready{s}") for s in range(RING)]
        table_dram = k.dram(name + "table_dram", [NPAD, width])
        project_nodes(k, name + "p_", x_in, heads_in, norm, w, H, table, table_dram, alpha)
        edge_weights(k, name + "w_", H, alpha, table, step_ex, table_dram, got, got_ready)
        sum_messages(k, name + "s_", H, table_dram, table, step_ex, got, got_ready, first_tile, tiles)
        normalize_sums(k, name + "n_", H, table, bias, add_to)
        k.free_sems()


def edge_network(k, table_dram, out):
    nc = k.nc
    acc = k.nodes[:, :, 0:D]
    LAST = STEPS - 1
    AHEAD = 8
    MSGS = 4
    tmp = ExitStack()
    with tmp:
        def sb(name, shape, dt=FP32):
            return k.sb("e_" + name, shape, dt, tmp)

        def sem(name):
            return k.sem("e_" + name)

        idx = sb("idx", [TE, RING], I32)
        node = sb("node", [TE, RING, HID])
        parts = sb("parts", [P, RING, D + HID])
        gated = sb("gated", [TE, 2, HID])
        gated_t = sb("gated_t", [HID, 2, TE])
        z = sb("z", [TE, 2, D])
        onehot = sb("onehot", [TE, MSGS, P])
        msg = sb("msg", [TE, MSGS, D])
        square = parts[:, :, :].rearrange("p s c -> p (s c)")[:, 0:NT * D].rearrange("p (i c) -> p i c", c=D)
        norm = sb("norm", [P, NT])
        ps_t = [k.ps(f"e_turn{i}", [HID, P], FP32, tmp) for i in range(2)]
        ps_z = [k.ps(f"e_z{i}", [TE, D], FP32, tmp) for i in range(2)]
        ps_s = [k.ps(f"e_sum{i}", [P, D], FP32, tmp) for i in range(4)]
        idx_ready = sem("idx_ready")
        node_in = [sem(f"node_in{s}") for s in range(RING)]
        parts_in = [sem(f"parts_in{s}") for s in range(RING)]
        gathers_begun = sem("gathers_begun")
        gated_ready = sem("gated_ready")
        turned = sem("turned")
        turned_out = sem("turned_out")
        combined = sem("combined")
        z_ready = sem("z_ready")
        msg_ready = sem("msg_ready")
        onehot_ready = sem("onehot_ready")
        summed = sem("summed")
        added = sem("added")
        dve_chain = sem("chain")
        squared = sem("squared")
        rooted = sem("rooted")
        done = sem("done")
        out_done = sem("out_done")
        block = tmp.enter_context(nc.Block())

        @block.sync
        def _(sp):
            regs = [sp.alloc_register(f"e_edge_tile{s}") for s in range(LIST)]

            def body(it):
                for s in range(RING):
                    if s % LIST == 0:
                        tiles = step_list(sp, regs, k.edge_tile, RING // LIST * it + s // LIST, ET)
                    at_least(sp, z_ready, RING * it + s + 1 - RING)
                    sp.dma_start(parts[:, s, :], k.parts_dram[bass.ds(tiles[s % LIST] * P, P), :]
                                 ).then_inc(parts_in[s], 16)

            rolled(sp, STEPS // RING, body)
            sp.wait_ge(done, 1)
            sp.dma_start(out[0:(NT - 1) * P, :].rearrange("(i p) c -> p i c", p=P),
                         k.x[:, 0:NT - 1, :]).then_inc(out_done, 16)
            sp.dma_start(out[(NT - 1) * P:N, :], k.x[0:NLAST, NT - 1, :]).then_inc(out_done, 16)
            sp.wait_ge(out_done, 32)

        @block.gpsimd
        def _(pool):
            for s in range(RING):
                pool.indirect_dma_start(node[:, s, :], None, table_dram,
                                        bass.IndirectOffsetOnAxis(ap=k.step_src[:, s:s + 1], axis=0)
                                        ).then_inc(node_in[s], 16)
            with pool.Fori(1, STEPS // RING) as it:
                for s in range(RING):
                    v = RING * it + s
                    pool.wait_ge(idx_ready, v + 1 - RING)
                    pool.wait_ge(gated_ready, v + 1 - RING)
                    pool.sem_inc(gathers_begun, 1)
                    pool.indirect_dma_start(node[:, s, :], None, table_dram,
                                            bass.IndirectOffsetOnAxis(ap=idx[:, s:s + 1], axis=0)
                                            ).then_inc(node_in[s], 16)

        @block.scalar
        def _(act):
            def index(v, s, landed):
                act.wait_ge(node_in[s], landed)
                act.activation(idx[:, s:s + 1], k.step_src[:, bass.ds(v, 1)], ACT.Copy).then_inc(idx_ready, 1)

            def copy_turned(v, s):
                act.wait_ge(turned, v + 1)
                at_least(act, combined, v - 1)
                act.activation(gated_t[:, s % 2, :], ps_t[s % 2][:, 0:TE], ACT.Copy).then_inc(turned_out, 1)

            def tanh(v, s):
                act.wait_ge(z_ready, v + 1)
                at_least(act, summed, v + 1 - MSGS)
                act.activation(msg[:, s % MSGS, :], z[:, s % 2, :], ACT.Tanh).then_inc(msg_ready, 1)

            copy_turned(0, 0)

            def body(it):
                for s in range(RING):
                    v = RING * it + s
                    if not isinstance(v, int) or v + AHEAD + RING <= LAST:
                        if isinstance(v, int) and v == 0:
                            for i in range(AHEAD):
                                index(RING + i, i, 16)
                        index(v + AHEAD + RING, (s + AHEAD) % RING, 16 * it + 16 * (1 + (s + AHEAD) // RING))
                    if not isinstance(v, int) or v + 1 <= LAST:
                        copy_turned(v + 1, s + 1)
                    if not isinstance(v, int) or v > 0:
                        tanh(v - 1, (s - 1) % RING)

            body(0)
            with act.Fori(1, STEPS // RING - 2) as it:
                body(it)
            for it in range(STEPS // RING - 2, STEPS // RING):
                body(it)
            tanh(LAST, LAST % RING)
            act.wait_ge(squared, 1)
            act.activation(norm[:, :], norm[:, :], ACT.Sqrt).then_inc(rooted, 1)

        @block.tensor
        def _(pe):
            def turn(v, s):
                pe.wait_ge(gated_ready, v + 1)
                at_least(pe, turned_out, v - 1)
                pe.transpose(ps_t[s % 2][:, 0:TE], gated[:, s % 2, :], k.ident[0:TE, 0:TE]).then_inc(turned, 1)

            def combine(v, s):
                pe.wait_ge(turned_out, v + 1)
                at_least(pe, z_ready, v - 1)
                pe.matmul(ps_z[s % 2][:, :], gated_t[:, s % 2, :], k.w_comb1[:, :], start=True,
                          stop=True).then_inc(combined, 1)

            def scatter(v, s):
                b = s % MSGS
                pe.wait_ge(msg_ready, v + 1)
                pe.wait_ge(onehot_ready, v + 1)
                at_least(pe, added, v + 1 - MSGS)
                pe.matmul(ps_s[b][:, :], onehot[:, b, :], msg[:, b, :], start=True, stop=True).then_inc(summed, 1)

            turn(0, 0)

            def body(it):
                for s in range(RING):
                    v = RING * it + s
                    if not isinstance(v, int) or v + 1 <= LAST:
                        turn(v + 1, s + 1)
                    combine(v, s)
                    if not isinstance(v, int) or v >= 2:
                        scatter(v - 2, (s - 2) % RING)

            rolled(pe, STEPS // RING, body)
            scatter(LAST - 1, (LAST - 1) % RING)
            scatter(LAST, LAST % RING)

        @block.vector
        def _(dve):
            link = chain(dve, dve_chain)
            regs = [dve.alloc_register(f"e_tile{s}") for s in range(LIST)]
            link(dve.memset(acc, 0.0))

            def gate(v, s, it):
                dve.wait_ge(node_in[s % RING], 16 * it + 16)
                dve.wait_ge(parts_in[s % RING], 16 * it + 16)
                at_least(dve, turned, v - 1)
                dve.tensor_tensor(gated[:, s % 2, :], node[:, s % RING, :], parts[0:TE, s % RING, D:D + HID],
                                  ALU.mult).then_inc(gated_ready, 1)

            def add_part(v, s):
                dve.wait_ge(combined, v + 1)
                at_least(dve, msg_ready, v - 1)
                dve.tensor_tensor(z[:, s % 2, :], ps_z[s % 2][:, :], parts[0:TE, s % RING, 0:D],
                                  ALU.add).then_inc(z_ready, 1)

            def place(v, s):
                at_least(dve, summed, v + 1 - MSGS)
                dve.tensor_scalar(onehot[:, s % MSGS, :], k.iota_n[0:TE, :], k.step_dst[:, bass.ds(v, 1)], None,
                                  ALU.is_equal).then_inc(onehot_ready, 1)

            def add(v, s, at):
                dve.wait_ge(summed, v + 1)
                at_least(dve, added, v)
                to = acc[:, at, :].rearrange("p a c -> p (a c)")
                dve.tensor_tensor(to, ps_s[s % MSGS][:, :], to, ALU.add).then_inc(added, 1)

            gate(0, 0, 0)
            gate(1, 1, 0)

            def body(it):
                for s in range(RING):
                    if s % LIST == 0:
                        before = step_list(dve, regs, k.node_tile_before, RING // LIST * it + s // LIST, NT)
                    v = RING * it + s
                    if not isinstance(v, int) or v + 2 <= LAST:
                        gate(v + 2, s + 2, it + (s + 2) // RING)
                    add_part(v, s)
                    place(v, s)
                    if not isinstance(v, int) or v >= SUM_LAG:
                        add(v - SUM_LAG, (s - SUM_LAG) % RING, bass.ds(before[s % LIST], 1))

            rolled(dve, STEPS // RING, body)
            before = step_list(dve, regs[0:SUM_LAG], k.node_tile_before, STEPS // LIST, NT)
            for v in range(STEPS - SUM_LAG, STEPS):
                add(v, v % RING, bass.ds(before[v + SUM_LAG - STEPS], 1))
            dve.wait_ge(added, STEPS)
            link(dve.tensor_tensor(square, acc, acc, ALU.mult))
            link(dve.tensor_reduce(norm[:, :], square, AX_X, ALU.add))
            dve.tensor_tensor(norm[:, NT - 1:NT], norm[:, NT - 1:NT], k.no_node[:, :], ALU.add).then_inc(squared, 1)
            dve.wait_ge(rooted, 1)
            link(dve.reciprocal(norm[:, :], norm[:, :]))
            link(dve.tensor_tensor(square, acc, bcast(norm[:, :], [[1, NT], [0, D]]), ALU.mult))
            dve.tensor_tensor(k.x[:, :, :], k.x[:, :, :], square, ALU.add).then_inc(done, 1)


def graph_kernel(nc, x, src, dst, edge_attr_128, edge_attr_64, w1, att_s1, att_d1, b1, w2, att_s2, att_d2, b2,
                 w_node, b_node, w_edge, b_edge, w_dist, b_dist, w_comb, out):
    with ExitStack() as ctx:
        k = Kernel(nc, ctx)
        k.alpha_dram = {4: k.dram("alpha4", [NPAD, 8]), 1: k.dram("alpha1", [NPAD, 2])}
        node_dram = k.dram("node_dram", [NPAD, HID])
        prepare_edges(k, src, dst)
        load_weights(k, x, w1, att_s1, att_d1, b1, w2, att_s2, att_d2, b2, w_node, b_node, w_edge, b_edge,
                     w_dist, b_dist, w_comb)
        k.ea, k.ed, k.x_dram = edge_attr_128, edge_attr_64, x
        k.parts_dram = k.dram("parts_dram", [ET * P, D + HID])
        attention_layer(k, "a", 4, k.x, 1, True, k.w1, k.b1, 0, FIRST_PART)
        attention_layer(k, "b", 1, k.nodes, 4, False, k.w2, k.b2, FIRST_PART, ET - FIRST_PART, add_to=k.x)
        project_nodes(k, "c_", k.x, 1, True, k.wn, 0, k.nodes[:, :, 0:HID], node_dram, None, k.bn)
        edge_network(k, node_dram, out)


_INS = ['x', 'src', 'dst', 'edge_attr_128', 'edge_attr_64'] + ['L0_gnn_' + n for n in (
    'W1', 'att_src1', 'att_dst1', 'b1', 'W2', 'att_src2', 'att_dst2', 'b2')] + ['L1_gnn_' + n for n in (
        'W_node', 'b_node', 'W_edge', 'b_edge', 'W_dist', 'b_dist', 'W_comb')]


def kernel(**inputs):
    import numpy as _np
    import concourse.bacc as _bacc
    from concourse import mybir as _mybir
    from concourse.bass_utils import run_bass_kernel_spmd as _run

    nc = _bacc.Bacc("TRN2", target_bir_lowering=False, num_devices=1)
    arrays, args = {}, []
    for name in _INS:
        a = _np.ascontiguousarray(inputs[name])
        arrays[f"in_{name}_dram"] = a
        args.append(nc.dram_tensor(f"in_{name}_dram", a.shape, _mybir.dt.from_np(a.dtype), kind="ExternalInput").ap())
    out = nc.dram_tensor("out_0_dram", (N, D), _mybir.dt.float32, kind="ExternalOutput").ap()
    graph_kernel(nc, *args, out)
    r = _run(nc, [arrays], core_ids=[0])
    return r.results[0]["out_0_dram"]
```

```python
from contextlib import ExitStack

import concourse.bass as bass
from concourse import mybir

FP32 = mybir.dt.float32
BF16 = mybir.dt.bfloat16
I32 = mybir.dt.int32
ALU = mybir.AluOpType
ACT = mybir.ActivationFunctionType
AX_X = mybir.AxisListType.X

P = 128
N, E = 2500, 40000
D = 256
HID = 128
DE, DC = 128, 64
NT = (N + P - 1) // P
NPAD = NT * P
NLAST = N - (NT - 1) * P

TE = 125
ET = E // TE
KR = 4
ER = ET // KR
EC = KR * TE

STEPS = ET + NT
VC = 4
VP = STEPS // VC
RING = 20
SUM_LAG = 3
LIST = 10
LOAD = 12
GROUP = 5
PER_ITER = 2 * GROUP
FIRST_PART = ET // 2

ATTRS = 2 * 2 * GROUP * 128
EARLY_A, EARLY_B = 2, 1
NOW_A, NOW_B = 34, 10

NA = 125
NB = N // NA
DIV_SHIFT = 16
DIV_MUL = -(-(1 << DIV_SHIFT) // NB)

NEG = -1.0e38
SKIP = 1 << 20
SLOPE = 0.2
EPS = 1e-5


def bcast(ap, dims):
    return bass.AP(tensor=ap.tensor, offset=ap.offset, ap=[ap.ap[0], *dims])


def backwards(ap):
    step, n = ap.ap[-1]
    return bass.AP(tensor=ap.tensor, offset=ap.offset + step * (n - 1), ap=[*ap.ap[:-1], [-step, n]])


def chain(eng, sem):
    count = [0]

    def link(ins):
        count[0] += 1
        ins.then_inc(sem, 1)
        eng.wait_ge(sem, count[0])

    return link


class Kernel:
    def __init__(self, nc, ctx):
        self.nc, self.ctx = nc, ctx
        self.sems = []

    def sb(self, name, shape, dt=FP32, ctx=None):
        return (ctx or self.ctx).enter_context(self.nc.sbuf_tensor(name, shape, dt))

    def ps(self, name, shape, dt=FP32, ctx=None):
        return (ctx or self.ctx).enter_context(self.nc.psum_tensor(name, shape, dt))

    def sem(self, name):
        self.sems.append(self.nc.alloc_semaphore(name=name))
        return self.sems[-1]

    def free_sems(self):
        self.nc.clear_and_free_semaphores(self.sems)
        self.nc.all_engine_barrier()
        self.sems = []

    def dram(self, name, shape, dt=FP32):
        return self.nc.dram_tensor(name, shape, dt).ap()


def keep_for_all(k):
    k.x = k.sb("x_nodes", [P, NT, D])
    k.nodes = k.sb("nodes", [P, NT, D + 4])
    k.ident = k.sb("ident", [P, P])
    k.mirror = k.sb("mirror", [P, P])
    k.iota_n = k.sb("iota_n", [P, P])
    k.no_node = k.sb("no_node", [P, 1])
    k.part_f = k.sb("part_f", [P, 1])
    k.onehot_a = k.sb("onehot_a", [NA, E], BF16)
    k.mask_b = k.sb("mask_b", [TE, ET, NB], BF16)
    k.keep = k.sb("keep", [ER, EC])
    k.stop_rev = k.sb("stop_rev", [ER, EC])
    k.stop = k.sb("stop", [ER, EC])
    k.row_stop_rev = k.sb("row_stop_rev", [4, ER])
    k.row_stop = k.sb("row_stop", [4, ER])
    k.row_first = k.sb("row_first", [ER, 1], I32)
    k.step_tile_p = k.sb("step_tile_p", [VP, VC], I32)
    k.edge_tile = k.sb("edge_tile", [1, STEPS // LIST, LOAD], I32)
    k.node_tile_before = k.sb("node_tile_before", [1, STEPS // LIST + 1, LOAD], I32)
    k.step_src = k.sb("step_src", [TE, STEPS], I32)
    k.step_dst = k.sb("step_dst", [TE, STEPS])
    k.start_at = k.sb("start_at", [P, NT], I32)
    k.start_rev = k.sb("start_rev", [P, NT], I32)
    k.w1 = k.sb("w1_ext", [P, 2, D + 8])
    k.w2 = k.sb("w2_ext", [P, 2, D + 2])
    k.wn = k.sb("w_node", [P, 2, HID])
    k.b1 = k.sb("b1_cols", [P, 2])
    k.b2 = k.sb("b2_row", [P, D])
    k.bn = k.sb("bn_row", [P, HID])
    k.w_edge_comb = k.sb("w_edge_comb", [DE, D])
    k.w_comb1 = k.sb("w_comb1", [HID, D])
    k.w_dist = k.sb("w_dist_ext", [DC + 1, HID])
    k.bias3 = k.sb("bias3", [DC + 1, D], BF16)
    k.ones3 = k.sb("ones3", [DC + 1, P], BF16)


def load_a(k, eng, column, n):
    part = k.src_a_row.rearrange("p j -> (p j)")[bass.ds(column, n)]
    return eng.dma_start(k.onehot_a[:, bass.ds(column, n)],
                         bass.AP(tensor=part.tensor, offset=part.offset, ap=[[0, NA], [1, n]]))


class Rows:

    def __init__(self, k, name, width, early, first_column, ctx):
        self.early = [(j + 1) * RING // early - 1 for j in range(early)]
        self.slot = {s: n for n, s in enumerate(s for s in range(RING) if s not in self.early)}
        self.ring = k.sb(name + "ring", [TE, RING - early, width], FP32, ctx)
        self.n = STEPS // RING * early
        self.first_column, self.columns = first_column, 2 * width
        self.kept = k.onehot_a[0:TE, first_column:first_column + self.columns * self.n].bitcast(FP32).rearrange(
            "p (s c) -> p s c", c=width)
        self.ring_ready = [k.sem(f"{name}ring_ready{n}") for n in range(RING - early)]
        self.kept_ready = k.sem(name + "kept_ready")

    def end_column(self, n):
        return self.first_column + self.columns * n

    def keep(self, k, pool, table_dram, n):
        v = n // len(self.early) * RING + self.early[n % len(self.early)]
        pool.indirect_dma_start(self.kept[:, n, :], None, table_dram,
                                bass.IndirectOffsetOnAxis(ap=k.step_src[:, v:v + 1], axis=0)
                                ).then_inc(self.kept_ready, 16)

    def of(self, it, s):
        if s in self.slot:
            return self.ring[:, self.slot[s], :]
        n = len(self.early) * it + self.early.index(s)
        return self.kept[:, bass.ds(n, 1), :].rearrange("p a c -> p (a c)")


def prepare_edges(k, block, tmp, bank, src, dst):
    nc = k.nc
    k.dst_rows = k.dram("dst_rows", [ET, TE])
    k.src_rows = k.dram("src_rows", [ET, TE])
    k.src_a_row = k.dram("src_a_row", [ER, EC], BF16)
    k.spread = {4: k.dram("spread4", [E, 8]), 1: k.dram("spread1", [E, 2])}

    def sb(name, shape, dt=FP32):
        return k.sb(name, shape, dt, tmp)

    iota_i = sb("iota_i", [P, NPAD], I32)
    iota_f = iota_i[:, :].bitcast(FP32)
    part_i = sb("part_i", [P, 1], I32)
    node_i = sb("node_i", [P, NT], I32)
    node_f = sb("node_f", [P, NT])
    tile_i = sb("tile_i", [ER, KR], I32)
    step_i = sb("step_i", [VP, VC], I32)
    step_f = sb("step_f", [VP, VC])
    room = k.mask_b[0:ER, :, :].rearrange("p t b -> p (t b)").bitcast(I32)
    dst_i, src_i, prev_i, next_i, src_b, src_bf = (room[:, i * EC:(i + 1) * EC] for i in range(6))
    src_bf = src_bf.bitcast(FP32)
    dst_f = sb("dst_f", [ER, EC])
    src_f = sb("src_f", [ER, EC])
    next_f = sb("next_f", [ER, EC])
    src_a = sb("src_a", [ER, EC], BF16)
    src_bt = sb("src_bt", [TE, ET])
    next_t = sb("next_t", [TE, KR, ER])
    key_i = sb("key_i", [ER, KR], I32)
    key_f = sb("key_f", [ER, KR])
    passed = sb("passed", [ER, KR, STEPS], BF16)
    ones_b = sb("ones_b", [P, 1], BF16)
    below = k.nodes[0:ER, :, :].rearrange("p i c -> p (i c)").bitcast(BF16)[:, 0:KR * NPAD].rearrange(
        "p (c n) -> p c n", n=NPAD)
    zeros = sb("zeros", [ER, KR * P])
    rowflag = sb("rowflag", [ER, 2])
    rowflag4 = sb("rowflag4", [ER, 2, 4])
    node_tile = sb("node_tile", [P, NT], I32)
    node_tile_f = sb("node_tile_f", [P, NT])
    node_row = sb("node_row", [P, NT], I32)
    rows = iota_f[:, 0:NT * TE].rearrange("p (i q) -> p i q", q=TE)
    cmp = k.nodes[:, :, :].rearrange("p i c -> p (i c)")[:, 0:NT * TE].rearrange("p (i q) -> p i q", q=TE)
    count = sb("count", [P, NT])
    has = sb("has", [P, NT])
    start = sb("start", [P, NT])
    tab_f = sb("tab_f", [1, 2, STEPS + SUM_LAG])
    win = sb("win", [VP, VC])
    src_v = sb("src_v", [VP, VC, TE])
    dst_v = sb("dst_v", [VP, VC, TE])

    ps_t = k.ps("prep_t", [TE, KR, P], FP32, tmp)
    ps_r = k.ps("prep_r", [ER, 512], FP32, tmp)
    ps_s = k.ps("prep_s", [P, 512], FP32, tmp)
    ps_n = bank

    edges_in = k.sem("edges_in")
    consts = k.sem("consts")
    pool_chain = k.sem("pool_chain0")
    dve_chain = k.sem("dve_chain0")
    rows_ready = k.sem("rows_ready")
    rows_out = k.sem("rows_out")
    a_ready = k.sem("a_ready")
    a_out = k.sem("a_out")
    a_in = [k.sem(f"a_in{i}") for i in range(4)]
    passed_ready = k.sem("passed_ready")
    steps_ready = k.sem("steps_ready")
    below_ready = k.sem("below_ready")
    tiles_ready = k.sem("tiles_ready")
    tile_idx = k.sem("tile_idx")
    rows_in = k.sem("rows_in")
    step_idx = k.sem("step_idx")
    step_rows = k.sem("step_rows")
    rows_preset = k.sem("rows_preset")
    tr = k.sem("prep_tr")
    tr_used = k.sem("prep_tr_used")
    b_ready = k.sem("b_ready")
    v_fixed = k.sem("v_fixed")
    flag_ready = k.sem("flag_ready")
    zero_ready = k.sem("zero_ready")
    zero_out = k.sem("zero_out")

    links = []
    d1 = dst.rearrange("(p j) -> p j", j=EC)
    s1 = src.rearrange("(p j) -> p j", j=EC)
    start_ready = k.sem("start_ready")

    @block.gpsimd
    def _(pool):
        link = chain(pool, pool_chain)
        pool.iota(part_i[:, :], [[0, 1]], base=0, channel_multiplier=1).then_inc(consts, 1)
        pool.iota(tile_i[:, :], [[1, KR]], base=0, channel_multiplier=KR).then_inc(consts, 1)
        pool.iota(iota_i[:, :], [[1, NPAD]], base=0, channel_multiplier=0).then_inc(consts, 1)
        pool.iota(node_i[:, :], [[P, NT]], base=0, channel_multiplier=1).then_inc(consts, 1)
        pool.iota(step_i[:, :], [[VP, VC]], base=0, channel_multiplier=1).then_inc(consts, 1)
        pool.memset(ones_b[:, :], 1.0).then_inc(consts, 1)
        link(pool.memset(k.ident[:, :], 0.0))
        link(pool.memset(k.mirror[:, :], 0.0))
        link(pool.memset(k.no_node[:, :], 1.0))
        pool.affine_select(out=k.no_node[:, :], in_=k.no_node[:, :], compare_op=ALU.is_ge, fill=0.0,
                           base=-NLAST, pattern=[[0, 1]], channel_multiplier=1)
        pool.affine_select(out=k.ident[:, :], in_=k.ident[:, :], compare_op=ALU.not_equal, fill=1.0,
                           base=0, pattern=[[-1, P]], channel_multiplier=1).then_inc(consts, 1)
        pool.affine_select(out=k.mirror[:, :], in_=k.mirror[:, :], compare_op=ALU.not_equal, fill=1.0,
                           base=1 - P, pattern=[[1, P]], channel_multiplier=1).then_inc(consts, 1)
        pool.wait_ge(step_idx, 1)
        pool.wait_ge(rows_preset, 2)
        pool.wait_ge(rows_out, 32)
        for c in range(VC):
            at = bass.IndirectOffsetOnAxis(ap=k.step_tile_p[:, c:c + 1], axis=0)
            pool.indirect_dma_start(src_v[:, c, :], None, k.src_rows, at, bounds_check=ET - 1,
                                    oob_is_err=False).then_inc(step_rows, 16)
            pool.indirect_dma_start(dst_v[:, c, :], None, k.dst_rows, at, bounds_check=ET - 1,
                                    oob_is_err=False).then_inc(step_rows, 16)
        pool.wait_ge(tile_idx, 1)
        for i in range(NT):
            pool.indirect_dma_start(rows[:, i, :], None, k.dst_rows,
                                    bass.IndirectOffsetOnAxis(ap=node_row[:, i:i + 1], axis=0),
                                    bounds_check=ET - 1, oob_is_err=False).then_inc(rows_in, 16)

    @block.sync
    def _(sp):
        sp.dma_start(dst_i[:, :], d1).then_inc(edges_in, 16)
        sp.dma_start(src_i[:, :], s1).then_inc(edges_in, 16)
        sp.wait_ge(rows_preset, 4)
        sp.dma_start(prev_i[0:1, 1:EC], dst[0:EC - 1].rearrange("(a n) -> a n", a=1)).then_inc(edges_in, 16)
        sp.dma_start(prev_i[1:ER, :], dst[EC - 1:E - 1].rearrange("(p j) -> p j", j=EC)).then_inc(edges_in, 16)
        sp.dma_start(next_i[0:ER - 1, :], dst[1:E - EC + 1].rearrange("(p j) -> p j", j=EC)).then_inc(edges_in, 16)
        sp.dma_start(next_i[ER - 1:ER, 0:EC - 1],
                     dst[E - EC + 1:E].rearrange("(a n) -> a n", a=1)).then_inc(edges_in, 16)
        sp.wait_ge(rows_ready, 2)
        sp.dma_start(k.dst_rows.rearrange("(p c) q -> p (c q)", c=KR), dst_f[:, :]).then_inc(rows_out, 16)
        sp.dma_start(k.src_rows.rearrange("(p c) q -> p (c q)", c=KR), src_f[:, :]).then_inc(rows_out, 16)
        sp.wait_ge(a_ready, 1)
        sp.dma_start(k.src_a_row, src_a[:, :]).then_inc(a_out, 16)
        sp.wait_ge(a_out, 16)
        for i in range(4):
            load_a(k, sp, i * (E // 4), E // 4).then_inc(a_in[i], 16)
        sp.wait_ge(zero_ready, 1)
        for width, at in ((8, k.spread[4]), (2, k.spread[1])):
            flat = at.rearrange("(p j) c -> p (j c)", p=ER)
            cols = EC * width
            for c in range(0, cols, 500):
                sp.dma_start(flat[:, c:c + 500], zeros[:, 0:500]).then_inc(zero_out, 16)

    @block.tensor
    def _(pe):
        pe.wait_ge(consts, 8)
        pe.wait_ge(passed_ready, 1)
        for c in range(KR):
            pe.matmul(ps_r[0:1, 0:STEPS], ones_b[0:ER, :], passed[:, c, :], start=c == 0, stop=c == KR - 1)
        for v in range(VC):
            for c in range(KR):
                last = pe.matmul(ps_s[0:VP, v:v + 1], passed[:, c, v * VP:(v + 1) * VP], ones_b[0:ER, :],
                                 start=c == 0, stop=c == KR - 1)
        last.then_inc(steps_ready, 1)
        pe.wait_ge(below_ready, 1)
        for i in range(NT):
            for c in range(KR):
                last = pe.matmul(ps_n[:, i:i + 1], below[:, c, i * P:(i + 1) * P], ones_b[0:ER, :],
                                 start=c == 0, stop=c == KR - 1)
        last.then_inc(tiles_ready, 1)
        pe.wait_ge(b_ready, 1)
        for c in range(KR):
            last = pe.transpose(ps_t[:, c, 0:ER], src_bf[:, c * TE:(c + 1) * TE], k.ident[0:ER, 0:ER])
        last.then_inc(tr, 1)
        pe.wait_ge(tr_used, 1)
        for c in range(KR):
            last = pe.transpose(ps_t[:, c, 0:ER], next_f[:, c * TE:(c + 1) * TE], k.ident[0:ER, 0:ER])
        last.then_inc(tr, 1)
        pe.wait_ge(tr_used, 2)
        for c in range(KR):
            last = pe.matmul(ps_r[:, (KR - 1 - c) * TE:(KR - c) * TE], next_t[:, c, :],
                             k.mirror[0:TE, P - TE:P], start=True, stop=True)
        last.then_inc(tr, 1)
        pe.wait_ge(flag_ready, 1)
        pe.matmul(ps_s[0:4, 128:128 + ER], rowflag4[:, 0, :], k.mirror[0:ER, P - ER:P],
                  start=True, stop=True)
        pe.matmul(ps_s[0:4, 256:256 + ER], rowflag4[:, 1, :], k.ident[0:ER, 0:ER],
                  start=True, stop=True).then_inc(tr, 1)

    def rest_tensor(pe):
        pe.wait_ge(v_fixed, 1)
        pe.wait_ge(tr_used, 3)
        for c in range(VC):
            last = pe.transpose(ps_t[:, c, 0:VP], src_v[:, c, :], k.ident[0:VP, 0:VP])
        last.then_inc(tr, 1)
        pe.wait_ge(tr_used, 4)
        for c in range(VC):
            last = pe.transpose(ps_t[:, c, 0:VP], dst_v[:, c, :], k.ident[0:VP, 0:VP])
        last.then_inc(tr, 1)

    @block.vector
    def _(dve):
        link = chain(dve, dve_chain)
        links.append(link)
        dve.memset(prev_i[:, :], -1).then_inc(rows_preset, 1)
        dve.memset(next_i[:, :], -1).then_inc(rows_preset, 1)
        dve.memset(src_v[:, :, :], 0.0).then_inc(rows_preset, 1)
        dve.memset(dst_v[:, :, :], -1.0).then_inc(rows_preset, 1)
        dve.memset(zeros[:, :], 0.0).then_inc(zero_ready, 1)
        dve.wait_ge(edges_in, 16 * 6)
        dve.tensor_copy(dst_f[:, :], dst_i[:, :]).then_inc(rows_ready, 1)
        dve.tensor_copy(src_f[:, :], src_i[:, :]).then_inc(rows_ready, 1)
        link(dve.tensor_scalar(src_b[:, :], src_i[:, :], float(DIV_MUL), None, ALU.mult))
        link(dve.tensor_scalar(src_b[:, :], src_b[:, :], DIV_SHIFT, None, ALU.logical_shift_right))
        dve.tensor_copy(src_a[:, :], src_b[:, :]).then_inc(a_ready, 1)
        dve.scalar_tensor_tensor(src_bf[:, :], src_b[:, :], -float(NB), src_i[:, :], ALU.mult,
                                 ALU.add).then_inc(b_ready, 1)
        dve.wait_ge(consts, 8)
        link(dve.tensor_scalar(key_i[:, :], dst_i[:, TE - 1::TE], 7, None, ALU.logical_shift_right))
        link(dve.tensor_tensor(key_f[:, :], key_i[:, :], tile_i[:, :], ALU.add))
        link(dve.tensor_copy(iota_f[:, :], iota_i[:, :]))
        dve.tensor_copy(k.iota_n[:, :], iota_f[:, 0:P])
        for c in range(KR):
            last = dve.tensor_scalar(passed[:, c, :], iota_f[0:ER, 0:STEPS], key_f[:, c:c + 1], None, ALU.is_gt)
        last.then_inc(passed_ready, 1)
        dve.wait_ge(rows_ready, 2)
        for c in range(KR):
            last = dve.tensor_scalar(below[:, c, :], iota_f[0:ER, :], dst_f[:, (c + 1) * TE - 1:(c + 1) * TE],
                                     None, ALU.is_gt)
        last.then_inc(below_ready, 1)
        link(dve.tensor_tensor(k.keep[:, :], prev_i[:, :], dst_i[:, :], ALU.is_equal))
        link(dve.tensor_tensor(next_f[:, :], next_i[:, :], dst_i[:, :], ALU.is_equal))
        dve.tensor_scalar(k.stop[:, :], k.keep[:, :], -1.0, -NEG, ALU.add, ALU.mult)
        link(dve.tensor_reduce(rowflag[:, 0:1], next_f[:, :], AX_X, ALU.min))
        link(dve.tensor_reduce(rowflag[:, 1:2], k.keep[:, :], AX_X, ALU.min))
        dve.tensor_scalar(rowflag4[:, :, :], bcast(rowflag[:, :], [[1, 2], [0, 4]]), -1.0, -NEG, ALU.add,
                          ALU.mult).then_inc(flag_ready, 1)
        link(dve.tensor_copy(k.row_first[:, :], dst_i[:, 0:1]))
        link(dve.tensor_copy(k.part_f[:, :], part_i[:, :]))
        link(dve.tensor_copy(node_f[:, :], node_i[:, :]))
        link(dve.tensor_copy(step_f[:, :], step_i[:, :]))
        dve.wait_ge(steps_ready, 1)
        link(dve.tensor_copy(k.step_tile_p[:, :], ps_s[0:VP, 0:VC]))
        dve.sem_inc(step_idx, 1)
        link(dve.tensor_tensor(win[:, :], step_f[:, :], ps_s[0:VP, 0:VC], ALU.subtract))
        link(dve.tensor_scalar(win[:, :], win[:, :], float(NT - 1), float(P), ALU.min, ALU.mult))
        link(dve.memset(tab_f[:, :, :], 0.0))
        link(dve.tensor_scalar(tab_f[:, 0, 0:STEPS], ps_r[0:1, 0:STEPS], float(ET - 1), None, ALU.min))
        link(dve.tensor_tensor(tab_f[:, 1, SUM_LAG:STEPS + SUM_LAG], iota_f[0:1, 0:STEPS], tab_f[:, 0, 0:STEPS], ALU.subtract))
        link(dve.tensor_scalar(tab_f[:, 1, :], tab_f[:, 1, :], float(NT - 1), None, ALU.min))
        dve.tensor_copy(k.edge_tile[:, :, 0:LIST], tab_f[:, 0, 0:STEPS].rearrange("a (i s) -> a i s", s=LIST))
        dve.tensor_copy(k.node_tile_before[:, STEPS // LIST, 0:SUM_LAG], tab_f[:, 1, STEPS:STEPS + SUM_LAG])
        dve.tensor_copy(k.node_tile_before[:, 0:STEPS // LIST, 0:LIST], tab_f[:, 1, 0:STEPS].rearrange("a (i s) -> a i s", s=LIST))
        dve.wait_ge(tiles_ready, 1)
        link(dve.tensor_scalar(node_tile_f[:, :], ps_n[:, 0:NT], float(ET - 1), None, ALU.min))
        dve.tensor_copy(node_row[:, :], node_tile_f[:, :]).then_inc(tile_idx, 1)
        dve.wait_ge(tile_idx, 1)
        dve.wait_ge(tr, 1)
        for c in range(KR):
            last = dve.tensor_copy(src_bt[:, c::KR], ps_t[:, c, 0:ER])
        last.then_inc(tr_used, 1)
        dve.wait_ge(tr, 2)
        dve.tensor_copy(next_t[:, :, :], ps_t[:, :, 0:ER]).then_inc(tr_used, 1)
        dve.wait_ge(tr, 4)
        dve.wait_ge(tr_used, 2)
        dve.tensor_scalar(k.stop_rev[:, :], ps_r[:, 0:EC], -1.0, -NEG, ALU.add, ALU.mult)
        dve.tensor_copy(k.row_stop_rev[:, :], ps_s[0:4, 128:128 + ER])
        dve.tensor_copy(k.row_stop[:, :], ps_s[0:4, 256:256 + ER]).then_inc(tr_used, 1)

    def rest_vector(dve):
        link = links[0]
        dve.wait_ge(step_rows, 16 * 2 * VC)
        for c in range(VC):
            last = dve.tensor_scalar(dst_v[:, c, :], dst_v[:, c, :], win[:, c:c + 1], None, ALU.subtract)
        last.then_inc(v_fixed, 1)
        dve.wait_ge(tr, 5)
        for c in range(VC):
            last = dve.tensor_copy(k.step_src[:, c * VP:(c + 1) * VP], ps_t[:, c, 0:VP])
        last.then_inc(tr_used, 1)
        dve.wait_ge(tr, 6)
        for c in range(VC):
            last = dve.tensor_copy(k.step_dst[:, c * VP:(c + 1) * VP], ps_t[:, c, 0:VP])
        last.then_inc(tr_used, 1)
        dve.wait_ge(rows_in, 16 * NT)
        node_b = bcast(node_f[:, :], [[1, NT], [0, TE]])
        link(dve.tensor_tensor(cmp[:, :, :], rows[:, :, :], node_b, ALU.is_lt))
        link(dve.tensor_reduce(count[:, :], cmp[:, :, :], AX_X, ALU.add))
        link(dve.tensor_tensor(cmp[:, :, :], rows[:, :, :], node_b, ALU.is_equal))
        link(dve.tensor_reduce(has[:, :], cmp[:, :, :], AX_X, ALU.max))
        link(dve.scalar_tensor_tensor(start[:, :], node_tile_f[:, :], float(TE), count[:, :], ALU.mult, ALU.add))
        link(dve.tensor_scalar(has[:, :], has[:, :], -float(SKIP), float(SKIP), ALU.mult, ALU.add))
        link(dve.tensor_tensor(k.start_at[:, :], start[:, :], has[:, :], ALU.add))
        link(dve.tensor_scalar(node_tile[:, :], node_row[:, :], 2, None, ALU.logical_shift_right))
        link(dve.tensor_scalar(count[:, :], node_tile[:, :], float(2 * EC), float(EC - 1), ALU.mult, ALU.add))
        link(dve.tensor_tensor(count[:, :], count[:, :], start[:, :], ALU.subtract))
        link(dve.tensor_tensor(k.start_rev[:, :], count[:, :], has[:, :], ALU.add))
        dve.sem_inc(start_ready, 1)
        for i in range(4):
            dve.wait_ge(a_in[i], 16)

    def masks(dve, v):
        share = bass.ds(v * (ET // NT), ET // NT)
        dve.tensor_tensor(k.mask_b[:, share, :], bcast(k.iota_n[0:TE, 0:NB], [[0, ET // NT], [1, NB]]),
                          bcast(src_bt[:, share], [[1, ET // NT], [0, NB]]), ALU.is_equal)
        part = k.onehot_a[:, bass.ds(v * (E // NT), E // NT)]
        dve.tensor_scalar(part, part, k.part_f[0:NA, :], None, ALU.is_equal)

    def rest():
        block.tensor(rest_tensor)
        block.vector(rest_vector)

        @block.gpsimd
        def _(pool):
            pool.wait_ge(start_ready, 1)
            pool.wait_ge(zero_out, 16 * 10)

    k.tile_idx = tile_idx
    return rest, masks


def at_least(eng, sem, value):
    if not isinstance(value, int) or value > 0:
        eng.wait_ge(sem, value)


def rolled(eng, n, body, by=1):
    body(0)
    if by > 1:
        rounds = (n - 2) // by
        with eng.Fori(0, rounds) as r:
            for i in range(by):
                body(by * r + i + 1)
        for it in range(by * rounds + 1, n):
            body(it)
        return
    with eng.Fori(1, n - 1) as it:
        body(it)
    body(n - 1)


def rolled_with(eng, n, upto, body):
    body(0, True)
    with eng.Fori(1, min(upto, n - 1)) as it:
        body(it, True)
    for it in range(upto, n - 1):
        body(it, False)
    body(n - 1, upto >= n)


def step_list(eng, regs, table, i, n):
    eng.load(regs, table[0:1, bass.ds(i, 1), 0:len(regs)].rearrange("a i s -> a (i s)"))
    return [eng.snap(r, min_val=0, max_val=n - 1) for r in regs]


def load_weights(k, block, tmp, bank, x, w1, att_s1, att_d1, b1, w2, att_s2, att_d2, b2, w_node, b_node, w_edge, b_edge,
                 w_dist, b_dist, w_comb):
    nc = k.nc
    H = att_s1.shape[0]
    att = k.sb("att", [P, 4, D], FP32, tmp)
    prod = k.sb("att_prod", [P, 2, D], FP32, tmp)
    we = k.sb("w_edge", [DE, HID], FP32, tmp)
    wet = k.sb("w_edge_t", [HID, DE], FP32, tmp)
    wc2 = k.sb("w_comb2", [HID, D], FP32, tmp)
    be = k.sb("b_edge", [HID, 1], FP32, tmp)
    rest = k.sb("bias_rest", [DC + 1, D], FP32, tmp)
    part = k.sb("bias_part", [DC + 1, D], BF16, tmp)
    pt = pw = bank
    pb = bank[:, 256:512]
    preset = k.sem("w_preset")
    loaded = k.sem("w_loaded")
    turned = k.sem("w_turned")
    turned_out = k.sem("w_turned_out")
    folded = k.sem("w_folded")
    dve_chain = k.sem("w_chain")

    links = []

    def everywhere(ap, n):
        return bass.AP(tensor=ap.tensor, offset=ap.offset, ap=[[0, P], [1, n]])

    @block.scalar
    def _(act):
        for n, a in enumerate((att_s1, att_d1, att_s2, att_d2)):
            act.dma_start(att[:, n, :], everywhere(a, D)).then_inc(loaded, 16)
        for c in range(2):
            act.dma_start(k.b1[:, c:c + 1], b1[c * P:(c + 1) * P].rearrange("(n a) -> n a", a=1)
                          ).then_inc(loaded, 16)
        act.dma_start(k.b2[:, :], everywhere(b2, D)).then_inc(loaded, 16)
        act.dma_start(k.bn[:, :], everywhere(b_node, HID)).then_inc(loaded, 16)
        act.dma_start(k.w_dist[DC:DC + 1, :], b_dist.rearrange("(a n) -> a n", a=1)).then_inc(loaded, 16)
        act.dma_start(be[:, :], b_edge.rearrange("(n a) -> n a", a=1)).then_inc(loaded, 16)
        act.dma_start(k.w1[:, :, 0:D], w1.rearrange("(c p) n -> p c n", p=P)).then_inc(loaded, 16)
        act.dma_start(k.w2[:, :, 0:D], w2.rearrange("(c p) n -> p c n", p=P)).then_inc(loaded, 16)
        act.dma_start(k.wn[:, :, :], w_node.rearrange("(c p) n -> p c n", p=P)).then_inc(loaded, 16)
        act.dma_start(k.w_comb1[:, :], w_comb[0:HID, :]).then_inc(loaded, 16)
        act.dma_start(wc2[:, :], w_comb[HID:2 * HID, :]).then_inc(loaded, 16)
        act.dma_start(we[:, :], w_edge).then_inc(loaded, 16)
        act.dma_start(k.w_dist[0:DC, :], w_dist).then_inc(loaded, 16)
        act.wait_ge(preset, 1)
        act.dma_start(k.x[:, 0:NT - 1, :], x[0:(NT - 1) * P, :].rearrange("(i p) c -> p i c", p=P)).then_inc(loaded, 16)
        act.dma_start(k.x[0:NLAST, NT - 1, :], x[(NT - 1) * P:N, :]).then_inc(loaded, 16)

    def fold_tensor(pe):
        pe.wait_ge(loaded, 16 * 19)
        pe.wait_ge(k.tile_idx, 1)
        pe.transpose(pt[:, 0:DE], we[:, :], k.ident[:, :]).then_inc(turned, 1)
        pe.wait_ge(turned_out, 1)
        pe.matmul(pw[:, 0:D], wet[:, :], wc2[:, :], start=True, stop=True)
        pe.matmul(pb[0:DC + 1, 0:D], bcast(be[:, :], [[0, DC + 1]]), wc2[:, :], start=True,
                  stop=True).then_inc(folded, 1)

    @block.vector
    def _(dve):
        link = chain(dve, dve_chain)
        links.append(link)
        dve.memset(k.x[:, NT - 1, :], 0.0).then_inc(preset, 1)
        link(dve.memset(k.bias3[:, :], 0.0))
        dve.memset(k.ones3[:, :], 1.0)

    def fold_vector(dve):
        link = links[0]
        dve.wait_ge(loaded, 16 * 19)
        for n, (w, heads) in enumerate(((k.w1, H), (k.w1, H), (k.w2, 1), (k.w2, 1))):
            link(dve.tensor_tensor(prod[:, :, :], w[:, :, 0:D], bcast(att[:, n, :], [[0, 2], [1, D]]), ALU.mult))
            at = D + heads * (n % 2)
            link(dve.tensor_reduce(w[:, :, at:at + heads],
                                   prod[:, :, :].rearrange("p c (h n) -> p c h n", h=heads), AX_X, ALU.add))
        dve.wait_ge(turned, 1)
        dve.tensor_copy(wet[:, :], pt[:, 0:DE]).then_inc(turned_out, 1)
        dve.wait_ge(folded, 1)
        dve.tensor_copy(k.w_edge_comb[:, :], pw[:, 0:D])
        link(dve.tensor_copy(rest[:, :], pb[0:DC + 1, 0:D]))
        link(dve.tensor_copy(k.bias3[0:1, :], rest[0:1, :]))
        for n in range(2):
            link(dve.tensor_copy(part[:, :], rest[:, :]))
            link(dve.tensor_tensor(rest[:, :], rest[:, :], part[:, :], ALU.subtract))
            row = 32 * (n + 1)
            link(dve.tensor_copy(k.bias3[row:row + 1, :], rest[row:row + 1, :]))

    def fold():
        block.tensor(fold_tensor)
        block.vector(fold_vector)

    return fold


def project_nodes(k, name, block, tmp, x_in, sums_in, w, heads, table, table_dram, alpha, bias=None,
                  spread_out=None, between=None, alongside=None):
    nc = k.nc
    cols = w.shape[2]
    norm = sums_in < 2
    inv = k.sb(name + "inv", [P, NT, max(sums_in, 1)], FP32, tmp)
    stats = k.sb(name + "stats", [P, NT, 6], FP32, tmp)
    ones = k.sb(name + "ones", [P, max(heads, 1)], FP32, tmp)
    mv = k.sb(name + "mv", [P, NT, 2], FP32, tmp)
    rstd = k.sb(name + "rstd", [P, NT], FP32, tmp)
    shift = k.sb(name + "shift", [P, NT], FP32, tmp)
    eps = k.sb(name + "eps", [P, 1], FP32, tmp)
    h = k.sb(name + "h", [P, 2, D], FP32, tmp)
    ht = k.sb(name + "ht", [P, 2, 2, P], FP32, tmp)
    ps_t = [k.ps(f"{name}ps_t{i}", [P, 2, P], FP32, tmp) for i in range(2)]
    ps_o = [k.ps(f"{name}ps_o{i}", [P, cols], FP32, tmp) for i in range(2)]
    aggr = k.sem(name + "aggr")
    root = k.sem(name + "root")
    normed = k.sem(name + "normed")
    h_ready = k.sem(name + "h_ready")
    h_turned = k.sem(name + "h_turned")
    ht_ready = k.sem(name + "ht_ready")
    projected = k.sem(name + "projected")
    out_ready = k.sem(name + "out_ready")
    stored = k.sem(name + "stored")
    dve_chain = k.sem(name + "chain")
    stat_chain = k.sem(name + "stat_chain")
    scaled = k.sem(name + "scaled")
    CH = 4
    AT_ONCE = 4
    width = table.shape[2]

    links = []

    @block.vector
    def _(dve):
        link = chain(dve, dve_chain)
        links.append(link)
        dve.memset(eps[:, :], EPS).then_inc(aggr, 1)
        link(dve.memset(ones[:, :], 1.0))
        if norm:
            def stat(it):
                for t in range(AT_ONCE):
                    v, s = AT_ONCE * it + t, t % 2
                    tile = bass.ds(v, 1)
                    if sums_in:
                        if not isinstance(v, int) or v + 1 < NT:
                            add_sums(v + 1)
                        dve.wait_ge(scaled, v + 1)
                    dve.bn_stats(stats[:, tile, :].rearrange("p a c -> p (a c)"),
                                 x_in[:, tile, :].rearrange("p a c -> p (a c)")).then_inc(stat_chain, 1)

            def add_sums(v):
                tile = bass.ds(v, 1)
                to = x_in[:, tile, :].rearrange("p a c -> p (a c)")
                dve.scalar_tensor_tensor(to, k.nodes[:, tile, 0:D].rearrange("p a c -> p (a c)"),
                                         inv[:, tile, :].rearrange("p a c -> p (a c)"), to, ALU.mult,
                                         ALU.add).then_inc(scaled, 1)

            if sums_in:
                link(dve.reciprocal(inv[:, :, 0], k.nodes[:, :, D]))
                add_sums(0)
            rolled(dve, NT // AT_ONCE, stat)
            dve.wait_ge(stat_chain, NT)
            for i in range(NT):
                dve.bn_aggr(mv[:, i, :], stats[:, i, :]).then_inc(stat_chain, 1)
            dve.wait_ge(stat_chain, 2 * NT)
            dve.sem_inc(aggr, 1)
            dve.wait_ge(root, 1)
            link(dve.reciprocal(rstd[:, :], rstd[:, :]))
            dve.scalar_tensor_tensor(shift[:, :], mv[:, :, 0], -1.0, rstd[:, :], ALU.mult,
                                     ALU.mult).then_inc(normed, 1)

    if between:
        between()

    @block.gpsimd
    def _(pool):
        for i in range(NT if heads else 0):
            pool.wait_ge(out_ready, i + 1)
            pool.indirect_dma_start(k.spread[heads], bass.IndirectOffsetOnAxis(ap=k.start_at[:, i:i + 1], axis=0),
                                    alpha[:, i, :], None, bounds_check=E - 1,
                                    oob_is_err=False).then_inc(spread_out, 16)

    @block.sync
    def _(sp):
        view = table_dram.rearrange("(i p) c -> p i c", p=P)
        for i in range(0, NT, CH):
            sp.wait_ge(out_ready, i + CH)
            sp.dma_start(view[:, i:i + CH, :], table[:, i:i + CH, :]).then_inc(stored, 16)
        if heads:
            sp.dma_start(k.alpha_dram[heads].rearrange("(i p) c -> p i c", p=P),
                         alpha[:, :, :]).then_inc(stored, 16)
        sp.wait_ge(stored, 16 * (NT // CH + (1 if heads else 0)))

    @block.scalar
    def _(act):
        if norm:
            act.wait_ge(aggr, 2)
            act.activation(rstd[:, :], mv[:, :, 1], ACT.Sqrt, bias=eps[:, :]).then_inc(root, 1)
            act.wait_ge(normed, 1)

        def body(it):
            for t in range(AT_ONCE):
                v, s = AT_ONCE * it + t, t % 2
                if not isinstance(v, int) or v + 1 < NT:
                    relu(v + 1, 1 - s)
                act.wait_ge(h_turned, v + 1)
                at_least(act, projected, v - 1)
                act.activation(ht[:, s, :, :], ps_t[s][:, :, :], ACT.Copy).then_inc(ht_ready, 1)

        def relu(v, s):
            at_least(act, h_turned, v - 1)
            tile = bass.ds(v, 1)
            act.activation(h[:, s, :], x_in[:, tile, :].rearrange("p a c -> p (a c)"), ACT.Relu,
                           bias=shift[:, tile], scale=rstd[:, tile]).then_inc(h_ready, 1)

        def body_sums(it):
            for t in range(AT_ONCE):
                v, s = AT_ONCE * it + t, t % 2
                act.wait_ge(h_turned, v + 1)
                at_least(act, projected, v - 1)
                act.activation(ht[:, s, 0, :], ps_t[s][:, 0, :], ACT.Relu, bias=k.b1[:, 0:1])
                act.activation(ht[:, s, 1, :], ps_t[s][:, 1, :], ACT.Relu, bias=k.b1[:, 1:2]).then_inc(ht_ready, 1)

        if norm:
            relu(0, 0)
        rolled(act, NT // AT_ONCE, body if norm else body_sums)

    @block.tensor
    def _(pe):
        def turn(v, s):
            pe.wait_ge(h_ready, v + 1)
            at_least(pe, ht_ready, v - 1)
            for c in range(2):
                last = pe.transpose(ps_t[s][:, c, :], h[:, s, c * P:(c + 1) * P], k.ident[:, :])
            last.then_inc(h_turned, 1)

        def project(v, s):
            pe.wait_ge(ht_ready, v + 1)
            at_least(pe, out_ready, v - 1)
            for c in range(2):
                last = pe.matmul(ps_o[s][:, :], ht[:, s, c, :], w[:, c, :], start=c == 0, stop=c == 1)
            last.then_inc(projected, 1)

        turn(0, 0)

        def body(it):
            for t in range(AT_ONCE):
                v, s = AT_ONCE * it + t, t % 2
                if not isinstance(v, int) or v + 1 < NT:
                    turn(v + 1, 1 - s)
                project(v, s)

        rolled(pe, NT // AT_ONCE, body)

    @block.vector
    def _(dve):
        link = links[0]

        def keep(v, s):
            dve.wait_ge(projected, v + 1)
            tile = bass.ds(v, 1)
            to = table[:, tile, :].rearrange("p a c -> p (a c)")
            if heads:
                dve.tensor_copy(to.rearrange("p (h c) -> p h c", h=heads)[:, :, D // heads], ones[:, :])
                dve.tensor_copy(to.rearrange("p (h c) -> p h c", h=heads)[:, :, 0:D // heads],
                                ps_o[s][:, 0:D].rearrange("p (h c) -> p h c", h=heads))
                dve.tensor_copy(alpha[:, tile, :].rearrange("p a c -> p (a c)"),
                                ps_o[s][:, D:D + 2 * heads]).then_inc(out_ready, 1)
            else:
                dve.tensor_tensor(to, ps_o[s][:, :], bias[:, :], ALU.add).then_inc(out_ready, 1)

        def scale(v, s):
            at_least(dve, h_turned, v - 1)
            tile = bass.ds(v, 1)
            sums = x_in[:, tile, :].rearrange("p a (h c) -> p (a h) c", h=sums_in)[:, :, 0:D // sums_in]
            dve.tensor_tensor(h[:, s, :].rearrange("p (h c) -> p h c", h=sums_in), sums,
                              bcast(inv[:, tile, :], [[1, sums_in], [0, D // sums_in]]), ALU.mult
                              ).then_inc(h_ready, 1)

        if not norm:
            link(dve.reciprocal(inv[:, :, :], x_in.rearrange("p i (h c) -> p i h c", h=sums_in)[:, :, :, D // sums_in]))
            scale(0, 0)
            scale(1, 1)

        def body(it):
            for t in range(AT_ONCE):
                v, s = AT_ONCE * it + t, t % 2
                if not norm and (not isinstance(v, int) or v + 2 < NT):
                    scale(v + 2, s)
                if alongside:
                    alongside(dve, v)
                keep(v, s)

        rolled(dve, NT // AT_ONCE, body)
        if not heads:
            dve.memset(k.nodes[:, :, HID:D], 0.0)


def edge_weights(k, name, H, alpha, table, step_ex, table_dram, rows, kept_now, spread_out, attributes):
    nc = k.nc
    W = 2 * H
    G = 400 // (H * NB)
    groups = ET // G
    PICKS = 4
    alpha_dram = k.alpha_dram[H]
    spread = k.spread[H]
    max_rev = k.dram(name + "max_rev", [E, H])
    ex_rows = k.dram(name + "ex_rows", [ET, H * TE])
    outer = ExitStack()
    with outer:
        as_t = k.sb(name + "as_t", [TE, ET, H], FP32, outer)
        turns = k.sb(name + "turns", [P, 2, H * EC], FP32, outer)
        sparse = turns[0:ER, :, :].rearrange("p a n -> p (a n)").rearrange("p (j c) -> p j c", c=W)
        first = k.sb(name + "first", [ER, W], FP32, outer)
        first_in = k.sem(name + "first_in")
        sparse_in = k.sem(name + "sparse_in")
        inner = ExitStack()
        with inner:
            parts = k.sb(name + "parts", [NA, 3, H, NB], BF16, inner)
            room = k.x[:, 0:NT - 1, :].rearrange("p i c -> p (i c)")
            used = PICKS * G * H * NB
            picked = room[0:TE, 0:used].rearrange("p (s g h b) -> p s g h b", s=PICKS, g=G, h=H)
            tab = room[0:NA, used:used + NB * W].rearrange("p (b w) -> p b w", w=W)
            rest = room[0:NA, used + NB * W:used + NB * W + H * NB].rearrange("p (h b) -> p h b", h=H)
            staged = k.sb(name + "staged", [NA, PICKS, G * TE + P - TE], BF16, inner)
            ps = [k.ps(f"{name}pick{i}", [P, G, H, NB], FP32, inner) for i in range(PICKS)]
            tab_in = k.sem(name + "tab_in")
            split = k.sem(name + "split")
            rows_read = k.sem(name + "rows_read")
            masked = k.sem(name + "masked")
            staged_ready = k.sem(name + "staged_ready")
            staged_odd = k.sem(name + "staged_odd")
            ends_preset = k.sem(name + "ends_preset")
            summed = k.sem(name + "summed")
            block = inner.enter_context(nc.Block())

            @block.sync
            def _(sp):
                sp.dma_start(tab[:, :, :], alpha_dram[0:N, :].rearrange("(a b) h -> a b h", b=NB)).then_inc(tab_in, 16)
                sp.wait_ge(spread_out, 16 * NT)
                sp.dma_start(sparse, spread.rearrange("(p j) c -> p j c", j=EC)).then_inc(sparse_in, 16)

            @block.vector
            def _(dve):
                link = chain(dve, split)
                dve.wait_ge(tab_in, 16)
                link(dve.tensor_copy(rest[:, :, :], tab[:, :, 0:H].rearrange("a b h -> a h b")))
                for n in range(3):
                    link(dve.tensor_copy(parts[:, n, :, :], rest[:, :, :]))
                    if n < 2:
                        link(dve.tensor_tensor(rest[:, :, :], rest[:, :, :], parts[:, n, :, :], ALU.subtract))

                def body(it):
                    for s in range(PICKS):
                        g = PICKS * it + s
                        dve.wait_ge(rows_read, g + 1)
                        at_least(dve, summed, g + 1 - PICKS)
                        mask = bcast(k.mask_b[:, bass.ds(g * G, G), :], [[NB, G], [0, H], [1, NB]])
                        dve.tensor_tensor(picked[:, s, :, :, :], ps[s][0:TE, :, :, :], mask, ALU.mult).then_inc(masked, 1)
                        if not isinstance(g, int) or g > 0:
                            add_up(g - 1, (s - 1) % PICKS)
                        if H == 1 and s % 2 == 1 and (not isinstance(g, int) or g + PICKS < groups):
                            stage(g + PICKS, s)

                def stage(g, s):
                    dve.tensor_copy(staged[:, s, 0:G * TE], k.onehot_a[:, bass.ds(g * (G * TE), G * TE)]
                                    ).then_inc(staged_odd, 1)

                if H == 1:
                    for g in range(1, PICKS, 2):
                        stage(g, g)

                def add_up(g, s):
                    dve.wait_ge(masked, g + 1)
                    dve.tensor_reduce(as_t[:, bass.ds(g * G, G), :], picked[:, s, :, :, :], AX_X,
                                      ALU.add).then_inc(summed, 1)

                rolled(dve, groups // PICKS, body)
                add_up(groups - 1, PICKS - 1)

            @block.scalar
            def _(act):
                def body(it):
                    for s in range(0, PICKS, 2 if H == 1 else 1):
                        g = PICKS * it + s
                        at_least(act, rows_read, g + 1 - PICKS)
                        act.activation(staged[:, s, 0:G * TE], k.onehot_a[:, bass.ds(g * (G * TE), G * TE)],
                                       ACT.Copy).then_inc(staged_ready, 1)

                rolled(act, groups // PICKS, body)

            @block.gpsimd
            def _(pool):
                pool.memset(staged[:, :, G * TE:], 0.0).then_inc(ends_preset, 1)
                pool.indirect_dma_start(first[:, :], None, alpha_dram,
                                        bass.IndirectOffsetOnAxis(ap=k.row_first[:, :], axis=0)
                                        ).then_inc(first_in, 16)
                for s, n in rows.slot.items():
                    pool.indirect_dma_start(rows.ring[:, n, :], None, table_dram,
                                            bass.IndirectOffsetOnAxis(ap=k.step_src[:, s:s + 1], axis=0)
                                            ).then_inc(rows.ring_ready[n], 16)
                for n in range(kept_now):
                    read = -(-rows.end_column(n + 1) // (G * TE))
                    if H > 1:
                        pool.wait_ge(staged_ready, read)
                    else:
                        pool.wait_ge(staged_ready, (read + 1) // 2)
                        at_least(pool, staged_odd, read // 2)
                    rows.keep(k, pool, table_dram, n)

            @block.tensor
            def _(pe):
                pe.wait_ge(split, 6)
                pe.wait_ge(ends_preset, 1)

                def body(it):
                    for s in range(PICKS):
                        g = PICKS * it + s
                        if H > 1:
                            pe.wait_ge(staged_ready, g + 1)
                        else:
                            pe.wait_ge((staged_ready, staged_odd)[s % 2], PICKS // 2 * it + s // 2 + 1)
                        at_least(pe, masked, g + 1 - PICKS)
                        for j in range(G):
                            for n in range(3):
                                last = pe.matmul(ps[s][:, j, :, :], staged[:, s, j * TE:j * TE + P],
                                                 parts[:, n, :, :], start=n == 0, stop=n == 2)
                        last.then_inc(rows_read, 1)

                rolled(pe, groups // PICKS, body)

        tmp = outer
        F = turns[0:ER, 0, :].rearrange("p (h j) -> p h j", h=H)
        max_rows = turns[0:ER, 1, :].rearrange("p (j h) -> p j h", h=H)
        ex_v = turns[0:VP, 0, :].rearrange("p (c h q) -> p c h q", c=VC, h=H)
        full = k.x[0:ER, 0:NT - 1, :].rearrange("p i c -> p (i c)")[:, 0:W * EC].rearrange("p (w j) -> p w j", w=W)
        own, own_d = full[:, 0:H, :], full[:, H:W, :]
        score = ex = own
        local = k.sb(name + "local", [ER, 2, H], FP32, tmp)
        across = k.sb(name + "across", [H, 2, ER + 1], FP32, tmp)
        carry_r = k.sb(name + "carry_r", [ER, H], FP32, tmp)
        carry = k.sb(name + "carry", [ER, 2, H], FP32, tmp)
        node_max = k.sb(name + "node_max", [P, NT, H], FP32, tmp)
        self_e = k.sb(name + "self_e", [P, NT, H], FP32, tmp)
        self_x = k.sb(name + "self_x", [P, NT, H], FP32, tmp)
        rev = [k.ps(f"{name}rev{i}", [P, 512], FP32, tmp) for i in range(H)]
        fwd = [k.ps(f"{name}fwd{i}", [P, 512], FP32, tmp) for i in range(H)]
        small_r, small_f = fwd[H - 1], rev[0]

        def sem(n):
            return k.sem(name + n)

        rev_ready, fwd_ready, rev_used, fwd_used = sem("rev_ready"), sem("fwd_ready"), sem("rev_used"), sem("fwd_used")
        local_ready, turned, turned_used = sem("local_ready"), sem("turned"), sem("turned_used")
        local_f_ready, turned_f, turned_f_used = sem("local_f_ready"), sem("turned_f"), sem("turned_f_used")
        max_ready, max_out, max_in, max_preset = sem("max_ready"), sem("max_out"), sem("max_in"), sem("max_preset")
        self_ready, self_done, score_ready, ex_ready = (sem("self_ready"), sem("self_done"), sem("score_ready"),
                                                        sem("ex_ready"))
        ex_preset, ex_out, ex_in, ex_turned, dve_chain = (sem("ex_preset"), sem("ex_out"), sem("ex_in"),
                                                          sem("ex_turned"), sem("chain"))
        ex_used = sem("ex_used")
        block = tmp.enter_context(nc.Block())

        @block.sync
        def _(sp):
            sp.wait_ge(max_ready, 1)
            sp.dma_start(max_rev.rearrange("(p j) h -> p j h", j=EC), max_rows[:, :, :]).then_inc(max_out, 16)
            sp.wait_ge(ex_ready, 1)
            to = ex_rows.rearrange("(p c) (h q) -> p h c q", c=KR, h=H)
            for h in range(H):
                sp.dma_start(to[:, h], ex[:, h, :].rearrange("p (c q) -> p c q", c=KR)).then_inc(ex_out, 16)
            for g in range(2):
                attributes.load(k, sp, g, g)

        @block.gpsimd
        def _(pool):
            for n in range(kept_now, rows.n):
                rows.keep(k, pool, table_dram, n)
            pool.wait_ge(max_preset, 1)
            pool.wait_ge(max_out, 16)
            for i in range(NT):
                pool.indirect_dma_start(node_max[:, i, :], None, max_rev,
                                        bass.IndirectOffsetOnAxis(ap=k.start_rev[:, i:i + 1], axis=0),
                                        bounds_check=E - 1, oob_is_err=False).then_inc(max_in, 16)
            pool.wait_ge(ex_preset, 1)
            pool.wait_ge(ex_out, 16 * H)
            for c in range(VC):
                pool.indirect_dma_start(ex_v[:, c, :, :].rearrange("p h q -> p (h q)"), None, ex_rows,
                                        bass.IndirectOffsetOnAxis(ap=k.step_tile_p[:, c:c + 1], axis=0),
                                        bounds_check=ET - 1, oob_is_err=False).then_inc(ex_in, 16)

        @block.scalar
        def _(act):
            act.wait_ge(score_ready, 1)
            act.activation(ex[:, :, :], score[:, :, :], ACT.Exp).then_inc(ex_ready, 1)
            act.wait_ge(self_ready, 1)
            act.activation(self_x[:, :, :], self_e[:, :, :], ACT.Exp).then_inc(self_done, 1)

        @block.tensor
        def _(pe):
            def forward(h):
                for c in range(KR):
                    last = pe.transpose(fwd[h][0:ER, c * TE:(c + 1) * TE], as_t[:, c::KR, h], k.ident[0:TE, 0:TE])
                last.then_inc(fwd_ready, 1)

            for h in range(H):
                for c in range(KR):
                    last = pe.matmul(rev[h][0:ER, (KR - 1 - c) * TE:(KR - c) * TE], as_t[:, c::KR, h],
                                     k.mirror[0:TE, P - TE:P], start=True, stop=True)
                last.then_inc(rev_ready, 1)
            for h in range(H - 1):
                forward(h)
            pe.wait_ge(local_ready, 1)
            pe.matmul(small_r[0:H, 0:ER], local[:, 0, :], k.mirror[0:ER, P - ER:P], start=True,
                      stop=True).then_inc(turned, 1)
            pe.wait_ge(turned_used, 1)
            pe.matmul(small_r[0:ER, 128:128 + H], across[:, 0, 0:ER], k.ident[0:H, 0:H], start=True,
                      stop=True).then_inc(turned, 1)
            pe.wait_ge(turned_used, 2)
            pe.matmul(small_r[0:ER, 256:256 + H], k.mirror[0:ER, P - ER:P], carry_r[:, :], start=True,
                      stop=True).then_inc(turned, 1)
            pe.wait_ge(turned_used, 3)
            forward(H - 1)
            pe.wait_ge(local_f_ready, 1)
            pe.wait_ge(rev_used, H)
            pe.matmul(small_f[0:H, 0:ER], local[:, 1, :], k.ident[0:ER, 0:ER], start=True,
                      stop=True).then_inc(turned_f, 1)
            pe.wait_ge(turned_f_used, 1)
            pe.matmul(small_f[0:ER, 128:128 + H], across[:, 1, 0:ER], k.ident[0:H, 0:H], start=True,
                      stop=True).then_inc(turned_f, 1)
            pe.wait_ge(fwd_used, H)
            pe.wait_ge(ex_in, 16 * VC)
            for h in range(H):
                for c in range(VC):
                    last = pe.transpose(fwd[h][0:TE, c * VP:(c + 1) * VP], ex_v[:, c, h, :], k.ident[0:VP, 0:VP])
                last.then_inc(ex_turned, 1)

        @block.vector
        def _(dve):
            link = chain(dve, dve_chain)
            dve.memset(node_max[:, :, :], NEG).then_inc(max_preset, 1)
            link(dve.memset(across[:, :, :], NEG))
            dve.wait_ge(sparse_in, 16)
            dve.wait_ge(first_in, 16)
            for c in range(W):
                last = dve.tensor_tensor_scan(full[:, c, :], k.keep[:, :], sparse[:, :, c], first[:, c:c + 1],
                                              ALU.mult, ALU.add)
            link(last)
            for h in range(H):
                dve.wait_ge(rev_ready, h + 1)
                last = dve.tensor_tensor_scan(max_rows[:, :, h], k.stop_rev[:, :], rev[h][0:ER, 0:EC], NEG,
                                              ALU.add, ALU.max)
            link(last)
            dve.tensor_copy(local[:, 0, :], max_rows[:, EC - 1, :]).then_inc(local_ready, 1)
            for h in range(H - 1):
                dve.wait_ge(fwd_ready, h + 1)
                dve.tensor_tensor_scan(F[:, h, :], k.stop[:, :], fwd[h][0:ER, 0:EC], NEG, ALU.add, ALU.max)
            dve.wait_ge(turned, 1)
            link(dve.tensor_tensor_scan(across[:, 0, 1:ER + 1], k.row_stop_rev[0:H, :], small_r[0:H, 0:ER], NEG,
                                        ALU.add, ALU.max))
            dve.sem_inc(turned_used, 1)
            dve.wait_ge(turned, 2)
            dve.tensor_copy(carry_r[:, :], small_r[0:ER, 128:128 + H]).then_inc(turned_used, 1)
            dve.wait_ge(turned, 3)
            link(dve.tensor_copy(carry[:, 0, :], small_r[0:ER, 256:256 + H]))
            dve.sem_inc(turned_used, 1)
            for h in range(H):
                last = dve.tensor_tensor_scan(max_rows[:, :, h], k.stop_rev[:, :], rev[h][0:ER, 0:EC],
                                              carry[:, 0, h:h + 1], ALU.add, ALU.max)
                last.then_inc(rev_used, 1)
            dve.wait_ge(rev_used, H)
            dve.sem_inc(max_ready, 1)
            dve.wait_ge(fwd_ready, H)
            link(dve.tensor_tensor_scan(F[:, H - 1, :], k.stop[:, :], fwd[H - 1][0:ER, 0:EC], NEG, ALU.add, ALU.max))
            dve.tensor_copy(local[:, 1, :], F[:, :, EC - 1]).then_inc(local_f_ready, 1)
            dve.wait_ge(turned_f, 1)
            link(dve.tensor_tensor_scan(across[:, 1, 1:ER + 1], k.row_stop[0:H, :], small_f[0:H, 0:ER], NEG,
                                        ALU.add, ALU.max))
            dve.sem_inc(turned_f_used, 1)
            dve.wait_ge(turned_f, 2)
            link(dve.tensor_copy(carry[:, 1, :], small_f[0:ER, 128:128 + H]))
            for h in range(H):
                last = dve.tensor_tensor_scan(F[:, h, :], k.stop[:, :], fwd[h][0:ER, 0:EC], carry[:, 1, h:h + 1],
                                              ALU.add, ALU.max)
            link(last)
            for h in range(H):
                last = dve.tensor_tensor(F[:, h, :], F[:, h, :], backwards(max_rows[:, :, h]), ALU.max)
            link(last)
            link(dve.tensor_tensor(F[:, :, :], F[:, :, :], own, ALU.max))
            dve.tensor_tensor(F[:, :, :], F[:, :, :], own_d, ALU.add)
            for h in range(H):
                dve.tensor_tensor(score[:, h, :], fwd[h][0:ER, 0:EC], own_d[:, h, :], ALU.add).then_inc(fwd_used, 1)
            dve.wait_ge(fwd_used, H)
            dve.scalar_tensor_tensor(F[:, :, :], F[:, :, :], SLOPE, F[:, :, :], ALU.mult, ALU.max)
            link(dve.scalar_tensor_tensor(score[:, :, :], score[:, :, :], SLOPE, score[:, :, :], ALU.mult, ALU.max))
            link(dve.tensor_tensor(score[:, :, :], score[:, :, :], F[:, :, :], ALU.subtract))
            dve.sem_inc(score_ready, 1)
            dve.memset(ex_v, 0.0).then_inc(ex_preset, 1)
            dve.wait_ge(max_in, 16 * NT)
            link(dve.tensor_tensor(node_max[:, :, :], node_max[:, :, :], alpha[:, :, 0:H], ALU.max))
            dve.tensor_tensor(self_e[:, :, :], alpha[:, :, 0:H], alpha[:, :, H:W], ALU.add)
            link(dve.tensor_tensor(node_max[:, :, :], node_max[:, :, :], alpha[:, :, H:W], ALU.add))
            dve.scalar_tensor_tensor(node_max[:, :, :], node_max[:, :, :], SLOPE, node_max[:, :, :], ALU.mult, ALU.max)
            link(dve.scalar_tensor_tensor(self_e[:, :, :], self_e[:, :, :], SLOPE, self_e[:, :, :], ALU.mult, ALU.max))
            dve.tensor_tensor(self_e[:, :, :], self_e[:, :, :], node_max[:, :, :], ALU.subtract).then_inc(self_ready, 1)
            dve.wait_ge(self_done, 1)
            for h in range(H):
                loop = table[:, :, h * (D // H + 1):(h + 1) * (D // H + 1)]
                dve.tensor_tensor(loop, loop, bcast(self_x[:, :, h], [[H, NT], [0, D // H + 1]]), ALU.mult)
            for h in range(H):
                dve.wait_ge(ex_turned, h + 1)
                last = dve.tensor_copy(step_ex[:, :, h], fwd[h][0:TE, 0:STEPS])
            last.then_inc(ex_used, 1)


class Attributes:

    def __init__(self, k, name, first_tile):
        self.first_tile = first_tile
        room = (k.x[0:TE, 0:NT - 1, :].rearrange("p i c -> p (i c)")[:, (NT - 1) * D - ATTRS:] if first_tile == 0
                else k.onehot_a[0:TE, 0:2 * ATTRS].bitcast(FP32))
        self.sb = room.rearrange("p (g n t c) -> p g n t c", g=2, n=2, t=GROUP)
        self.ready = [k.sem(f"{name}attrs_in{g}") for g in range(2)]

    def load(self, k, sp, n, g):
        at = bass.ds((self.first_tile + GROUP * n) * TE, GROUP * TE)
        sp.dma_start(self.sb[:, g, 0, :, :], k.ea[at, :].rearrange("(t p) c -> p t c", p=TE)
                     ).then_inc(self.ready[g], 16)
        sp.dma_start(self.sb[:, g, 1, :, 0:DC], k.ed[at, :].rearrange("(t p) c -> p t c", p=TE)
                     ).then_inc(self.ready[g], 16)


def sum_messages(k, name, H, table_dram, acc, step_ex, rows, attributes, first_tile, tiles):
    nc = k.nc
    cols = D + H
    SUMS = 4
    LAST = STEPS - 1
    AHEAD = 8
    iters = tiles // PER_ITER
    tmp = ExitStack()
    with tmp:
        def sb(n, shape, dt=FP32):
            return k.sb(name + n, shape, dt, tmp)

        def sem(n):
            return k.sem(name + n)

        idx = sb("idx", [TE, RING], I32)
        onehot = sb("onehot", [TE, SUMS, P])
        msg = sb("msg", [TE, SUMS, cols]) if H > 1 else None
        ps = [k.ps(f"{name}sum{i}", [P, cols], FP32, tmp) for i in range(SUMS)]
        attrs = attributes.sb
        attrs_t = sb("attrs_t", [DE, 2, 2, P])
        parts = sb("parts", [P, 2, GROUP, D + HID])
        ps_t = [k.ps(f"{name}turn{i}", [DE, 2, P], FP32, tmp) for i in range(2)]
        ps_p = [k.ps(f"{name}part{i}", [P, D + HID], FP32, tmp) for i in range(2)]
        idx_ready = sem("idx_ready")
        msg_ready = sem("msg_ready")
        gathers_begun = sem("gathers_begun")
        summed = sem("summed_step")
        added = sem("added")
        preset = sem("preset")
        preset_zero = sem("preset_zero")
        x_in = sem("x_in")
        turned = sem("turned")
        turned_out = sem("turned_out")
        parts_made = sem("parts_made")
        parts_ready = sem("parts_ready")
        parts_out = [sem(f"parts_out{g}") for g in range(2)]
        block = tmp.enter_context(nc.Block())

        def wait_rows(eng, it, s):
            if s in rows.slot:
                eng.wait_ge(rows.ring_ready[rows.slot[s]], 16 * it + 16)
            elif isinstance(it, int) and it == 0:
                eng.wait_ge(rows.kept_ready, 16 * rows.n)

        @block.sync
        def _(sp):
            def load(n, g):
                at_least(sp, turned, GROUP * (n - 1))
                attributes.load(k, sp, n, g)

            def store(n, g):
                sp.wait_ge(parts_ready, GROUP * (n + 1))
                at = bass.ds((first_tile + GROUP * n) * P, GROUP * P)
                sp.dma_start(k.parts_dram[at, :].rearrange("(t p) c -> p t c", p=P),
                             parts[:, g, :, :]).then_inc(parts_out[g], 16)

            if first_tile > 0:
                sp.dma_start(k.x[:, 0:NT - 1, :], k.x_dram[0:(NT - 1) * P, :].rearrange("(i p) c -> p i c", p=P)
                             ).then_inc(x_in, 16)

            def body(it):
                for g in range(2):
                    n = 2 * it + g
                    store(n, g)
                    if not isinstance(n, int) or n + 2 < 2 * iters:
                        load(n + 2, g)
                if first_tile == 0 and (not isinstance(it, int) or it > 0):
                    restore(it)

            def restore(it, done=k.a_again):
                sp.wait_ge(msg_ready, RING * it)
                n = len(rows.early) * rows.columns
                load_a(k, sp, (it - 1) * n, n).then_inc(done, 16)

            rolled(sp, iters, body)
            if first_tile == 0:
                for it in range(iters, STEPS // RING):
                    restore(it)
                restore(STEPS // RING, k.a_last)
            for g in range(2):
                sp.wait_ge(parts_out[g], 16 * iters)
            if first_tile > 0:
                sp.wait_ge(x_in, 16)

        @block.scalar
        def _(act):
            def index(v, s, landed):
                act.wait_ge(rows.ring_ready[rows.slot[s]], landed)
                act.activation(idx[:, s:s + 1], k.step_src[:, bass.ds(v, 1)], ACT.Copy).then_inc(idx_ready, 1)

            def copy_turned(u, j):
                act.wait_ge(turned, u + 1)
                at_least(act, parts_made, u - 1)
                act.activation(attrs_t[:, j % 2, :, 0:TE], ps_t[j % 2][:, :, 0:TE], ACT.Copy).then_inc(turned_out, 1)

            def copy_parts(u, j, it):
                act.wait_ge(parts_made, u + 1)
                if j % GROUP == 0:
                    at_least(act, parts_out[j // GROUP], 16 * it)
                act.activation(parts[:, j // GROUP, j % GROUP, :], ps_p[j % 2][:, :], ACT.Copy).then_inc(parts_ready, 1)

            for s in range(AHEAD):
                if s in rows.slot:
                    index(RING + s, s, 16)

            def body(it, with_tiles):
                for s in range(RING):
                    v = RING * it + s
                    to = (s + AHEAD) % RING
                    if to in rows.slot and (not isinstance(v, int) or v + AHEAD + RING <= LAST):
                        index(v + AHEAD + RING, to, 16 * it + 16 * (1 + (s + AHEAD) // RING))
                    u, j = PER_ITER * it + s // 2, s // 2
                    if with_tiles and s % 2 == 0:
                        copy_turned(u, j)
                    elif with_tiles:
                        copy_parts(u, j, it)

            body(0, True)
            with act.Fori(1, min(iters, STEPS // RING - 2)) as it:
                body(it, True)
            for it in range(min(iters, STEPS // RING - 2), STEPS // RING):
                body(it, it < iters)

        @block.gpsimd
        def _(pool):
            with pool.Fori(1, STEPS // RING) as it:
                for s, n in rows.slot.items():
                    v = RING * it + s
                    pool.wait_ge(idx_ready, len(rows.slot) * (it - 1) + n + 1)
                    pool.wait_ge(msg_ready if H > 1 else summed, v + 1 - RING)
                    pool.sem_inc(gathers_begun, 1)
                    pool.indirect_dma_start(rows.ring[:, n, :], None, table_dram,
                                            bass.IndirectOffsetOnAxis(ap=idx[:, s:s + 1], axis=0)
                                            ).then_inc(rows.ring_ready[n], 16)

        @block.tensor
        def _(pe):
            pe.wait_ge(preset, 3)

            def turn(u, j, it):
                pe.wait_ge(attributes.ready[j // GROUP], 32 * it + 32)
                at_least(pe, turned_out, u - 1)
                for n in range(2):
                    last = pe.transpose(ps_t[j % 2][:, n, 0:TE], attrs[:, j // GROUP, n, j % GROUP, :],
                                        k.ident[0:TE, 0:TE])
                last.then_inc(turned, 1)

            def products(u, j):
                pe.wait_ge(turned_out, u + 1)
                at_least(pe, parts_ready, u - 1)
                ea_t, ed_t = attrs_t[:, j % 2, 0, :], attrs_t[0:DC + 1, j % 2, 1, :]
                pe.matmul(ps_p[j % 2][:, 0:D], k.ones3[:, :], k.bias3[:, :], start=True, stop=False)
                pe.matmul(ps_p[j % 2][:, 0:D], ea_t, k.w_edge_comb[:, :], start=False, stop=True)
                pe.matmul(ps_p[j % 2][:, D:D + HID], ed_t, k.w_dist[:, :], start=True, stop=True
                          ).then_inc(parts_made, 1)

            def body(it, with_tiles):
                for s in range(RING):
                    v, b = RING * it + s, s % SUMS
                    u, j = PER_ITER * it + s // 2, s // 2
                    if with_tiles and s % 2 == 0:
                        turn(u, j, it)
                    pe.wait_ge(msg_ready, v + 1)
                    if H == 1:
                        wait_rows(pe, it, s)
                    at_least(pe, added, v + 1 - SUMS)
                    pe.matmul(ps[b][:, :], onehot[:, b, :], msg[:, b, :] if H > 1 else rows.of(it, s),
                              start=True, stop=True).then_inc(summed, 1)
                    if with_tiles and s % 2 == 1:
                        products(u, j)

            rolled_with(pe, STEPS // RING, iters, body)

        @block.vector
        def _(dve):
            regs = [dve.alloc_register(f"{name}tile{s}") for s in range(LIST)]
            for n in range(2):
                dve.memset(attrs[:, n, 1, :, DC:], 0.0).then_inc(preset_zero, 1)
            dve.wait_ge(preset_zero, 2)
            dve.memset(attrs[:, 0, 1, :, DC:DC + 1], 1.0).then_inc(preset, 1)
            dve.memset(attrs[:, 1, 1, :, DC:DC + 1], 1.0).then_inc(preset, 1)
            dve.memset(attrs_t[:, :, :, TE:], 0.0).then_inc(preset, 1)

            def add(v, b, at):
                dve.wait_ge(summed, v + 1)
                at_least(dve, added, v)
                to = acc[:, at, :].rearrange("p a c -> p (a c)")
                dve.tensor_tensor(to, ps[b][:, :], to, ALU.add).then_inc(added, 1)

            def body(it):
                for s in range(RING):
                    if s % LIST == 0:
                        before = step_list(dve, regs, k.node_tile_before, RING // LIST * it + s // LIST, NT)
                    v, b = RING * it + s, s % SUMS
                    step = bass.ds(v, 1)
                    if H > 1:
                        dve.tensor_scalar(onehot[:, b, :], k.iota_n[0:TE, :], k.step_dst[:, step], None, ALU.is_equal)
                        wait_rows(dve, it, s)
                        dve.tensor_tensor(msg[:, b, :].rearrange("p (h c) -> p h c", h=H),
                                          rows.of(it, s).rearrange("p (h c) -> p h c", h=H),
                                          bcast(step_ex[:, step, :], [[1, H], [0, D // H + 1]]),
                                          ALU.mult).then_inc(msg_ready, 1)
                    else:
                        dve.tensor_scalar(onehot[:, b, :], k.iota_n[0:TE, :], k.step_dst[:, step],
                                          step_ex[:, step, :].rearrange("p a c -> p (a c)"), ALU.is_equal,
                                          ALU.mult).then_inc(msg_ready, 1)
                    if not isinstance(v, int) or v >= SUM_LAG:
                        add(v - SUM_LAG, (s - SUM_LAG) % SUMS, bass.ds(before[s % LIST], 1))
                    if first_tile > 0 and isinstance(v, int) and v >= STEPS - NT:
                        i = v - (STEPS - NT)
                        dve.wait_ge(x_in, 16)
                        dve.tensor_tensor(k.x[:, i, :], k.x[:, i, :], k.b2[:, :], ALU.add)

            rolled(dve, STEPS // RING, body)
            before = step_list(dve, regs[0:SUM_LAG], k.node_tile_before, STEPS // LIST, NT)
            for v in range(STEPS - SUM_LAG, STEPS):
                add(v, v % SUMS, bass.ds(before[v + SUM_LAG - STEPS], 1))


def compare_again(k, restored):
    n = restored // NT
    loads = STEPS // RING

    def share(dve, v):
        if isinstance(v, int) and v == 0:
            dve.wait_ge(k.a_again, 16 * (loads - 1))
        if isinstance(v, int) and (v + 1) * n > restored - restored // loads:
            dve.wait_ge(k.a_last, 16)
        part = k.onehot_a[:, bass.ds(v * n, n)]
        dve.tensor_scalar(part, part, k.part_f[0:NA, :], None, ALU.is_equal)

    return share


def attention_layer(k, name, H, x_in, sums_in, w, first_tile, tiles, early, kept_now, inputs=None,
                    alongside=None):
    nc = k.nc
    width = D + H
    outer = ExitStack()
    with outer:
        table = k.nodes[:, :, 0:width]
        alpha = k.sb(name + "alpha", [P, NT, 2 * H], FP32, outer)
        table_dram = k.dram(name + "table_dram", [NPAD, width])
        spread_out = k.sem(name + "spread_out")
        tmp = ExitStack()
        with tmp:
            block = tmp.enter_context(nc.Block())
            finish_edges, masks = None, alongside
            if inputs:
                bank = k.ps("prep_bank", [P, 512], FP32, tmp)
                src, dst, x, *weights = inputs
                fold_weights = load_weights(k, block, tmp, bank, x, *weights)
                finish_edges, masks = prepare_edges(k, block, tmp, bank, src, dst)
                fold_weights()
            project_nodes(k, name + "p_", block, tmp, x_in, sums_in, w, H, table, table_dram, alpha,
                          spread_out=spread_out, between=finish_edges, alongside=masks)
        step_ex = k.sb(name + "step_ex", [TE, STEPS, H], FP32, outer)
        rows = Rows(k, name, width, early, 0 if inputs else 2 * ATTRS, outer)
        attributes = Attributes(k, name, first_tile)
        edge_weights(k, name + "w_", H, alpha, table, step_ex, table_dram, rows, kept_now, spread_out, attributes)
        sum_messages(k, name + "s_", H, table_dram, table, step_ex, rows, attributes, first_tile, tiles)
        k.free_sems()


def edge_network(k, table_dram, out):
    nc = k.nc
    acc = k.nodes[:, :, 0:D]
    LAST = STEPS - 1
    AHEAD = 6
    MSGS = 4
    FEW = 5
    tmp = ExitStack()
    with tmp:
        def sb(name, shape, dt=FP32):
            return k.sb("e_" + name, shape, dt, tmp)

        def sem(name):
            return k.sem("e_" + name)

        idx = sb("idx", [TE, RING], I32)
        node = sb("node", [TE, RING, HID])
        parts = sb("parts", [P, RING, D + HID])
        gated = sb("gated", [TE, 4, HID])
        gated_t = sb("gated_t", [HID, 2, TE])
        z = sb("z", [TE, 2, D])
        onehot = sb("onehot", [TE, MSGS, P])
        msg = sb("msg", [TE, MSGS, D])
        square = parts[:, :, :].rearrange("p s c -> p (s c)")[:, 0:NT * D].rearrange("p (i c) -> p i c", c=D)
        norm = sb("norm", [P, NT])
        ps_t = [k.ps(f"e_turn{i}", [HID, P], FP32, tmp) for i in range(2)]
        ps_z = [k.ps(f"e_z{i}", [TE, D], FP32, tmp) for i in range(2)]
        ps_s = [k.ps(f"e_sum{i}", [P, D], FP32, tmp) for i in range(4)]
        idx_ready = sem("idx_ready")
        node_in = [sem(f"node_in{s}") for s in range(RING)]
        parts_in = [sem(f"parts_in{s}") for s in range(RING)]
        gathers_begun = sem("gathers_begun")
        gated_ready = sem("gated_ready")
        turned = sem("turned")
        turned_out = sem("turned_out")
        combined = sem("combined")
        z_ready = sem("z_ready")
        msg_ready = sem("msg_ready")
        onehot_ready = sem("onehot_ready")
        summed = sem("summed")
        added = sem("added")
        dve_chain = sem("chain")
        square_ready = sem("square_ready")
        squared = sem("squared")
        rooted = sem("rooted")
        done = sem("done")
        out_done = sem("out_done")
        block = tmp.enter_context(nc.Block())

        @block.sync
        def _(sp):
            regs = [sp.alloc_register(f"e_edge_tile{s}") for s in range(LIST)]

            def body(it):
                for s in range(RING):
                    if s % LIST == 0:
                        tiles = step_list(sp, regs, k.edge_tile, RING // LIST * it + s // LIST, ET)
                    at_least(sp, z_ready, RING * it + s + 1 - RING)
                    sp.dma_start(parts[:, s, :], k.parts_dram[bass.ds(tiles[s % LIST] * P, P), :]
                                 ).then_inc(parts_in[s], 16)

            rolled(sp, STEPS // RING, body)
            for i in range(0, NT, FEW):
                whole = min(FEW, NT - 1 - i)
                sp.wait_ge(done, i + whole)
                sp.dma_start(out[i * P:(i + whole) * P, :].rearrange("(i p) c -> p i c", p=P),
                             k.x[:, i:i + whole, :]).then_inc(out_done, 16)
            sp.wait_ge(done, NT)
            sp.dma_start(out[(NT - 1) * P:N, :], k.x[0:NLAST, NT - 1, :]).then_inc(out_done, 16)
            sp.wait_ge(out_done, 16 * (NT // FEW + 1))

        @block.gpsimd
        def _(pool):
            for s in range(RING):
                pool.indirect_dma_start(node[:, s, :], None, table_dram,
                                        bass.IndirectOffsetOnAxis(ap=k.step_src[:, s:s + 1], axis=0)
                                        ).then_inc(node_in[s], 16)
            with pool.Fori(1, STEPS // RING) as it:
                for s in range(RING):
                    v = RING * it + s
                    pool.wait_ge(idx_ready, v + 1 - RING)
                    pool.wait_ge(gated_ready, RING // 2 * (it - 1) + s // 2 + 1)
                    pool.sem_inc(gathers_begun, 1)
                    pool.indirect_dma_start(node[:, s, :], None, table_dram,
                                            bass.IndirectOffsetOnAxis(ap=idx[:, s:s + 1], axis=0)
                                            ).then_inc(node_in[s], 16)

        @block.scalar
        def _(act):
            def index(v, s, landed):
                at_least(act, node_in[s], landed)
                act.activation(idx[:, s:s + 1], k.step_src[:, bass.ds(v, 1)], ACT.Copy).then_inc(idx_ready, 1)

            def copy_turned(v, s):
                act.wait_ge(turned, v + 1)
                at_least(act, combined, v - 1)
                act.activation(gated_t[:, s % 2, :], ps_t[s % 2][:, 0:TE], ACT.Copy).then_inc(turned_out, 1)

            def tanh(v, s):
                act.wait_ge(z_ready, v + 1)
                at_least(act, summed, v + 1 - MSGS)
                act.activation(msg[:, s % MSGS, :], z[:, s % 2, :], ACT.Tanh).then_inc(msg_ready, 1)

            copy_turned(0, 0)

            def body(it):
                for s in range(RING):
                    v = RING * it + s
                    if not isinstance(v, int) or v + AHEAD + RING <= LAST:
                        if isinstance(v, int) and v == 0:
                            for i in range(AHEAD):
                                index(RING + i, i, 0)
                        first = isinstance(v, int) and v + AHEAD < RING
                        index(v + AHEAD + RING, (s + AHEAD) % RING,
                              0 if first else 16 * it + 16 * (1 + (s + AHEAD) // RING))
                    if not isinstance(v, int) or v + 1 <= LAST:
                        copy_turned(v + 1, s + 1)
                    if not isinstance(v, int) or v > 0:
                        tanh(v - 1, (s - 1) % RING)

            body(0)
            with act.Fori(1, STEPS // RING - 2) as it:
                body(it)
            for it in range(STEPS // RING - 2, STEPS // RING):
                body(it)
            tanh(LAST, LAST % RING)
            for i in range(0, NT, FEW):
                act.wait_ge(added, STEPS)
                act.activation(square[:, i:i + FEW, :], acc[:, i:i + FEW, :], ACT.Square).then_inc(square_ready, 1)
            act.wait_ge(squared, 1)
            act.activation(norm[:, :], norm[:, :], ACT.Sqrt).then_inc(rooted, 1)

        @block.tensor
        def _(pe):
            def turn(v, s, it):
                pe.wait_ge(gated_ready, RING // 2 * it + s // 2 + 1)
                at_least(pe, turned_out, v - 1)
                pe.transpose(ps_t[s % 2][:, 0:TE], gated[:, s % 4, :], k.ident[0:TE, 0:TE]).then_inc(turned, 1)

            def combine(v, s):
                pe.wait_ge(turned_out, v + 1)
                at_least(pe, z_ready, v - 1)
                pe.matmul(ps_z[s % 2][:, :], gated_t[:, s % 2, :], k.w_comb1[:, :], start=True,
                          stop=True).then_inc(combined, 1)

            def scatter(v, s, it):
                b = s % MSGS
                pe.wait_ge(msg_ready, v + 1)
                pe.wait_ge(onehot_ready, RING // 2 * it + s // 2 + 1)
                at_least(pe, added, v + 1 - MSGS)
                pe.matmul(ps_s[b][:, :], onehot[:, b, :], msg[:, b, :], start=True, stop=True).then_inc(summed, 1)

            turn(0, 0, 0)

            def body(it):
                for s in range(RING):
                    v = RING * it + s
                    if not isinstance(v, int) or v + 1 <= LAST:
                        turn(v + 1, s + 1, it)
                    combine(v, s)
                    if not isinstance(v, int) or v >= 2:
                        scatter(v - 2, (s - 2) % RING, it if s >= 2 else it - 1)

            rolled(pe, STEPS // RING, body, 2)
            scatter(LAST - 1, RING - 2, STEPS // RING - 1)
            scatter(LAST, RING - 1, STEPS // RING - 1)

        @block.vector
        def _(dve):
            link = chain(dve, dve_chain)
            regs = [dve.alloc_register(f"e_tile{s}") for s in range(LIST)]
            def gate(v, s, it):
                r, g = s % RING, s % 4
                for n in (r, r + 1):
                    dve.wait_ge(node_in[n], 16 * it + 16)
                    dve.wait_ge(parts_in[n], 16 * it + 16)
                at_least(dve, turned, v - 2)
                dve.tensor_tensor(gated[:, g:g + 2, :], node[:, r:r + 2, :], parts[0:TE, r:r + 2, D:D + HID],
                                  ALU.mult).then_inc(gated_ready, 1)

            def add_part(v, s):
                dve.wait_ge(combined, v + 1)
                at_least(dve, msg_ready, v - 1)
                dve.tensor_tensor(z[:, s % 2, :], ps_z[s % 2][:, :], parts[0:TE, s % RING, 0:D],
                                  ALU.add).then_inc(z_ready, 1)

            def place(v, s):
                b = s % MSGS
                at_least(dve, summed, v + 2 - MSGS)
                dve.tensor_tensor(onehot[:, b:b + 2, :], bcast(k.iota_n[0:TE, :], [[0, 2], [1, P]]),
                                  bcast(k.step_dst[:, bass.ds(v, 2)], [[1, 2], [0, P]]),
                                  ALU.is_equal).then_inc(onehot_ready, 1)

            def add(v, s, at):
                dve.wait_ge(summed, v + 1)
                at_least(dve, added, v)
                to = acc[:, at, :].rearrange("p a c -> p (a c)")
                dve.tensor_tensor(to, ps_s[s % MSGS][:, :], to, ALU.add).then_inc(added, 1)

            link(dve.memset(acc[:, :, 0:HID], 0.0))
            gate(0, 0, 0)

            def body(it):
                for s in range(RING):
                    if s % LIST == 0:
                        before = step_list(dve, regs, k.node_tile_before, RING // LIST * it + s // LIST, NT)
                    v = RING * it + s
                    if s % 2 == 0 and (not isinstance(v, int) or v + 2 <= LAST):
                        gate(v + 2, s + 2, it + (s + 2) // RING)
                    add_part(v, s)
                    if s % 2 == 0:
                        place(v, s)
                    if not isinstance(v, int) or v >= SUM_LAG:
                        add(v - SUM_LAG, (s - SUM_LAG) % RING, bass.ds(before[s % LIST], 1))

            rolled(dve, STEPS // RING, body, 2)
            before = step_list(dve, regs[0:SUM_LAG], k.node_tile_before, STEPS // LIST, NT)
            for v in range(STEPS - SUM_LAG, STEPS):
                add(v, v % RING, bass.ds(before[v + SUM_LAG - STEPS], 1))
            dve.wait_ge(added, STEPS)
            for i in range(0, NT, FEW):
                dve.wait_ge(square_ready, i // FEW + 1)
                last = dve.tensor_reduce(norm[:, i:i + FEW], square[:, i:i + FEW, :], AX_X, ALU.add)
            link(last)
            dve.tensor_tensor(norm[:, NT - 1:NT], norm[:, NT - 1:NT], k.no_node[:, :], ALU.add).then_inc(squared, 1)
            dve.wait_ge(rooted, 1)
            link(dve.reciprocal(norm[:, :], norm[:, :]))
            for i in range(NT):
                dve.scalar_tensor_tensor(k.x[:, i, :], acc[:, i, :], norm[:, i:i + 1], k.x[:, i, :], ALU.mult,
                                         ALU.add).then_inc(done, 1)


def graph_kernel(nc, x, src, dst, edge_attr_128, edge_attr_64, w1, att_s1, att_d1, b1, w2, att_s2, att_d2, b2,
                 w_node, b_node, w_edge, b_edge, w_dist, b_dist, w_comb, out):
    with ExitStack() as ctx:
        k = Kernel(nc, ctx)
        k.alpha_dram = {4: k.dram("alpha4", [NPAD, 8]), 1: k.dram("alpha1", [NPAD, 2])}
        node_dram = k.dram("node_dram", [NPAD, HID])
        keep_for_all(k)
        inputs = (src, dst, x, w1, att_s1, att_d1, b1, w2, att_s2, att_d2, b2, w_node, b_node, w_edge, b_edge,
                  w_dist, b_dist, w_comb)
        k.ea, k.ed, k.x_dram = edge_attr_128, edge_attr_64, x
        k.parts_dram = k.dram("parts_dram", [ET * P, D + HID])
        k.a_again, k.a_last = nc.alloc_semaphore(name="a_again"), nc.alloc_semaphore(name="a_last")
        restored = EARLY_A * STEPS // RING * 2 * (D + 4)
        attention_layer(k, "a", 4, k.x, 0, k.w1, 0, FIRST_PART, EARLY_A, NOW_A, inputs)
        attention_layer(k, "b", 1, k.nodes, 4, k.w2, FIRST_PART, ET - FIRST_PART, EARLY_B, NOW_B,
                        alongside=compare_again(k, restored))
        tmp = ExitStack()
        with tmp:
            block = tmp.enter_context(nc.Block())
            project_nodes(k, "c_", block, tmp, k.x, 1, k.wn, 0, k.nodes[:, :, 0:HID], node_dram, None, k.bn)
        edge_network(k, node_dram, out)


_INS = ['x', 'src', 'dst', 'edge_attr_128', 'edge_attr_64'] + ['L0_gnn_' + n for n in (
    'W1', 'att_src1', 'att_dst1', 'b1', 'W2', 'att_src2', 'att_dst2', 'b2')] + ['L1_gnn_' + n for n in (
        'W_node', 'b_node', 'W_edge', 'b_edge', 'W_dist', 'b_dist', 'W_comb')]


def kernel(**inputs):
    import numpy as _np
    import concourse.bacc as _bacc
    from concourse import mybir as _mybir
    from concourse.bass_utils import run_bass_kernel_spmd as _run

    nc = _bacc.Bacc("TRN2", target_bir_lowering=False, num_devices=1)
    arrays, args = {}, []
    for name in _INS:
        a = _np.ascontiguousarray(inputs[name])
        arrays[f"in_{name}_dram"] = a
        args.append(nc.dram_tensor(f"in_{name}_dram", a.shape, _mybir.dt.from_np(a.dtype), kind="ExternalInput").ap())
    out = nc.dram_tensor("out_0_dram", (N, D), _mybir.dt.float32, kind="ExternalOutput").ap()
    graph_kernel(nc, *args, out)
    r = _run(nc, [arrays], core_ids=[0])
    return r.results[0]["out_0_dram"]
```
